# Optimizing a Trainium2 kernel written in Bass

```python
import numpy as np
import jax
import jax.numpy as jnp

def _softmax(x, axis=-1):
    return jax.nn.softmax(x, axis=axis)

def _gelu(x):
    return jax.nn.gelu(x, approximate=True)

def _silu(x):
    return jax.nn.silu(x)

def _sigmoid(x):
    return jax.nn.sigmoid(x)

def _layernorm(x, axis=-1, eps=1e-05):
    m = jnp.mean(x, axis=axis, keepdims=True)
    v = jnp.var(x, axis=axis, keepdims=True)
    return (x - m) / jnp.sqrt(v + eps)

def _scatter_add(tgt, idx, src, axis=0):
    return tgt.at[idx].add(src)

def _segment_sum(src, seg, n):
    return jax.ops.segment_sum(src, seg, n)
kernel_name = 'mk_decoder_preln_d1_seqx_r8_d09ab9'

def setup_inputs(seed: int=0):
    np.random.seed(seed)
    _w = jnp.asarray

    def _rec_inputs():
        import jax
        import jax.numpy as jnp
        _rk = jax.random.key(seed)
        x = -0.0002928 + 1 * jax.random.normal(jax.random.fold_in(_rk, 1), (32, 64, 256), jnp.float32)
        _lenS = 64 - jax.random.randint(jax.random.fold_in(_rk, 7), (32,), 0, max(1, 64 // 4) + 1, jnp.int32)
        _lenS2 = 64 - jax.random.randint(jax.random.fold_in(_rk, 8), (32,), 0, max(1, 64 // 4) + 1, jnp.int32)
        _ctx_512P = jax.random.normal(jax.random.fold_in(_rk, 11), (32, 16, 64), jnp.float32)
        _ctx_512c = jax.random.dirichlet(jax.random.fold_in(_rk, 511), 0.3 * jnp.ones((16,), jnp.float32), (32, 64))
        _ctx_512t = jnp.einsum('bsk,bkd->bsd', _ctx_512c, _ctx_512P)
        _ctx_512t = _ctx_512t * jax.lax.rsqrt(jnp.mean(jnp.square(_ctx_512t)) + 1e-12) * 0.953939
        ctx_512 = 0.000227908 + 0.99994 * (_ctx_512t + 0.3 * jax.random.normal(jax.random.fold_in(_rk, 611), (32, 64, 64), jnp.float32))
        return (x, ctx_512)
    x, ctx_512 = _rec_inputs()

    def _L0_attn_setup():
        import jax, jax.numpy as jnp
        import numpy as np
        DIMS = 256
        HEAD = 16
        HD = DIMS // HEAD
        HD2 = HD // 2
        B, C = (1, 256)

        def layernorm(x, g, b, eps=1e-05):
            mu = x.mean(-1, keepdims=True)
            var = x.var(-1, keepdims=True)
            return (x - mu) / jnp.sqrt(var + eps) * g + b

        def rotary_freqs():
            f = (8000.0 / 200.0) ** jnp.linspace(0.0, 1.0, HD2) * 200.0 / 1000.0
            return 200.0 * f / 1000.0

        def apply_rotary(y, xa):
            t = jnp.arange(y.shape[2], dtype=jnp.float32)
            ang = jnp.einsum('i,j->ij', t, rotary_freqs())
            m = jnp.linalg.norm(xa, axis=-1)
            rr = (m[..., None] * jnp.cos(ang))[:, None]
            ri = (m[..., None] * jnp.sin(ang))[:, None]
            yp = y.reshape(*y.shape[:-1], HD2, 2)
            yr, yi = (yp[..., 0], yp[..., 1])
            out_r = yr * rr - yi * ri
            out_i = yr * ri + yi * rr
            return jnp.stack([out_r, out_i], axis=-1).reshape(y.shape)
        key = jax.random.key(seed)
        ks = jax.random.split(key, 4)
        s = 0.02
        return {'x': jax.random.normal(ks[0], (B, C, DIMS), jnp.float32), 'ln_q_g': jnp.ones((DIMS,), jnp.float32), 'ln_q_b': jnp.zeros((DIMS,), jnp.float32), 'Wq': jax.random.normal(ks[1], (DIMS, DIMS), jnp.float32) * s, 'bq': jnp.zeros((DIMS,), jnp.float32), 'ln_kv_g': jnp.ones((DIMS,), jnp.float32), 'ln_kv_b': jnp.zeros((DIMS,), jnp.float32), 'Wkv': jax.random.normal(ks[2], (DIMS, 2 * DIMS), jnp.float32) * s, 'bkv': jnp.zeros((2 * DIMS,), jnp.float32), 'ln_h_g': jnp.ones((HD,), jnp.float32), 'ln_h_b': jnp.zeros((HD,), jnp.float32), 'Wo': jax.random.normal(ks[3], (DIMS, DIMS), jnp.float32) * s, 'bo': jnp.zeros((DIMS,), jnp.float32)}
    _L0_attn_all = _L0_attn_setup()
    _L0_attn_in = {k: v for k, v in _L0_attn_all.items() if k in ('ln_q_g', 'ln_q_b', 'Wq', 'bq', 'ln_kv_g', 'ln_kv_b', 'Wkv', 'bkv', 'ln_h_g', 'ln_h_b', 'Wo', 'bo')}
    del _L0_attn_all

    def _L0_xattn_setup():
        import jax, jax.numpy as jnp
        import numpy as np
        B, S, L = (2, 128, 128)
        DIM_Q, H, K, D_C, D_CQ, R = (256, 16, 128, 64, 192, 64)

        def _rope_tables(length, dim):
            inv = 1.0 / 10000.0 ** (jnp.arange(0, dim, 2, dtype=jnp.float32) / dim)
            f = jnp.arange(length, dtype=jnp.float32)[:, None] * inv[None, :]
            sin = jnp.repeat(jnp.sin(f), 2, axis=-1)
            cos = jnp.repeat(jnp.cos(f), 2, axis=-1)
            return (sin, cos)

        def _rotate_half(x):
            half = x.shape[-1] // 2
            return jnp.concatenate([-x[..., half:], x[..., :half]], axis=-1)

        def _apply_rope(x, sin, cos):
            return x * cos + _rotate_half(x) * sin
        key = jax.random.key(seed)
        ks = jax.random.split(key, 8)
        return {'hidden_q': jax.random.normal(ks[0], (B, S, DIM_Q), jnp.float32), 'kv_c': jax.random.normal(ks[1], (B, L, D_C), jnp.float32), 'Wq': jax.random.normal(ks[2], (H * K, DIM_Q), jnp.float32) / np.sqrt(DIM_Q).astype(np.float32), 'w_kc_q': jax.random.normal(ks[3], (H, K, D_CQ), jnp.float32) / np.sqrt(K).astype(np.float32), 'w_kc_kv': jax.random.normal(ks[4], (H, K, D_C), jnp.float32) / np.sqrt(K).astype(np.float32), 'W_qr': jax.random.normal(ks[5], (H, D_CQ, R), jnp.float32) / np.float32(np.sqrt(D_CQ) * np.sqrt(R)), 'W_kr': jax.random.normal(ks[6], (H, D_C, R), jnp.float32) / np.sqrt(D_C).astype(np.float32), 'Wo': jax.random.normal(ks[7], (DIM_Q, H * K), jnp.float32) / np.sqrt(H * K).astype(np.float32)}
    _L0_xattn_all = _L0_xattn_setup()
    _L0_xattn_in = {k: v for k, v in _L0_xattn_all.items() if k in ('Wq', 'w_kc_q', 'w_kc_kv', 'W_qr', 'W_kr', 'Wo')}
    del _L0_xattn_all

    def _L0_ffn_setup():
        import jax, jax.numpy as jnp
        import numpy as np
        B, T, D = (4, 256, 256)
        E = 8
        K = 2
        F = 1024 // (E // 2)
        key = jax.random.key(seed)
        ks = jax.random.split(key, 5)
        s_in = 1.0 / np.sqrt(D)
        s_mid = 1.0 / np.sqrt(F)
        x = jax.random.normal(ks[0], (B, T, D), dtype=jnp.float32)
        Wr = jax.random.normal(ks[1], (D, E), dtype=jnp.float32) * s_in
        Wg = jax.random.normal(ks[2], (E, D, F), dtype=jnp.float32) * s_in
        Wu = jax.random.normal(ks[3], (E, D, F), dtype=jnp.float32) * s_in
        Wd = jax.random.normal(ks[4], (E, F, D), dtype=jnp.float32) * s_mid
        return {'x': x, 'Wr': Wr, 'Wg': Wg, 'Wu': Wu, 'Wd': Wd}
    _L0_ffn_all = _L0_ffn_setup()
    _L0_ffn_in = {k: v for k, v in _L0_ffn_all.items() if k in ('Wr', 'Wg', 'Wu', 'Wd')}
    del _L0_ffn_all
    return {'x': x, 'ctx_512': ctx_512, 'L0_attn_ln_q_g': _L0_attn_in['ln_q_g'], 'L0_attn_ln_q_b': _L0_attn_in['ln_q_b'], 'L0_attn_Wq': _L0_attn_in['Wq'], 'L0_attn_bq': _L0_attn_in['bq'], 'L0_attn_ln_kv_g': _L0_attn_in['ln_kv_g'], 'L0_attn_ln_kv_b': _L0_attn_in['ln_kv_b'], 'L0_attn_Wkv': _L0_attn_in['Wkv'], 'L0_attn_bkv': _L0_attn_in['bkv'], 'L0_attn_ln_h_g': _L0_attn_in['ln_h_g'], 'L0_attn_ln_h_b': _L0_attn_in['ln_h_b'], 'L0_attn_Wo': _L0_attn_in['Wo'], 'L0_attn_bo': _L0_attn_in['bo'], 'L0_xattn_Wq': _L0_xattn_in['Wq'], 'L0_xattn_w_kc_q': _L0_xattn_in['w_kc_q'], 'L0_xattn_w_kc_kv': _L0_xattn_in['w_kc_kv'], 'L0_xattn_W_qr': _L0_xattn_in['W_qr'], 'L0_xattn_W_kr': _L0_xattn_in['W_kr'], 'L0_xattn_Wo': _L0_xattn_in['Wo'], 'L0_ffn_Wr': _L0_ffn_in['Wr'], 'L0_ffn_Wg': _L0_ffn_in['Wg'], 'L0_ffn_Wu': _L0_ffn_in['Wu'], 'L0_ffn_Wd': _L0_ffn_in['Wd']}

def reference(x, ctx_512, L0_attn_ln_q_g, L0_attn_ln_q_b, L0_attn_Wq, L0_attn_bq, L0_attn_ln_kv_g, L0_attn_ln_kv_b, L0_attn_Wkv, L0_attn_bkv, L0_attn_ln_h_g, L0_attn_ln_h_b, L0_attn_Wo, L0_attn_bo, L0_xattn_Wq, L0_xattn_w_kc_q, L0_xattn_w_kc_kv, L0_xattn_W_qr, L0_xattn_W_kr, L0_xattn_Wo, L0_ffn_Wr, L0_ffn_Wg, L0_ffn_Wu, L0_ffn_Wd):
    import jax
    import jax.numpy as jnp

    def _L0_attn_ref(x, ln_q_g, ln_q_b, Wq, bq, ln_kv_g, ln_kv_b, Wkv, bkv, ln_h_g, ln_h_b, Wo, bo):
        import jax, jax.numpy as jnp
        import numpy as np
        DIMS = 256
        HEAD = 16
        HD = DIMS // HEAD
        HD2 = HD // 2
        B, C = (1, 256)

        def layernorm(x, g, b, eps=1e-05):
            mu = x.mean(-1, keepdims=True)
            var = x.var(-1, keepdims=True)
            return (x - mu) / jnp.sqrt(var + eps) * g + b

        def rotary_freqs():
            f = (8000.0 / 200.0) ** jnp.linspace(0.0, 1.0, HD2) * 200.0 / 1000.0
            return 200.0 * f / 1000.0

        def apply_rotary(y, xa):
            t = jnp.arange(y.shape[2], dtype=jnp.float32)
            ang = jnp.einsum('i,j->ij', t, rotary_freqs())
            m = jnp.linalg.norm(xa, axis=-1)
            rr = (m[..., None] * jnp.cos(ang))[:, None]
            ri = (m[..., None] * jnp.sin(ang))[:, None]
            yp = y.reshape(*y.shape[:-1], HD2, 2)
            yr, yi = (yp[..., 0], yp[..., 1])
            out_r = yr * rr - yi * ri
            out_i = yr * ri + yi * rr
            return jnp.stack([out_r, out_i], axis=-1).reshape(y.shape)
        b, c, d = x.shape
        q = (layernorm(x, ln_q_g, ln_q_b) @ Wq + bq).reshape(b, c, HEAD, HD).transpose(0, 2, 1, 3)
        kv = (layernorm(x, ln_kv_g, ln_kv_b) @ Wkv + bkv).reshape(b, c, 2, HEAD, HD)
        k = kv[:, :, 0].transpose(0, 2, 1, 3)
        v = kv[:, :, 1].transpose(0, 2, 1, 3)
        scale = HD ** (-0.25)
        q = q * scale
        k = k * scale
        q = apply_rotary(q, x)
        k = apply_rotary(k, x)
        qn = layernorm(q, ln_h_g, ln_h_b)
        kn = layernorm(k, ln_h_g, ln_h_b)
        logits = jnp.einsum('bhqd,bhkd->bhqk', qn, kn) / jnp.sqrt(jnp.float32(HD))
        att = jax.nn.softmax(logits, axis=-1)
        a = jnp.einsum('bhqk,bhkd->bhqd', att, v)
        a = a.transpose(0, 2, 1, 3).reshape(b, c, d)
        return a @ Wo + bo

    def _L0_xattn_ref(hidden_q, kv_c, Wq, w_kc_q, w_kc_kv, W_qr, W_kr, Wo):
        import jax, jax.numpy as jnp
        import numpy as np
        B, S, L = (2, 128, 128)
        DIM_Q, H, K, D_C, D_CQ, R = (256, 16, 128, 64, 192, 64)

        def _rope_tables(length, dim):
            inv = 1.0 / 10000.0 ** (jnp.arange(0, dim, 2, dtype=jnp.float32) / dim)
            f = jnp.arange(length, dtype=jnp.float32)[:, None] * inv[None, :]
            sin = jnp.repeat(jnp.sin(f), 2, axis=-1)
            cos = jnp.repeat(jnp.cos(f), 2, axis=-1)
            return (sin, cos)

        def _rotate_half(x):
            half = x.shape[-1] // 2
            return jnp.concatenate([-x[..., half:], x[..., :half]], axis=-1)

        def _apply_rope(x, sin, cos):
            return x * cos + _rotate_half(x) * sin
        Bv, Sv, _ = hidden_q.shape
        _, Lv, _ = kv_c.shape
        q_hk = (hidden_q @ Wq.T).reshape(Bv, Sv, H, K)
        q_big = jnp.einsum('bshk,hkq->bshq', q_hk, w_kc_q)
        sin_q, cos_q = _rope_tables(Sv, D_CQ)
        q_big = _apply_rope(q_big, sin_q[None, :, None, :], cos_q[None, :, None, :])
        sin_k, cos_k = _rope_tables(Lv, D_C)
        kv_r = _apply_rope(kv_c, sin_k[None], cos_k[None])
        q_r = jnp.einsum('bshq,hqr->bhsr', q_big, W_qr)
        k_r = jnp.einsum('bld,hdr->bhlr', kv_r, W_kr)
        scores = jnp.einsum('bhsr,bhlr->bhsl', q_r, k_r)
        attn = jax.nn.softmax(scores, axis=-1)
        ctx_c = jnp.einsum('bhsl,bld->bhsd', attn, kv_r)
        ctx_lat = jnp.einsum('bhsd,hkd->bhsk', ctx_c, w_kc_kv)
        ctx = ctx_lat.transpose(0, 2, 1, 3).reshape(Bv, Sv, H * K)
        return ctx @ Wo.T

    def _L0_ffn_ref(x, Wr, Wg, Wu, Wd):
        import jax, jax.numpy as jnp
        import numpy as np
        B, T, D = (4, 256, 256)
        E = 8
        K = 2
        F = 1024 // (E // 2)
        probs = jax.nn.softmax(x @ Wr, axis=-1)
        topk_w, topk_idx = jax.lax.top_k(probs, K)
        topk_w = topk_w / jnp.sum(topk_w, axis=-1, keepdims=True)
        output = jnp.zeros_like(x)
        for i in range(E):
            sel = topk_idx == i
            w_i = jnp.sum(topk_w * sel.astype(x.dtype), axis=-1, keepdims=True)
            h = jax.nn.silu(x @ Wg[i]) * (x @ Wu[i])
            e_out = h @ Wd[i]
            output = output + w_i * e_out
        return output
    x = x + _L0_attn_ref(_layernorm(x, axis=-1), L0_attn_ln_q_g, L0_attn_ln_q_b, L0_attn_Wq, L0_attn_bq, L0_attn_ln_kv_g, L0_attn_ln_kv_b, L0_attn_Wkv, L0_attn_bkv, L0_attn_ln_h_g, L0_attn_ln_h_b, L0_attn_Wo, L0_attn_bo)
    x = x + _L0_xattn_ref(_layernorm(x, axis=-1), ctx_512, L0_xattn_Wq, L0_xattn_w_kc_q, L0_xattn_w_kc_kv, L0_xattn_W_qr, L0_xattn_W_kr, L0_xattn_Wo)
    x = x + _L0_ffn_ref(_layernorm(x, axis=-1), L0_ffn_Wr, L0_ffn_Wg, L0_ffn_Wu, L0_ffn_Wd)
    return x

_drawn_inputs = setup_inputs


def setup_inputs(seed=0):
    import zlib

    import numpy as np

    out = dict(_drawn_inputs(seed))
    spreads = {'L0_attn_ln_q_g': (1.0, 0.6),
     'L0_attn_ln_q_b': (0.0, 0.8),
     'L0_attn_bq': (0.0, 0.391),
     'L0_attn_ln_kv_g': (1.0, 0.6),
     'L0_attn_ln_kv_b': (0.0, 0.286),
     'L0_attn_bkv': (0.0, 0.1),
     'L0_attn_ln_h_g': (1.0, 0.6),
     'L0_attn_ln_h_b': (0.0, 0.8),
     'L0_attn_bo': (0.0, 0.1)}
    factors = {}
    for name, (base, spread) in spreads.items():
        noise = np.random.default_rng([zlib.crc32(name.encode()), seed]).standard_normal(out[name].shape)
        drawn = base * np.exp(spread * noise) if base else spread * noise
        out[name] = jnp.asarray(drawn.astype(out[name].dtype))
    for name, factor in factors.items():
        out[name] = (out[name] * factor).astype(out[name].dtype)
    return out
```

```python
from contextlib import ExitStack, contextmanager

import numpy as np

import concourse.bass as bass
from concourse import mybir

F32 = mybir.dt.float32
F32R = mybir.dt.float32r
I32 = mybir.dt.int32
ALU = mybir.AluOpType
ACT = mybir.ActivationFunctionType
AX = mybir.AxisListType.X
EPS = 1e-5

B, S, D = 32, 64, 256
P = 128
NT = B * S // P
KD = D // P
H, HD = 16, 16
NP = H // 2
VW = 2 * HD + 2
XH, XK, XC, XQ = 16, 128, 64, 192
HQ = XQ // 2
E, F = 8, 256
KF = F // P


def constants():
    p = np.arange(P)
    c = {}
    c["ident"] = np.eye(P)
    c["ones"] = np.ones((P, P))
    c["half"] = np.stack([p < 64, p >= 64], 1)
    c["parity"] = np.stack([p // HD % 2 == 0, p // HD % 2 == 1], 1)
    f = (np.float32(8000.0 / 200.0) ** np.linspace(0.0, 1.0, HD // 2, dtype=np.float32)) * np.float32(200.0) / np.float32(1000.0)
    f = (np.float32(200.0) * f / np.float32(1000.0)).astype(np.float32)
    ang = ((p % S).astype(np.float32)[:, None] * f[None, :]).astype(np.float32).astype(np.float64)
    c["rotc"], c["rots"] = np.cos(ang), np.sin(ang)

    def angles(pos, dim):
        inv = (np.float32(1.0) / np.float32(10000.0) ** (np.arange(0, dim, 2, dtype=np.float32) / np.float32(dim))).astype(np.float32)
        return (pos.astype(np.float32)[:, None] * inv[None, :]).astype(np.float32).astype(np.float64)
    a = np.repeat(angles(p % S, XC), 2, axis=1)
    c["kvc"] = np.cos(a)
    c["kvs"] = np.sin(a) * np.where(np.arange(XC) < XC // 2, -1.0, 1.0)
    a = np.repeat(angles(np.arange(S), XQ), 2, axis=1)
    t = np.zeros((P, 3, 4, S))
    for j in range(3):
        i = (P * j + p) % HQ
        t[:, j, 0], t[:, j, 1] = np.cos(a[:, i]).T, np.sin(a[:, i]).T
        t[:, j, 2], t[:, j, 3] = np.cos(a[:, HQ + i]).T, np.sin(a[:, HQ + i]).T
    c["xrope"] = t.reshape(P, -1)
    sel = np.zeros((P, 4, P))
    for hl in range(2):
        for x in range(4):
            for h2 in range(2):
                sel[hl * 8 + x * 2 + h2, x, 64 * h2:64 * h2 + 64] = -1.0
    c["sel"] = sel.reshape(P, -1)
    i = np.arange(E)
    c["before"] = np.tile((i[None, :] < i[:, None]).astype(np.float64).reshape(1, -1), (P, 1))
    c["power"] = np.tile(np.array([[-0.5, -0.5, 0.5, 0.5] + [-0.5] * 32]), (P, 1))
    return {k: np.ascontiguousarray(v, dtype=np.float32) for k, v in c.items()}


class Counter:

    def __init__(self, sem, step):
        self.sem, self.step, self.counts = sem, step, [0]

    def count_up(self, k):
        self.counts += [0] * (k + 1 - len(self.counts))
        self.counts[k] += 1
        return Done(self, k, self.counts[k])


class Done:

    def __init__(self, counter, k, n):
        self.counter, self.k, self.n = counter, k, n


class Carried:

    def __init__(self, name, k, first):
        self.name, self.k, self.first = name, k, first


class Program:
    def __init__(self, nc, ctx):
        self.nc, self.ctx = nc, ctx
        self.trips = [1]
        self.queues = {e: [[]] for e in ("tensor", "vector", "scalar", "gpsimd", "sync")}
        self.counters = {e: Counter(self.semaphore("done_" + e), 1) for e in self.queues if e != "sync"}
        self.channels = {}
        self.last = {}
        self.finals = {}
        self.gate = {}

    def semaphore(self, name):
        return self.ctx.enter_context(self.nc.semaphore(name))

    @property
    def k(self):
        return len(self.trips) - 1

    def segment(self, trips):
        self.trips.append(trips)
        for q in self.queues.values():
            q.append([])

    @contextmanager
    def loop(self, trips):
        self.segment(trips)
        self.inside = set()
        yield
        self.finals[self.k] = dict(self.last)
        self.segment(1)

    def ref(self, name):
        if self.trips[-1] > 1 and name not in self.inside:
            return Carried(name, self.k, self.last.get(name))
        return self.last.get(name)

    def do(self, engine, fn, after=(), name=None):
        done = self.counters[engine].count_up(self.k)
        self.add(engine, fn, after, self.counters[engine])
        return self.named(name, done)

    def dma(self, channel, fn, after=(), name=None, engine="sync"):
        if channel not in self.channels:
            self.channels[channel] = Counter(self.semaphore("dma_" + channel), 16)
        done = self.channels[channel].count_up(self.k)
        self.add(engine, fn, after, self.channels[channel])
        return self.named(name or channel, done)

    def named(self, name, done):
        if name:
            self.last[name] = done
            if self.trips[-1] > 1:
                self.inside.add(name)
        return done

    def add(self, engine, fn, after, counter):
        after = [self.ref(a) if isinstance(a, str) else a for a in after] + self.gate.pop(engine, [])
        self.queues[engine][-1].append((fn, [a for a in after if a], counter))

    def barrier(self):
        ends = [Done(c, self.k, 0) for c in list(self.counters.values()) + list(self.channels.values())]
        for d in ends:
            d.n = d.counter.counts[self.k] if self.k < len(d.counter.counts) else 0
        self.gate = {e: list(ends) for e in self.queues}

    def base(self, c, k):
        return sum(n * t for n, t in zip(c.counts[:k], self.trips[:k]))

    def count(self, c, k):
        return c.counts[k] if k < len(c.counts) else 0

    def value(self, d, k):
        if isinstance(d, Carried):
            first = self.value(d.first, k) if d.first else []
            end = self.finals[d.k].get(d.name)
            if end is None or end.k != d.k:
                return first
            c, per = end.counter, self.count(end.counter, k)
            assert self.base(c, k) >= 1, "a wait for a register's value needs to be positive"
            const = max(self.base(c, k) - per + end.n, 1)
            if first and first[0][0] is c:
                const = max(const, first[0][1])
            return first + [(c, const, per)]
        c = d.counter
        if d.k == k and self.trips[k] > 1:
            return [(c, self.base(c, k) + d.n, self.count(c, k))]
        return [(c, self.base(c, d.k) + (self.trips[d.k] - 1) * self.count(c, d.k) + d.n, 0)]

    def emit(self):
        with self.nc.Block() as block:
            for engine, segments in self.queues.items():
                def body(e, segments=segments):
                    known = {}
                    for k, steps in enumerate(segments):
                        if not steps:
                            continue
                        waits = [[v for a in after for v in self.value(a, k)] for _, after, _ in steps]
                        if self.trips[k] == 1:
                            self.run(e, steps, waits, None, known)
                            continue
                        for w in waits:
                            for c, const, per in w:
                                if not per and known.get(c, 0) < const:
                                    e.wait_ge(c.sem, const * c.step)
                                    known[c] = const
                        with e.Fori(0, self.trips[k]) as i:
                            self.run(e, steps, waits, i, dict(known))
                {"tensor": block.tensor, "vector": block.vector, "scalar": block.scalar,
                 "gpsimd": block.gpsimd, "sync": block.sync}[engine](body)

    def run(self, e, steps, waits, i, known):
        moving = {}
        for (fn, _, counter), w in zip(steps, waits):
            for c, const, per in w:
                if per:
                    if moving.get(c, -1) < const:
                        e.wait_ge(c.sem, (i * per + const) * c.step)
                        moving[c] = const
                elif known.get(c, 0) < const:
                    e.wait_ge(c.sem, const * c.step)
                    known[c] = const
            last = fn(e, i)
            if counter:
                last.then_inc(counter.sem, counter.step)


class Space:

    def __init__(self, nc, start):
        self.nc, self.at = nc, start

    def __call__(self, name, shape, dt=F32):
        t = self.nc.alloc_sbuf_tensor_at(name, shape, dt, offset=self.at)
        self.at += (4 * int(np.prod(shape[1:])) + 31) // 32 * 32
        assert self.at <= 229300, (name, self.at)
        return t


def decoder(nc, a, const_dram, const_at, out, phases=3):
    ctx = ExitStack()
    with ctx:
        pr = Program(nc, ctx)
        T = lambda fn, after=(), name=None: pr.do("tensor", fn, after, name)
        V = lambda fn, after=(), name=None: pr.do("vector", fn, after, name)
        A = lambda fn, after=(), name=None: pr.do("scalar", fn, after, name)
        G = lambda fn, after=(), name=None: pr.do("gpsimd", fn, after, name)
        ctx.enter_context(nc.allow_non_contiguous_dma(reason="small parameter vectors"))

        bank = [ctx.enter_context(nc.psum_tensor(f"bank{i}", [P, 512], F32)) for i in range(8)]

        keep = Space(nc, 16512)
        x = keep("x", [P, NT * D])
        cst = keep("cst", [P, const_at["_"]])
        C = lambda name: cst[:, const_at[name][0]:const_at[name][1]]
        sel = keep("sel", [16, 4, P], F32R)
        stat = keep("stat", [P, 4, 6])
        mv = keep("mv", [P, 4, 2])
        gate_word = keep("gate_word", [P, 1])
        rstd = keep("rstd", [P, 4])
        small = keep("small", [P, 4])
        top = keep("top", [P, 4])
        hrow = [keep(f"hrow{i}", [P, 4]) for i in range(2)]
        maxT = keep("maxT", [16, P], F32R)
        maxs = keep("maxs", [P, 8])
        mhl = keep("mhl", [P, 16], F32R)
        selp = keep("selp", [16, 4, P], F32R)
        inv = keep("inv", [P, 8])
        ihl = keep("ihl", [P, 16], F32R)
        invT = keep("invT", [16, P], F32R)
        ssb = [keep(f"ssb{i}", [P, 512]) for i in range(2)]
        ex = [keep(f"ex{i}", [P, 512]) for i in range(2)]
        xhat = keep("xhat", [P, 4, D])
        xth = keep("xth", [P, KD, 512], F32R)
        xtl = keep("xtl", [P, KD, 512], F32R)
        ident = C("ident")

        s1 = Space(nc, keep.at)
        w1 = s1("w1", [P, KD, 3 * D])
        w1h, w1l = s1("w1h", [P, KD, 3 * D], F32R), s1("w1l", [P, KD, 3 * D], F32R)
        wo1 = s1("wo1", [P, KD, D])
        lncol = s1("lncol", [P, 4, KD])
        hcol = s1("hcol", [P, 2])
        kcol = s1("kcol", [P, 2, 2])
        bwide = s1("bwide", [P, 2, KD, P])
        brow = s1("brow", [P, 4 * D])
        crow = s1("crow", [P, 3 * D])
        cvT = s1("cvT", [P, KD, P])
        borow = s1("borow", [P, D])
        crh, crl = s1("crh", [P, 512], F32R), s1("crl", [P, 512], F32R)
        onesr = s1("onesr", [P, P], F32R)
        qkb = s1("qkb", [P, 2, 512])
        prod = [s1(f"prod{i}", [P, 512]) for i in range(4)]
        yr = s1("yr", [P, 2, 512])
        sq = s1("sq", [P, 2, 512])
        hsum = s1("hsum", [P, 64])
        hvar = s1("hvar", [P, 64])
        half_v = s1("half_v", [P, 64])
        newton = s1("newton", [P, 64])
        hstd = s1("hstd", [P, 64])
        qT = [s1(f"qT{i}", [P, 2, 256]) for i in range(2)]
        kbd = [s1(f"kbd{i}", [P, 2, 4, P]) for i in range(2)]
        vbd = [s1(f"vbd{i}", [P, 4, NP * VW]) for i in range(2)]
        rden = s1("rden", [P, 2, 16])
        an = s1("an", [P, 2, D])
        aT = s1("aT", [P, KD, 256])
        w2 = Space(nc, keep.at)
        wbh = w2("wbh", [P, KD, 2, XH * HQ], F32R)
        wbl = w2("wbl", [P, KD, 2, XH * HQ], F32R)
        wqk = w2("wqk", [P, 4, 2, 2, 2, P])
        wop = w2("wop", [P, NP, D])
        third = max(s1.at, w2.at)
        s2 = Space(nc, third)
        wq_s = s2("wq_s", [P, XH, D])
        wkc_s = s2("wkc_s", [P, XH, XQ])
        wqr_s = s2("wqr_s", [HQ, XH, 2, XC])
        wkr_s = s2("wkr_s", [XC, XH, XC])
        wkv_s = s2("wkv_s", [P, XH, XC])
        wo_s = s2("wo_s", [P, 2, XH * XK])
        woT = Space(nc, third)("woT", [P, XH, D])
        wqrT = s2("wqrT", [XC, 8, 4 * HQ])
        wkrT = s2("wkrT", [XC, XH, XC])
        a2 = Space(nc, third)
        ctxs = a2("ctxs", [P, 8, XC])
        kvt = a2("kvt", [P, 8, XC])
        kvr = a2("kvr", [P, 8, XC])
        kvbd = a2("kvbd", [P, 8, P])
        kvbdT = a2("kvbdT", [P, 8, P])
        m4 = [[a2(f"m{i}_{n}", [P, 512]) for n in range(4)] for i in range(2)]
        rope = [[a2(f"r{i}_{n}", [P, 512]) for n in range(2)] for i in range(6)]
        qc = a2("qc", [P, NP, 512])
        rd = [a2(f"rd{i}", [P, 512]) for i in range(2)]
        s3 = Space(nc, keep.at)
        wgh, wgl = s3("wgh", [P, E, KD, F], F32R), s3("wgl", [P, E, KD, F], F32R)
        wuh, wul = s3("wuh", [P, E, KD, F], F32R), s3("wul", [P, E, KD, F], F32R)
        wd = s3("wd", [P, E, KF, D])
        wr, wrh, wrl = s3("wr", [P, KD, E]), s3("wrh", [P, KD, E], F32R), s3("wrl", [P, KD, E], F32R)
        raw = [s3(f"raw{i}", [P, 2, KD, F]) for i in range(3)]
        sg = [s3(f"sg{i}", [P, 512]) for i in range(2)]
        hh = [s3(f"hh{i}", [P, KF, 512]) for i in range(2)]
        ew = s3("ew", [P, 4, E])
        emax = s3("emax", [P, 4])
        esum = s3("esum", [P, 4])
        rank = s3("rank", [P, E])
        cmpa, cmpb = s3("cmpa", [P, E, E]), s3("cmpb", [P, E, E])

        def mm(e, o, l, r, start, stop):
            return e.matmul(o, l, r, start=start, stop=stop, skip_group_check=True)

        def mm3(e, o, lh, ll, rh, rl, start, stop):
            mm(e, o, lh, rh, start, False)
            mm(e, o, lh, rl, False, False)
            return mm(e, o, ll, rh, False, stop)

        def tiles(first, n):
            def at(i):
                f = first(i)
                if isinstance(f, int):
                    return x[:, f * D:(f + n) * D]
                return x[:, bass.ds(f * D, n * D)]
            return at

        xv = a["x"].rearrange("b s d -> (b s) d").rearrange("(t p) d -> p t d", p=P)
        x3 = x[:, :].rearrange("p (t d) -> p t d", d=D)
        dx0 = pr.dma("x0", lambda e, i: e.dma_start(x3[:, 0:2, :], xv[:, 0:2, :]))
        dcst = pr.dma("cst", lambda e, i: e.dma_start(cst[:, :], const_dram), engine="scalar")
        dw = [pr.dma("w1q", lambda e, i: e.dma_start(w1[:, :, 0:D], a["L0_attn_Wq"].rearrange("(k p) n -> p k n", p=P))),
              pr.dma("w1kv", lambda e, i: e.dma_start(w1[:, :, D:3 * D], a["L0_attn_Wkv"].rearrange("(k p) n -> p k n", p=P)))]
        dln = [pr.dma("ln", lambda e, i, n=n, s=s: e.dma_start(lncol[:, n, :], a[s].rearrange("(k p) -> p k", p=P)), engine="scalar")
               for n, s in enumerate(["L0_attn_ln_q_g", "L0_attn_ln_q_b", "L0_attn_ln_kv_g", "L0_attn_ln_kv_b"])]
        dbr = [pr.dma("brow", lambda e, i, s=s, lo=lo, hi=hi: e.dma_start(
            brow[:, lo:hi], a[s].rearrange("(o n) -> o n", o=1).broadcast_to([P, hi - lo])), engine="scalar")
            for s, lo, hi in (("L0_attn_bq", 0, D), ("L0_attn_bkv", D, 3 * D), ("L0_attn_bo", 3 * D, 4 * D))]
        dh = [pr.dma("hcol", lambda e, i, n=n, s=s, r=r: e.dma_start(
            hcol[r * HD:(r + 1) * HD, n:n + 1], a[s].rearrange("(d o) -> d o", o=1)), engine="sync")
            for n, s in enumerate(["L0_attn_ln_h_g", "L0_attn_ln_h_b"]) for r in range(8)]
        dwo = pr.dma("wo1", lambda e, i: e.dma_start(wo1[:, :, :], a["L0_attn_Wo"].rearrange("(k p) n -> p k n", p=P)))
        dx1 = [pr.dma("x1", lambda e, i, t=t: e.dma_start(x3[:, t:t + 7, :], xv[:, t:t + 7, :])) for t in (2, 9)]
        stage_loads = [
            (wq_s[:, :, :], a["L0_xattn_Wq"].rearrange("(h k) i -> k h i", k=XK)),
            (wkc_s[:, :, :], a["L0_xattn_w_kc_q"].rearrange("h k q -> k h q")),
            (wqr_s[:, :, 0, :], a["L0_xattn_W_qr"][:, 0:HQ, :].rearrange("h q r -> q h r")),
            (wqr_s[:, :, 1, :], a["L0_xattn_W_qr"][:, HQ:XQ, :].rearrange("h q r -> q h r")),
            (wkr_s[:, :, :], a["L0_xattn_W_kr"].rearrange("h d r -> d h r")),
            (wkv_s[:, :, :], a["L0_xattn_w_kc_kv"].rearrange("h k d -> k h d")),
            (wo_s[:, :, :], a["L0_xattn_Wo"].rearrange("(t o) n -> o t n", o=P)),
        ]
        dst = [pr.dma("stage", lambda e, i, o=o, s=s: e.dma_start(o, s)) for o, s in stage_loads]

        A(lambda e, i: e.activation(sel[:, :, :], C("sel").rearrange("p (x c) -> p x c", x=4)[0:16], ACT.Copy), [dcst], "sel")
        A(lambda e, i: e.activation(selp[:, :, :], C("sel").rearrange("p (x c) -> p x c", x=4)[0:16], ACT.Copy, scale=-1.0), [dcst], "selp")
        zero = [G(lambda e, i, t=t: e.memset(t[:, :, :], 0.0)) for t in (vbd[0], vbd[1])]
        for t in (vbd[0], vbd[1]):
            G(lambda e, i, t=t: e.tensor_copy(
                t[:, :, :].rearrange("p b (n w) -> p (b n) w", w=VW)[:, :, 2 * HD:VW],
                C("half").rearrange("p (o w) -> p o w", o=1).broadcast_to([P, 4 * NP, 2])), [dcst, zero[-1]], "vones")
        for k in range(KD):
            for n, lo, hi in ((0, 0, D), (2, D, 3 * D)):
                V(lambda e, i, k=k, n=n, lo=lo, hi=hi: e.tensor_scalar(
                    w1h[:, k, lo:hi], w1[:, k, lo:hi], lncol[:, n, k:k + 1], None, ALU.mult), [dw[-1], dw[0], dln[-1]], "w1h")
                V(lambda e, i, k=k, n=n, lo=lo, hi=hi: e.scalar_tensor_tensor(
                    w1l[:, k, lo:hi], w1[:, k, lo:hi], lncol[:, n, k:k + 1], w1h[:, k, lo:hi].bitcast(F32),
                    ALU.mult, ALU.subtract), ["w1h"], "w1l")
        for n in range(2):
            for k in range(KD):
                V(lambda e, i, n=n, k=k: e.tensor_scalar(bwide[:, n, k, :], C("ones"), lncol[:, 2 * n + 1, k:k + 1], None, ALU.mult),
                  [dcst], "bwide")
        for n in range(2):
            V(lambda e, i, n=n: e.tensor_scalar(kcol[:, n, :], hcol[:, :], C("parity")[:, n:n + 1], None, ALU.mult), [dh[-1]], "kcol")

        def bias_rows(e, i):
            for k in range(KD):
                mm(e, bank[0][:, 0:D], bwide[:, 0, k, :], w1[:, k, 0:D], k == 0, k == KD - 1)
            for k in range(KD):
                last = mm(e, bank[1][:, :], bwide[:, 1, k, :], w1[:, k, D:3 * D], k == 0, k == KD - 1)
            return last
        t = T(bias_rows, ["bwide", dw[0], dw[-1]])
        V(lambda e, i: e.tensor_tensor(crow[:, 0:D], bank[0][:, 0:D], brow[:, 0:D], ALU.add), [t, dbr[-1]])
        t = V(lambda e, i: e.tensor_tensor(crow[:, D:3 * D], bank[1][:, :], brow[:, D:3 * D], ALU.add), name="crow")
        V(lambda e, i: e.tensor_copy(crh[:, :], crow[:, 0:512]), ["crow"], "crh")
        V(lambda e, i: e.tensor_tensor(crl[:, :], crow[:, 0:512], crh[:, :].bitcast(F32), ALU.subtract), ["crh"])
        V(lambda e, i: e.tensor_copy(onesr[:, :], C("ones")), [dcst], "crow_split")

        def value_bias_T(e, i):
            for k in range(KD):
                last = e.transpose(bank[2][:, k * P:(k + 1) * P], crow[:, 2 * D + k * P:2 * D + (k + 1) * P], ident)
            return last
        t = T(value_bias_T, [t, dcst])
        t = A(lambda e, i: e.activation(cvT[:, :, :], bank[2][:, 0:2 * P].rearrange("p (k c) -> p k c", k=KD), ACT.Copy), [t])

        def out_bias(e, i):
            for k in range(KD):
                last = mm(e, bank[3][:, 0:D], cvT[:, k, :], wo1[:, k, :], k == 0, k == KD - 1)
            return last
        t = T(out_bias, [t, dwo])
        V(lambda e, i: e.tensor_tensor(borow[:, :], bank[3][:, 0:D], brow[:, 3 * D:4 * D], ALU.add), [t], "borow")

        def layer_norm(tag, xs, n, self_attn, after):
            for t in range(n):
                V(lambda e, i, t=t: e.bn_stats(stat[:, t, :], xs(t)(i)), list(after) + ["mv"], "stat")
            V(lambda e, i: e.memset(gate_word[:, :], 0.0), ["stat", "xhat"], "gate_word")
            for t in range(n):
                V(lambda e, i, t=t: e.bn_aggr(mv[:, t, :], stat[:, t, :]), ["stat", "xhat"], "mv")
            var = mv[:, 0:n, 1]
            if self_attn:
                V(lambda e, i: e.tensor_scalar(small[:, 0:2], var, 1.0 + EPS, EPS * EPS, ALU.mult, ALU.add), ["mv", "rstd"])
                u = V(lambda e, i: e.tensor_scalar(small[:, 2:4], var, EPS, None, ALU.add), ["mv"])
                u = V(lambda e, i: e.reciprocal(small[:, 2:4], small[:, 2:4]), [u])
                u = V(lambda e, i: e.scalar_tensor_tensor(top[:, 2:4], var, 4.0, small[:, 2:4], ALU.mult, ALU.mult), [u, "hstd"])
                u = V(lambda e, i: e.tensor_copy(top[:, 0:2], small[:, 0:2]), [u])
                G(lambda e, i: e.tensor_tensor(rstd[:, :], top[:, 0:4], C("power")[:, 0:4], ALU.pow), [u, "xhat", "hstd"], "rstd")
            else:
                u = V(lambda e, i: e.tensor_scalar(small[:, 0:n], var, EPS, None, ALU.add), ["mv", "rstd"])
                G(lambda e, i: e.tensor_tensor(rstd[:, 0:n], small[:, 0:n], C("power")[:, 4:4 + n], ALU.pow), [u, "xhat"], "rstd")
            for t in range(n):
                V(lambda e, i, t=t: e.tensor_scalar(xhat[:, t, :], xs(t)(i), mv[:, t, 0:1], rstd[:, t:t + 1],
                                                    ALU.subtract, ALU.mult), ["rstd", "xhatT"], "xhat")

        def normed(blk, c):
            at = slice(256 * c, 256 * c + 256)
            layer_norm("self", lambda t: tiles(lambda i: 2 * blk(i) + t, 1), 2, True, [dx0, dx1[-1]] if c or blk(0) else [dx0])
            yield

            def xhat_T(e, i):
                for k in range(KD):
                    for t in range(2):
                        last = e.transpose(bank[0][:, k * 256 + t * P:k * 256 + (t + 1) * P], xhat[:, t, k * P:(k + 1) * P], ident)
                return last
            T(xhat_T, ["xhat", "bank0", dcst], "xhatT")
            src = bank[0][:, :].rearrange("p (k n) -> p k n", k=KD)
            A(lambda e, i: e.activation(xth[:, :, at], src, ACT.Copy), ["xhatT", f"proj{c}"], "xth")
            V(lambda e, i: e.tensor_tensor(xtl[:, :, at], src, xth[:, :, at].bitcast(F32), ALU.subtract), ["xth", f"proj{c}"], "bank0")
            pr.named(f"xt{c}", pr.last["bank0"])
            V(lambda e, i: e.tensor_copy(hrow[c][:, 0:2], top[:, 2:4]), ["hrow_read"])
            V(lambda e, i: e.tensor_scalar(hrow[c][:, 2:4], rstd[:, 2:4], 4.0, None, ALU.mult), ["rstd", "hrow_read"], f"hrow{c}")
            pr.named("hstd", pr.last[f"hrow{c}"])
            yield

        def heads_front(blk, c):
            cols = lambda t: slice(256 * c + t * P, 256 * c + (t + 1) * P)
            for t in range(2):
                def qk(e, i, t=t):
                    mm(e, bank[1][:, :], onesr[0:1, :], crh[0:1, :], True, False)
                    mm(e, bank[1][:, :], onesr[0:1, :], crl[0:1, :], False, False)
                    for k in range(KD):
                        last = mm3(e, bank[1][:, :], xth[:, k, cols(t)], xtl[:, k, cols(t)],
                                   w1h[:, k, 0:512], w1l[:, k, 0:512], False, k == KD - 1)
                    return last
                T(qk, [f"xt{c}", "bank1", "w1l", "crow_split"], "qk")
                A(lambda e, i, t=t: e.activation(qkb[:, t, :], bank[1][:, :], ACT.Copy), ["qk", "rot_g", "rot_v"], "bank1")
                pr.named("qkb", pr.last["bank1"])
                yield

            def vv(e, i):
                for t in range(2):
                    for k in range(KD):
                        last = mm3(e, bank[1][:, t * D:(t + 1) * D], xth[:, k, cols(t)], xtl[:, k, cols(t)],
                                   w1h[:, k, 512:768], w1l[:, k, 512:768], k == 0, k == KD - 1)
                return last
            T(vv, [f"xt{c}", "bank1"], f"proj{c}")
            pair = qkb[:, :, :].rearrange("p t (h f two) -> p (t h) f two", f=8, two=2)
            ev, od = pair[:, :, :, 0], pair[:, :, :, 1]
            yp = yr[:, :, :].rearrange("p t (h f two) -> p (t h) f two", f=8, two=2)
            cc = C("rotc").rearrange("p (o f) -> p o f", o=1).broadcast_to([P, 64, 8])
            ss = C("rots").rearrange("p (o f) -> p o f", o=1).broadcast_to([P, 64, 8])
            pv = [q[:, :].rearrange("p (h f) -> p h f", f=8) for q in prod]
            G(lambda e, i: e.tensor_tensor(pv[2], ev, ss, ALU.mult), ["qkb", "rot_g"], "p2")
            V(lambda e, i: e.tensor_tensor(pv[3], od, cc, ALU.mult), ["qkb", "rot_g"], "p3")
            G(lambda e, i: e.tensor_tensor(yp[:, :, :, 1], pv[2], pv[3], ALU.add), ["p2", "p3", "ynT"], "rot_g")
            V(lambda e, i: e.tensor_tensor(pv[0], ev, cc, ALU.mult), ["qkb", "rot_v"], "p0")
            V(lambda e, i: e.tensor_tensor(pv[1], od, ss, ALU.mult), ["qkb", "rot_v"], "p1")
            yield
            V(lambda e, i: e.tensor_tensor(yp[:, :, :, 0], pv[0], pv[1], ALU.subtract), ["p0", "p1", "ynT"], "rot_v")
            for b in range(4):
                r, t = slice(64 * (b % 2), 64 * (b % 2) + 64), b // 2
                for h2 in range(2):
                    u = A(lambda e, i, b=b, r=r, t=t, h2=h2: e.activation(
                        vbd[c][64 * h2:64 * h2 + 64, b, :].rearrange("p (n w) -> p n w", w=VW)[:, :, HD * h2:HD * h2 + HD],
                        bank[1][r, t * D:(t + 1) * D].rearrange("p (n h d) -> p n h d", n=NP, h=2)[:, :, h2, :], ACT.Copy),
                        [f"proj{c}", f"av{c}", "vones"], "bank1")
            pr.named(f"values{c}", u)
            yield
            y3 = yr[:, :, :].rearrange("p t (h d) -> p (t h) d", d=HD)
            wide = lambda v: v[:, :].rearrange("p (h o) -> p h o", o=1).broadcast_to([P, 64, HD])
            V(lambda e, i: e.tensor_reduce(hsum[:, :], y3, AX, ALU.add), ["rot_v", "rot_g"], "hsum")
            yield
            V(lambda e, i: e.scalar_tensor_tensor(y3, wide(hsum), -1.0 / HD, y3, ALU.mult, ALU.add), ["hsum"], "centred")
            A(lambda e, i: e.activation(sq[:, :, :], yr[:, :, :], ACT.Square), ["centred", "hss"], "sq")
            yield
            V(lambda e, i: e.tensor_reduce(hvar[:, :], sq[:, :, :].rearrange("p t (h d) -> p (t h) d", d=HD), AX, ALU.add), ["sq", "yn"], "hss")
            for t in range(2):
                V(lambda e, i, t=t: e.tensor_scalar(hvar[:, 32 * t:32 * t + 32], hvar[:, 32 * t:32 * t + 32], hrow[c][:, t:t + 1], EPS,
                                                    ALU.mult, ALU.add), ["hss", f"hrow{c}"], "hvar")
            V(lambda e, i: e.tensor_scalar(newton[:, :].bitcast(I32), hvar[:, :].bitcast(I32), 1, None, ALU.logical_shift_right), ["hvar"], "guess")
            V(lambda e, i: e.tensor_scalar(half_v[:, :], hvar[:, :], -0.5, None, ALU.mult), ["hvar"], "half_v")
            V(lambda e, i: e.tensor_scalar(hstd[:, :].bitcast(I32), newton[:, :].bitcast(I32), -1.0, float(0x5f3759df), ALU.mult, ALU.add),
              ["guess"], "root")
            yield
            for _ in range(3):
                V(lambda e, i: e.tensor_tensor(newton[:, :], hstd[:, :], hstd[:, :], ALU.mult), ["root"], "n1")
                V(lambda e, i: e.tensor_tensor(newton[:, :], newton[:, :], half_v[:, :], ALU.mult), ["n1", "half_v"], "n2")
                V(lambda e, i: e.scalar_tensor_tensor(hstd[:, :], newton[:, :], 1.5, hstd[:, :], ALU.add, ALU.mult), ["n2"], "root")
                if _ % 2 == 0:
                    yield
            for t in range(2):
                V(lambda e, i, t=t: e.tensor_scalar(hstd[:, 32 * t:32 * t + 32], hstd[:, 32 * t:32 * t + 32], hrow[c][:, 2 + t:3 + t], None,
                                                    ALU.mult), ["root"], "hscale")
            pr.named("hrow_read", pr.last["hscale"])
            V(lambda e, i: e.tensor_tensor(y3, y3, wide(hstd), ALU.mult), ["hscale", "sq"], "yn")
            yield
            for t in range(2):
                def yn_T(e, i, t=t):
                    for n in range(4):
                        last = e.transpose(bank[0][:, n * P:(n + 1) * P], yr[:, t, n * P:(n + 1) * P], ident)
                    return last
                T(yn_T, ["yn", "bank0"], "ynT")
                A(lambda e, i, t=t: e.activation(
                    qT[c][:, :, t * P:(t + 1) * P], bank[0][:, 0:256].rearrange("p (t n) -> p t n", t=2), ACT.Identity,
                    bias=hcol[:, 1:2], scale=hcol[:, 0:1]), ["ynT", f"scores{c}", dh[-1]])
                for h2 in range(2):
                    for tt in range(2):
                        u = A(lambda e, i, t=t, h2=h2, tt=tt: e.activation(
                            kbd[c][:, tt, 2 * t:2 * t + 2, 64 * h2:64 * h2 + 64],
                            bank[0][:, 256 + tt * P:256 + (tt + 1) * P].rearrange("p (b l) -> p b l", b=2), ACT.Identity,
                            bias=kcol[:, h2, 1:2], scale=kcol[:, h2, 0:1]), ["ynT", f"scores{c}", "kcol"], f"keys{c}")
                pr.named("bank0", u)
                yield

        def softmax_steps(j, s, scale, tb=5, mb=2):
            p2 = j % 2

            def step_copy():
                A(lambda e, i: e.activation(ssb[p2][:, :], bank[s][:, :], ACT.Copy), [f"S{s}", f"ssbT{p2}"], f"ssb{p2}")

            def step_T():
                def go(e, i):
                    for n in range(4):
                        last = e.transpose(bank[tb][:, n * P:(n + 1) * P], ssb[p2][:, n * P:(n + 1) * P], ident)
                    return last
                T(go, [f"ssb{p2}", "maxs"], f"ssbT{p2}")
                V(lambda e, i: e.tensor_reduce(maxs[:, :], bank[tb][:, :].rearrange("p (n l) -> p n l", l=64), AX, ALU.max),
                  [f"ssbT{p2}", "mlow"], "maxs")
                V(lambda e, i: e.tensor_copy(mhl[:, 0:8], maxs[:, :]), ["maxs", "maxTT"], "mhigh")
                V(lambda e, i: e.tensor_tensor(mhl[:, 8:16], maxs[:, :], mhl[:, 0:8].bitcast(F32), ALU.subtract), ["mhigh"], "mlow")

            def step_maxT():
                T(lambda e, i: e.transpose(bank[mb][0:16, 0:P], mhl[:, :].bitcast(F32), ident), ["mlow", "maxT"], "maxTT")
                V(lambda e, i: e.tensor_copy(maxT[:, :], bank[mb][0:16, 0:P]), ["maxTT", "shift"], "maxT")

            def step_shift():
                def go(e, i):
                    for n in range(4):
                        last = mm(e, bank[s][:, n * P:(n + 1) * P], sel[:, n, :], maxT[:, :], False, n == 3)
                    return last
                T(go, ["maxT", f"ssb{p2}", "sel"], "shift")
                A(lambda e, i: e.activation(ex[p2][:, :], bank[s][:, :], ACT.Exp, scale=scale), ["shift", f"pv{p2}"], f"ex{p2}")
            return step_copy, step_T, step_maxT, step_shift

        def heads_back(blk, c):
            def scores(j):
                def go(e, i):
                    for tt in range(2):
                        for b in range(4):
                            r = slice(32 * j, 32 * j + 32)
                            last = mm(e, bank[3 + j % 2][:, (tt * 4 + b) * 64:(tt * 4 + b + 1) * 64],
                                      kbd[c][r, tt, b, :], qT[c][r, tt, b * 64:(b + 1) * 64],
                                      tt == 0 and b == 0, tt == 1 and b == 3)
                    return last
                T(go, [f"keys{c}", f"ex{j % 2}"], f"S{3 + j % 2}")
                pr.named(f"scores{c}", pr.last[f"S{3 + j % 2}"])

            def av(j):
                def go(e, i):
                    for tt in range(2):
                        for b in range(4):
                            n = tt * 4 + j
                            last = mm(e, bank[6 + b // 2][64 * (b % 2):64 * (b % 2) + 64, n * VW:(n + 1) * VW],
                                      ex[j % 2][:, (tt * 4 + b) * 64:(tt * 4 + b + 1) * 64],
                                      vbd[c][:, b, n * VW:(n + 1) * VW], True, True)
                    return last
                T(go, [f"ex{j % 2}", f"values{c}", "an"], f"pv{j % 2}")
                pr.named(f"av{c}", pr.last[f"pv{j % 2}"])

            steps = [softmax_steps(j, 3 + j % 2, 0.25) for j in range(4)]
            scores(0)
            steps[0][0]()
            yield
            for j in range(4):
                steps[j][1]()
                if j:
                    av(j - 1)
                steps[j][2]()
                yield
                if j < 3:
                    scores(j + 1)
                steps[j][3]()
                if j < 3:
                    steps[j + 1][0]()
                yield
            av(3)
            yield
            for t in range(2):
                o4 = bank[6 + t][:, 0:NP * VW].rearrange("p (n w) -> p n w", w=VW)
                V(lambda e, i, t=t, o4=o4: e.reciprocal(rden[:, t, :].rearrange("p (n w) -> p n w", w=2), o4[:, :, 2 * HD:VW]),
                  [f"av{c}", "an"], "rden")
                V(lambda e, i, t=t, o4=o4: e.tensor_tensor(
                    an[:, t, :].rearrange("p (n h d) -> p n h d", n=NP, h=2),
                    o4[:, :, 0:2 * HD].rearrange("p n (h d) -> p n h d", h=2),
                    rden[:, t, :].rearrange("p (n h o) -> p n h o", n=NP, o=1).broadcast_to([P, NP, 2, HD]), ALU.mult),
                  ["rden", "anT"], "an")
            yield

            def an_T(e, i):
                for k in range(KD):
                    for t in range(2):
                        last = e.transpose(bank[0][:, k * 256 + t * P:k * 256 + (t + 1) * P], an[:, t, k * P:(k + 1) * P], ident)
                return last
            T(an_T, ["an", "bank0"], "anT")
            A(lambda e, i: e.activation(aT[:, :, :], bank[0][:, :].rearrange("p (k n) -> p k n", k=KD), ACT.Copy), ["anT", "attn_out"], "aT")
            pr.named("bank0", pr.last["aT"])
            yield

            def proj_out(e, i):
                for t in range(2):
                    for k in range(KD):
                        last = mm(e, bank[1][:, t * 256:(t + 1) * 256], aT[:, k, t * P:(t + 1) * P], wo1[:, k, :], k == 0, k == KD - 1)
                return last
            T(proj_out, ["aT", "bank1"], "attn_out")
            two = tiles(lambda i: 2 * blk(i), 2)
            G(lambda e, i: e.tensor_tensor(two(i).rearrange("p (t d) -> p t d", t=2), two(i).rearrange("p (t d) -> p t d", t=2),
                                           borow[:, :].rearrange("p (o d) -> p o d", o=1).broadcast_to([P, 2, D]), ALU.add),
              ["borow", f"keys{c}"], "xb")
            V(lambda e, i: e.tensor_tensor(two(i), bank[1][:, :], two(i), ALU.add), ["attn_out", "xb"], "bank1")


        def interleave(*parts):
            parts = list(parts)
            while parts:
                for g in list(parts):
                    try:
                        next(g)
                    except StopIteration:
                        parts.remove(g)

        interleave(normed(lambda i: 0, 0))
        interleave(heads_front(lambda i: 0, 0), normed(lambda i: 1, 1))
        with pr.loop(3):
            interleave(heads_back(lambda i: 2 * i, 0), heads_front(lambda i: 2 * i + 1, 1), normed(lambda i: 2 * i + 2, 0))
            interleave(heads_back(lambda i: 2 * i + 1, 1), heads_front(lambda i: 2 * i + 2, 0), normed(lambda i: 2 * i + 3, 1))
        interleave(heads_back(lambda i: 6, 0), heads_front(lambda i: 7, 1))
        interleave(heads_back(lambda i: 7, 1))
        pr.barrier()

        if phases >= 2:
            bi = [0]

            def fold(mms, evacs):
                n = bi[0] % 8
                bi[0] += 1
                t = T(lambda e, i: mms(e, bank[n]), [f"fb{n}", dst[-1]])
                for eng, f in evacs(bank[n]):
                    t = (A if eng == "A" else V)(f, [t])
                pr.named(f"fb{n}", t)
                return t
            G(lambda e, i: e.memset(wqk[:, :, :, :, :, :], 0.0), name="wqk0")
            for hp in range(NP):
                for k in range(KD):
                    def mms(e, o, hp=hp, k=k):
                        for g in range(2):
                            last = mm(e, o[:, g * XQ:(g + 1) * XQ], wq_s[:, 2 * hp + g, k * P:(k + 1) * P], wkc_s[:, 2 * hp + g, :], True, True)
                        return last

                    def evacs(o, hp=hp, k=k):
                        src = o[:, 0:2 * XQ].rearrange("p (g t q) -> p g t q", g=2, t=2)
                        at = lambda w: w[:, k, :, 2 * hp * HQ:(2 * hp + 2) * HQ].rearrange("p t (g q) -> p g t q", g=2)
                        return [("A", lambda e, i: e.activation(at(wbh), src, ACT.Copy)),
                                ("V", lambda e, i: e.tensor_tensor(at(wbl), src, at(wbh).bitcast(F32), ALU.subtract))]
                    folded = fold(mms, evacs)
            for g8 in range(8):
                def mms(e, o, g8=g8):
                    for h in range(4):
                        last = e.transpose(o[0:XC, h * HQ:(h + 1) * HQ], wqr_s[:, (g8 // 2) * 4 + h, g8 % 2, :], ident[0:HQ, 0:HQ])
                    return last
                fold(mms, lambda o, g8=g8: [("A", lambda e, i: e.activation(wqrT[:, g8, :], o[0:XC, 0:4 * HQ], ACT.Copy))])
            for g in range(2):
                def mms(e, o, g=g):
                    for h in range(8):
                        last = e.transpose(o[0:XC, h * 64:(h + 1) * 64], wkr_s[:, 8 * g + h, :], ident[0:XC, 0:XC])
                    return last
                t = fold(mms, lambda o, g=g: [("A", lambda e, i: e.activation(
                    wkrT[:, 8 * g:8 * g + 8, :], o[0:XC, :].rearrange("p (h d) -> p h d", d=XC), ACT.Copy))])
            rows = {(0, 0): [(0, 96)], (1, 0): [(96, 128)], (1, 1): [(0, 64)], (2, 1): [(64, 128)],
                    (2, 2): [(0, 32)], (3, 2): [(32, 64), (64, 128)]}
            for (h, j), spans in rows.items():
                def mms(e, o, h=h, j=j):
                    for g8 in range(8):
                        last = mm(e, o[:, g8 * 64:(g8 + 1) * 64], wqrT[:, g8, j * P:(j + 1) * P], wkrT[:, (g8 // 2) * 4 + h, :], True, True)
                    return last

                def evacs(o, h=h, j=j, spans=spans):
                    pair, kt = h // 2, j - h // 2
                    res = []
                    for lo, hi in spans:
                        res.append(("A", lambda e, i, lo=lo, hi=hi: e.activation(
                            wqk[lo:hi, :, pair, :, kt, 64 * (h % 2):64 * (h % 2) + 64],
                            o[lo:hi, :].rearrange("p (g t d) -> p g t d", g=4, t=2), ACT.Copy)))
                    return res
                pr.gate.setdefault("tensor", []).append(t)
                pr.gate.setdefault("scalar", []).append(pr.last["wqk0"])
                fold(mms, evacs)
            for g in range(8):
                def mms(e, o, g=g):
                    for h in range(2):
                        for t in range(2):
                            last = e.transpose(o[:, (h * 2 + t) * P:(h * 2 + t + 1) * P], wo_s[:, t, (2 * g + h) * P:(2 * g + h + 1) * P], ident)
                    return last
                pr.gate.setdefault("vector", []).append(folded)
                t = fold(mms, lambda o, g=g: [("V", lambda e, i: e.tensor_copy(
                    woT[:, 2 * g:2 * g + 2, :], o[:, :].rearrange("p (h n) -> p h n", h=2)))])
            for g in range(4):
                def mms(e, o, g=g):
                    for q in range(2):
                        for h2 in range(2):
                            h = 4 * g + 2 * q + h2
                            last = mm(e, o[64 * h2:64 * h2 + 64, q * D:(q + 1) * D], wkv_s[:, h, :], woT[:, h, :], True, True)
                    return last
                pr.gate.setdefault("tensor", []).append(t)
                fold(mms, lambda o, g=g: [("A", lambda e, i: e.activation(
                    wop[:, 2 * g:2 * g + 2, :], o[:, :].rearrange("p (q n) -> p q n", q=2), ACT.Copy))])
            pr.barrier()

            cv = a["ctx_512"].rearrange("b l d -> l b d")

            def context_load(blk):
                for h in range(2):
                    def go(e, i, h=h):
                        f = blk(i)
                        src = cv[:, f * 8:f * 8 + 8, :] if isinstance(f, int) else cv[:, bass.ds(f * 8, 8), :]
                        return e.dma_start(ctxs[64 * h:64 * h + 64, :, :], src)
                    pr.dma("ctx", go, ["kvt"])

            def context(blk):
                bc = lambda n, lo, hi: C(n)[:, lo:hi].rearrange("p (o d) -> p o d", o=1).broadcast_to([P, 8, hi - lo])
                hc = XC // 2
                G(lambda e, i: e.tensor_tensor(kvr[:, :, :], ctxs[:, :, :], bc("kvc", 0, XC), ALU.mult), ["ctx", "kvbd", "kvt"], "kv_c")
                G(lambda e, i: e.tensor_tensor(kvt[:, :, 0:hc], ctxs[:, :, hc:XC], bc("kvs", 0, hc), ALU.mult), ["kvr"])
                G(lambda e, i: e.tensor_tensor(kvt[:, :, hc:XC], ctxs[:, :, 0:hc], bc("kvs", hc, XC), ALU.mult), ["kvr"], "kvt")
                G(lambda e, i: e.tensor_tensor(kvr[:, :, :], kvr[:, :, :], kvt[:, :, :], ALU.add), ["kv_c", "kvt"], "kvr")

            def context_diag():
                for h2 in range(2):
                    G(lambda e, i, h2=h2: e.tensor_tensor(
                        kvbd[:, :, 64 * h2:64 * h2 + 64], kvr[:, :, :],
                        C("half")[:, h2:h2 + 1].rearrange("p (o d) -> p o d", o=1).broadcast_to([P, 8, XC]), ALU.mult),
                        ["kvr", "ctxv", "kvbdT_ps"], "kvbd")

                def go(e, i):
                    for b in range(8):
                        last = e.transpose(bank[b // 4][:, (b % 4) * P:(b % 4 + 1) * P], kvbd[:, b, :], ident)
                    return last
                T(go, ["kvbd", "cn0", "cn1"], "kvbdT_ps")
                for n in range(2):
                    A(lambda e, i, n=n: e.activation(kvbdT[:, 4 * n:4 * n + 4, :], bank[n][:, :].rearrange("p (b c) -> p b c", c=P), ACT.Copy),
                      ["kvbdT_ps", "S2", "S3"], "kvbdT")

            def norm_vectors(blk, after):
                layer_norm("cross", lambda t: tiles(lambda i: 4 * blk(i) + t, 1), 4, False, after)

            def norm_T(after):
                for k in range(KD):
                    def go(e, i, k=k):
                        for t in range(4):
                            last = e.transpose(bank[6 + k][:, t * P:(t + 1) * P], xhat[:, t, k * P:(k + 1) * P], ident)
                        return last
                    T(go, ["xhat", "xtl"] + after, "xhatT")
                    A(lambda e, i, k=k: e.activation(xth[:, k, :], bank[6 + k][:, :], ACT.Copy), ["xhatT", "proj"], "xth")
                    V(lambda e, i, k=k: e.tensor_tensor(xtl[:, k, :], bank[6 + k][:, :], xth[:, k, :].bitcast(F32), ALU.subtract), ["xth"], "xtl")

            def queries():
                def half_products(g, j):
                    n = (3 * g + j) % 2
                    for half in range(2):
                        def go(e, i, half=half):
                            for k in range(KD):
                                lo = (4 * HQ * g) + P * j
                                last = mm3(e, bank[2 * half + n][:, :], wbh[:, k, half, lo:lo + P], wbl[:, k, half, lo:lo + P],
                                           xth[:, k, :], xtl[:, k, :], k == 0, k == KD - 1)
                            return last
                        T(go, ["xth", "xtl", f"rm{n}", "S2", "ex0", "ex1", "kvbdT", "cn0", "cn1"], "proj")
                    bc = lambda q: C("xrope").rearrange("p (j f s) -> p j f s", j=3, f=4)[:, j, q, :].rearrange(
                        "p (o s) -> p o s", o=1).broadcast_to([P, 8, S])
                    for m, (half, q) in enumerate(((0, 0), (1, 1), (1, 2), (0, 3))):
                        V(lambda e, i, m=m, half=half, q=q: e.tensor_tensor(
                            m4[n][m][:, :].rearrange("p (b s) -> p b s", s=S), bank[2 * half + n][:, :].rearrange("p (b s) -> p b s", s=S),
                            bc(q), ALU.mult), ["proj", f"rope{n}"], f"rm{n}")
                    r = (3 * g + j) % 6
                    G(lambda e, i: e.tensor_tensor(rope[r][0][:, :], m4[n][0][:, :], m4[n][1][:, :], ALU.subtract), [f"rm{n}", f"qk{r}"])
                    G(lambda e, i: e.tensor_tensor(rope[r][1][:, :], m4[n][2][:, :], m4[n][3][:, :], ALU.add), [f"rm{n}", f"qk{r}"], f"rope{n}")
                    pr.named(f"rope_{r}", pr.last[f"rope{n}"])

                def latents(g, pair):
                    o = bank[4 + pair]

                    def go(e, i):
                        for kt in range(2):
                            for half in range(2):
                                r = (3 * g + pair + kt) % 6
                                last = mm(e, o[:, :], wqk[:, g, pair, half, kt, :], rope[r][half][:, :], kt == 0 and half == 0, kt == 1 and half == 1)
                        return last
                    T(go, [f"rope_{(3 * g + pair + 1) % 6}", f"rope_{(3 * g + pair) % 6}", f"qb{pair}", "cn0", "cn1", "x_cross"], "lat")
                    pr.named(f"qk{(3 * g + pair) % 6}", pr.last["lat"])
                    if pair:
                        pr.named(f"qk{(3 * g + 2) % 6}", pr.last["lat"])
                    A(lambda e, i: e.activation(qc[:, 2 * g + pair, :], o[:, :], ACT.Copy), ["lat", "cross_out"], f"qb{pair}")
                todo = []
                for n in range(12):
                    g, j = divmod(n, 3)
                    half_products(g, j)
                    if j:
                        todo.append((n, g, j - 1))
                    while todo and todo[0][0] <= n - 2:
                        latents(*todo.pop(0)[1:])
                for q in todo:
                    latents(*q[1:])

            def cross_attention():
                def scores(b):
                    s = 2 + b % 2
                    T(lambda e, i: mm(e, bank[s][:, :], kvbdT[:, b, :], qc[:, :, b * 64:(b + 1) * 64], True, True),
                      ["qb0", "qb1", "kvbdT", f"ex{b % 2}", "rm0", "rm1"], f"S{s}")

                def context_sums(b):
                    n = b % 2

                    def go(e, i):
                        for q in range(4):
                            mm(e, bank[4][:, 2 * q:2 * q + 2], ex[n][:, q * P:(q + 1) * P], C("half"), True, True)
                        return mm(e, bank[n][:, :], kvbd[:, b, :], ex[n][:, :], True, True)
                    T(go, [f"ex{n}", f"cn{n}", "invT", "rm0", "rm1"], f"pv{n}")
                    pr.named("ctxv", pr.last[f"pv{n}"])
                    V(lambda e, i: e.reciprocal(inv[:, :], bank[4][:, 0:8]), [f"pv{n}", "ilow"], "inv")
                    V(lambda e, i: e.tensor_copy(ihl[:, 0:8], inv[:, :]), ["inv", "invTT"], "ihigh")
                    V(lambda e, i: e.tensor_tensor(ihl[:, 8:16], inv[:, :], ihl[:, 0:8].bitcast(F32), ALU.subtract), ["ihigh"], "ilow")

                def spread_a(b):
                    T(lambda e, i: e.transpose(bank[4][0:16, 0:P], ihl[:, :].bitcast(F32), ident), ["ilow", "invT"], "invTT")
                    V(lambda e, i: e.tensor_copy(invT[:, :], bank[4][0:16, 0:P]), ["invTT", "spread"], "invT")

                def spread_b(b):
                    n = b % 2

                    def go(e, i):
                        for q in range(4):
                            last = mm(e, bank[5][:, q * P:(q + 1) * P], selp[:, q, :], invT[:, :], True, True)
                        return last
                    T(go, ["invT", "selp", "rd0", "rd1", "qb1"], "spread")
                    A(lambda e, i: e.activation(rd[n][:, :], bank[5][:, :], ACT.Copy), ["spread", f"cn{n}"], f"rd{n}")

                def normalise(b):
                    n = b % 2
                    V(lambda e, i: e.tensor_tensor(
                        qc[:, :, b * 64:(b + 1) * 64], bank[n][:, :].rearrange("p (n s) -> p n s", s=S),
                        rd[n][:, :].rearrange("p (n s) -> p n s", s=S), ALU.mult), [f"rd{n}", f"S{2 + n}"], f"cn{n}")
                steps = [softmax_steps(b, 2 + b % 2, 1.0, 6, 7) for b in range(8)]
                scores(0)
                steps[0][0]()
                yield
                for b in range(8):
                    steps[b][1]()
                    if b > 1:
                        normalise(b - 2)
                    if b:
                        context_sums(b - 1)
                    steps[b][2]()
                    if b < 7:
                        scores(b + 1)
                        steps[b + 1][0]()
                    if b:
                        spread_a(b - 1)
                    steps[b][3]()
                    yield
                    if b:
                        spread_b(b - 1)
                    yield
                context_sums(7)
                normalise(6)
                spread_a(7)
                spread_b(7)
                normalise(7)

            def cross_out(blk):
                for half in range(2):
                    def go(e, i, half=half):
                        for t in range(2):
                            for n in range(NP):
                                tt = 2 * half + t
                                last = mm(e, bank[2 + half][:, t * D:(t + 1) * D], qc[:, n, tt * P:(tt + 1) * P], wop[:, n, :], n == 0, n == NP - 1)
                        return last
                    T(go, ["cn0", "cn1", "ex0", "ex1"], "cross_out")
                    two = tiles(lambda i, half=half: 4 * blk(i) + 2 * half, 2)
                    V(lambda e, i, two=two, half=half: e.tensor_tensor(two(i), bank[2 + half][:, :], two(i), ALU.add), ["cross_out"], "x_cross")
                pr.named("rm0", pr.last["x_cross"])
                pr.named("rm1", pr.last["x_cross"])

            def ahead(blk):
                context_load(blk)
                yield
                context(blk)
                yield
                norm_vectors(blk, [])
                yield

            def block2(blk, nxt):
                queries()
                interleave(cross_attention(), *([ahead(nxt)] if nxt else []))
                if nxt:
                    norm_T(["maxs", "maxT"])
                    context_diag()
                cross_out(blk)

            interleave(ahead(lambda i: 0))
            norm_T([])
            context_diag()
            with pr.loop(3):
                block2(lambda i: i, lambda i: i + 1)
            block2(lambda i: 3, None)
            pr.barrier()

        if phases >= 3:
            dwr = pr.dma("wr", lambda e, i: e.dma_start(wr[:, :, :], a["L0_ffn_Wr"].rearrange("(k p) n -> p k n", p=P)))
            V(lambda e, i: e.tensor_copy(wrh[:, :, :], wr[:, :, :]), [dwr], "wrh")
            V(lambda e, i: e.tensor_tensor(wrl[:, :, :], wr[:, :, :], wrh[:, :, :].bitcast(F32), ALU.subtract), ["wrh"], "wrl")

            def expert_weights(n):
                q = n % 3
                d = [pr.dma(f"raw{q}", lambda e, i, s=s, w=w: e.dma_start(raw[q][:, w, :, :], a[s][n].rearrange("(k p) f -> p k f", p=P)), [f"split{q}"])
                     for w, s in enumerate(["L0_ffn_Wg", "L0_ffn_Wu"])][-1]
                pr.dma(f"wd{n}", lambda e, i: e.dma_start(wd[:, n, :, :], a["L0_ffn_Wd"][n].rearrange("(k p) d -> p k d", p=P)))
                u = None
                for w, (hi, lo) in enumerate(((wgh, wgl), (wuh, wul))):
                    A(lambda e, i, w=w, hi=hi: e.activation(hi[:, n, :, :], raw[q][:, w, :, :], ACT.Copy), [d], "whigh")
                    u = G(lambda e, i, w=w, hi=hi, lo=lo: e.tensor_tensor(lo[:, n, :, :], raw[q][:, w, :, :], hi[:, n, :, :].bitcast(F32), ALU.subtract),
                          ["whigh"], f"split{q}")
                pr.named(f"we{n}", u)

            def norm3(blk, after):
                layer_norm("ffn", lambda t: tiles(lambda i: 4 * blk(i) + t, 1), 4, False, after)

            def norm3_T():
                for k in range(KD):
                    def go(e, i, k=k):
                        for t in range(4):
                            last = e.transpose(bank[6 + k][:, t * P:(t + 1) * P], xhat[:, t, k * P:(k + 1) * P], ident)
                        return last
                    T(go, ["xhat", "xtl", "elog"], "xhatT")
                    A(lambda e, i, k=k: e.activation(xth[:, k, :], bank[6 + k][:, :], ACT.Copy), ["xhatT", "proj"], "xth")
                    V(lambda e, i, k=k: e.tensor_tensor(xtl[:, k, :], bank[6 + k][:, :], xth[:, k, :].bitcast(F32), ALU.subtract), ["xth", "proj"], "xtl")

            def route():
                def logits(e, i):
                    for t in range(4):
                        for k in range(KD):
                            last = mm3(e, bank[6][:, t * E:(t + 1) * E], xth[:, k, t * P:(t + 1) * P], xtl[:, k, t * P:(t + 1) * P],
                                       wrh[:, k, :], wrl[:, k, :], k == 0, k == KD - 1)
                    return last
                T(logits, ["xtl", "wrl"], "logits")
                l3 = bank[6][:, 0:4 * E].rearrange("p (t n) -> p t n", n=E)
                bc = lambda v: v[:, :].rearrange("p (t o) -> p t o", o=1).broadcast_to([P, 4, E])
                V(lambda e, i: e.tensor_reduce(emax[:, :], l3, AX, ALU.max), ["logits", "ffn_acc"], "emax")
                V(lambda e, i: e.tensor_tensor(ew[:, :, :], l3, bc(emax), ALU.subtract), ["emax", "ffn_acc"], "elog")
                A(lambda e, i: e.activation(ew[:, :, :], ew[:, :, :], ACT.Exp), ["elog"], "eexp")
                before = C("before").rearrange("p (i j) -> p i j", j=E)
                for t in range(4):
                    mine = ew[:, t, :].rearrange("p (i o) -> p i o", o=1).broadcast_to([P, E, E])
                    other = ew[:, t, :].rearrange("p (o j) -> p o j", o=1).broadcast_to([P, E, E])
                    V(lambda e, i, mine=mine, other=other: e.tensor_tensor(cmpa[:, :, :], other, mine, ALU.is_gt), ["eexp", "rank"], "cmpa")
                    V(lambda e, i, mine=mine, other=other: e.tensor_tensor(cmpb[:, :, :], other, mine, ALU.is_equal), ["eexp", "rank"], "cmpb")
                    V(lambda e, i: e.tensor_tensor(cmpb[:, :, :], cmpb[:, :, :], before, ALU.mult), ["cmpb"], "cmpb")
                    V(lambda e, i: e.tensor_tensor(cmpa[:, :, :], cmpa[:, :, :], cmpb[:, :, :], ALU.add), ["cmpa", "cmpb"], "cmpa")
                    V(lambda e, i: e.tensor_reduce(rank[:, :], cmpa[:, :, :], AX, ALU.add), ["cmpa"], "rank")
                    V(lambda e, i, t=t: e.scalar_tensor_tensor(ew[:, t, :], rank[:, :], 2.0, ew[:, t, :], ALU.is_lt, ALU.mult), ["rank"], "rank")
                V(lambda e, i: e.tensor_reduce(esum[:, :], ew[:, :, :], AX, ALU.add), ["rank"], "esum")
                V(lambda e, i: e.reciprocal(esum[:, :], esum[:, :]), ["esum"], "esum")
                V(lambda e, i: e.tensor_tensor(ew[:, :, :], ew[:, :, :], bc(esum), ALU.mult), ["esum"], "ew")

            def gate_up(n):
                p2 = n % 2
                for f in range(KF):
                    for w, (hi, lo) in enumerate(((wgh, wgl), (wuh, wul))):
                        def go(e, i, f=f, w=w, hi=hi, lo=lo):
                            for k in range(KD):
                                last = mm3(e, bank[2 * w + f][:, :], hi[:, n, k, f * P:(f + 1) * P], lo[:, n, k, f * P:(f + 1) * P],
                                           xth[:, k, :], xtl[:, k, :], k == 0, k == KD - 1)
                            return last
                        T(go, ["xth", "xtl", f"gu{f}", f"we{n}"], "proj")
                        pr.named(f"gu_ps{w}", pr.last["proj"])
                    A(lambda e, i, f=f: e.activation(sg[f][:, :], bank[f][:, :], ACT.Silu), ["gu_ps0", f"gu{f}"], f"silu{f}")
                    V(lambda e, i, f=f: e.tensor_tensor(hh[p2][:, f, :], bank[2 + f][:, :], sg[f][:, :], ALU.mult),
                      ["gu_ps1", f"silu{f}", f"down{p2}"], f"gu{f}")
                    pr.named(f"hh{p2}", pr.last[f"gu{f}"])

            def down(n, blk):
                p2 = n % 2
                for half in range(2):
                    def go(e, i, half=half):
                        for t in range(2):
                            for k in range(KF):
                                tt = 2 * half + t
                                last = mm(e, bank[4 + half][:, t * D:(t + 1) * D], hh[p2][:, k, tt * P:(tt + 1) * P], wd[:, n, k, :], k == 0, k == KF - 1)
                        return last
                    T(go, [f"hh{p2}", f"acc{half}", f"wd{n}"], f"down{p2}")
                    for t in range(2):
                        tt = 2 * half + t
                        one = tiles(lambda i, tt=tt: 4 * blk(i) + tt, 1)
                        V(lambda e, i, t=t, tt=tt, one=one, half=half: e.scalar_tensor_tensor(
                            one(i), bank[4 + half][:, t * D:(t + 1) * D], ew[:, tt, n:n + 1], one(i), ALU.mult, ALU.add),
                          [f"down{p2}", "ew", f"acc{half}", "xhat"], f"acc{half}")
                        pr.named("ffn_acc", pr.last[f"acc{half}"])

            ov = out.rearrange("b s d -> (b s) d").rearrange("(t p) d -> p t d", p=P)

            def block3(blk, nxt):
                for n in range(E):
                    gate_up(n)
                    if n:
                        down(n - 1, blk)
                    if n == 4 and nxt:
                        norm3(nxt, [])
                if nxt:
                    norm3_T()
                down(E - 1, blk)

                def store(e, i):
                    f = blk(i)
                    d = ov[:, f * 4:f * 4 + 4, :] if isinstance(f, int) else ov[:, bass.ds(f * 4, 4), :]
                    s = x3[:, f * 4:f * 4 + 4, :] if isinstance(f, int) else x3[:, bass.ds(f * 4, 4), :]
                    return e.dma_start(d, s)
                pr.dma("out", store, ["ffn_acc"])
                if nxt:
                    route()

            norm3(lambda i: 0, [])
            for n in range(E):
                expert_weights(n)
                if n == 0:
                    norm3_T()
                    route()
            block3(lambda i: 0, lambda i: 1)
            with pr.loop(2):
                block3(lambda i: i + 1, lambda i: i + 2)
            block3(lambda i: 3, None)
            pr.barrier()
            pr.add("sync", lambda e, i: e.nop(), [], None)
        else:
            ov = out.rearrange("b s d -> (b s) d").rearrange("(t p) d -> p t d", p=P)
            pr.dma("out", lambda e, i: e.dma_start(ov, x3))
            pr.barrier()
            pr.add("sync", lambda e, i: e.nop(), [], None)
        pr.emit()


_INS = ["x", "ctx_512", "L0_attn_ln_q_g", "L0_attn_ln_q_b", "L0_attn_Wq", "L0_attn_bq", "L0_attn_ln_kv_g", "L0_attn_ln_kv_b",
        "L0_attn_Wkv", "L0_attn_bkv", "L0_attn_ln_h_g", "L0_attn_ln_h_b", "L0_attn_Wo", "L0_attn_bo", "L0_xattn_Wq",
        "L0_xattn_w_kc_q", "L0_xattn_w_kc_kv", "L0_xattn_W_qr", "L0_xattn_W_kr", "L0_xattn_Wo", "L0_ffn_Wr", "L0_ffn_Wg",
        "L0_ffn_Wu", "L0_ffn_Wd"]
PHASES = 3


def kernel(**inputs):
    import concourse.bacc as bacc
    from concourse.bass_utils import run_bass_kernel_spmd

    nc = bacc.Bacc("TRN2", target_bir_lowering=False, num_devices=1)
    arrays, aps = {}, {}

    def give(name, array):
        arrays[f"in_{name}"] = array
        return nc.dram_tensor(f"in_{name}", array.shape, mybir.dt.from_np(array.dtype), kind="ExternalInput").ap()

    for name in _INS:
        aps[name] = give(name, np.ascontiguousarray(inputs[name]))
    parts, at, n = [], {}, 0
    for name, c in constants().items():
        at[name] = (n, n + c.shape[1])
        n += c.shape[1]
        parts.append(c)
    at["_"] = n
    const = give("constants", np.ascontiguousarray(np.concatenate(parts, axis=1)))
    out = nc.dram_tensor("out", (B, S, D), F32, kind="ExternalOutput").ap()
    decoder(nc, aps, const, at, out, PHASES)
    return run_bass_kernel_spmd(nc, [arrays], core_ids=[0]).results[0]["out"]
```

```python
from contextlib import ExitStack, contextmanager

import numpy as np

import concourse.bass as bass
from concourse import mybir

F32 = mybir.dt.float32
F32R = mybir.dt.float32r
I32 = mybir.dt.int32
ALU = mybir.AluOpType
ACT = mybir.ActivationFunctionType
AX = mybir.AxisListType.X
EPS = 1e-5

B, S, D = 32, 64, 256
P = 128
NT = B * S // P
KD = D // P
H, HD = 16, 16
NP = H // 2
VW = 2 * HD + 2
XH, XK, XC, XQ = 16, 128, 64, 192
HQ = XQ // 2
E, F = 8, 256
KF = F // P


def constants():
    p = np.arange(P)
    c = {}
    c["ident"] = np.eye(P)
    c["ones"] = np.ones((P, P))
    c["half"] = np.stack([p < 64, p >= 64], 1)
    c["parity"] = np.stack([p // HD % 2 == 0, p // HD % 2 == 1], 1)
    f = (np.float32(8000.0 / 200.0) ** np.linspace(0.0, 1.0, HD // 2, dtype=np.float32)) * np.float32(200.0) / np.float32(1000.0)
    f = (np.float32(200.0) * f / np.float32(1000.0)).astype(np.float32)
    ang = ((p % S).astype(np.float32)[:, None] * f[None, :]).astype(np.float32).astype(np.float64)
    c["rotc"], c["rots"] = np.cos(ang), np.sin(ang)

    def angles(pos, dim):
        inv = (np.float32(1.0) / np.float32(10000.0) ** (np.arange(0, dim, 2, dtype=np.float32) / np.float32(dim))).astype(np.float32)
        return (pos.astype(np.float32)[:, None] * inv[None, :]).astype(np.float32).astype(np.float64)
    a = np.repeat(angles(p % S, XC), 2, axis=1)
    c["kvc"] = np.cos(a)
    c["kvs"] = np.sin(a) * np.where(np.arange(XC) < XC // 2, -1.0, 1.0)
    a = np.repeat(angles(np.arange(S), XQ), 2, axis=1)
    t = np.zeros((P, 3, 4, S))
    for j in range(3):
        i = (P * j + p) % HQ
        t[:, j, 0], t[:, j, 1] = np.cos(a[:, i]).T, np.sin(a[:, i]).T
        t[:, j, 2], t[:, j, 3] = np.cos(a[:, HQ + i]).T, np.sin(a[:, HQ + i]).T
    c["xrope"] = t.reshape(P, -1)
    sel = np.zeros((P, 4, P))
    for hl in range(2):
        for x in range(4):
            for h2 in range(2):
                sel[hl * 8 + x * 2 + h2, x, 64 * h2:64 * h2 + 64] = -1.0
    c["sel"] = sel.reshape(P, -1)
    i = np.arange(E)
    c["before"] = np.tile((i[None, :] < i[:, None]).astype(np.float64).reshape(1, -1), (P, 1))
    c["power"] = np.tile(np.array([[-0.5, -0.5, 0.5, 0.5] + [-0.5] * 32]), (P, 1))
    return {k: np.ascontiguousarray(v, dtype=np.float32) for k, v in c.items()}


class Counter:

    def __init__(self, sem, step):
        self.sem, self.step, self.counts = sem, step, [0]

    def count_up(self, k):
        self.counts += [0] * (k + 1 - len(self.counts))
        self.counts[k] += 1
        return Done(self, k, self.counts[k])


class Done:

    def __init__(self, counter, k, n):
        self.counter, self.k, self.n = counter, k, n


class Carried:

    def __init__(self, name, k, first):
        self.name, self.k, self.first = name, k, first


class Program:
    def __init__(self, nc, ctx):
        self.nc, self.ctx = nc, ctx
        self.trips = [1]
        self.queues = {e: [[]] for e in ("tensor", "vector", "scalar", "gpsimd", "sync")}
        self.counters = {e: Counter(self.semaphore("done_" + e), 1) for e in self.queues if e != "sync"}
        self.channels = {}
        self.last = {}
        self.finals = {}
        self.gate = {}

    def semaphore(self, name):
        return self.ctx.enter_context(self.nc.semaphore(name))

    @property
    def k(self):
        return len(self.trips) - 1

    def segment(self, trips):
        self.trips.append(trips)
        for q in self.queues.values():
            q.append([])

    @contextmanager
    def loop(self, trips):
        self.segment(trips)
        self.inside = set()
        yield
        self.finals[self.k] = dict(self.last)
        self.segment(1)

    def ref(self, name):
        if self.trips[-1] > 1 and name not in self.inside:
            return Carried(name, self.k, self.last.get(name))
        return self.last.get(name)

    def do(self, engine, fn, after=(), name=None):
        done = self.counters[engine].count_up(self.k)
        self.add(engine, fn, after, self.counters[engine])
        return self.named(name, done)

    def dma(self, channel, fn, after=(), name=None, engine="sync"):
        if channel not in self.channels:
            self.channels[channel] = Counter(self.semaphore("dma_" + channel), 16)
        done = self.channels[channel].count_up(self.k)
        self.add(engine, fn, after, self.channels[channel])
        return self.named(name or channel, done)

    def named(self, name, done):
        if name:
            self.last[name] = done
            if self.trips[-1] > 1:
                self.inside.add(name)
        return done

    def add(self, engine, fn, after, counter):
        after = [self.ref(a) if isinstance(a, str) else a for a in after] + self.gate.pop(engine, [])
        self.queues[engine][-1].append((fn, [a for a in after if a], counter))

    def barrier(self):
        ends = [Done(c, self.k, 0) for c in list(self.counters.values()) + list(self.channels.values())]
        for d in ends:
            d.n = d.counter.counts[self.k] if self.k < len(d.counter.counts) else 0
        self.gate = {e: list(ends) for e in self.queues}

    def base(self, c, k):
        return sum(n * t for n, t in zip(c.counts[:k], self.trips[:k]))

    def count(self, c, k):
        return c.counts[k] if k < len(c.counts) else 0

    def value(self, d, k):
        if isinstance(d, Carried):
            first = self.value(d.first, k) if d.first else []
            end = self.finals[d.k].get(d.name)
            if end is None or end.k != d.k:
                return first
            c, per = end.counter, self.count(end.counter, k)
            assert self.base(c, k) >= 1, "a wait for a register's value needs to be positive"
            const = max(self.base(c, k) - per + end.n, 1)
            if first and first[0][0] is c:
                const = max(const, first[0][1])
            return first + [(c, const, per)]
        c = d.counter
        if d.k == k and self.trips[k] > 1:
            return [(c, self.base(c, k) + d.n, self.count(c, k))]
        return [(c, self.base(c, d.k) + (self.trips[d.k] - 1) * self.count(c, d.k) + d.n, 0)]

    def emit(self):
        with self.nc.Block() as block:
            for engine, segments in self.queues.items():
                def body(e, segments=segments):
                    known = {}
                    for k, steps in enumerate(segments):
                        if not steps:
                            continue
                        waits = [[v for a in after for v in self.value(a, k)] for _, after, _ in steps]
                        if self.trips[k] == 1:
                            self.run(e, steps, waits, None, known)
                            continue
                        for w in waits:
                            for c, const, per in w:
                                if not per and known.get(c, 0) < const:
                                    e.wait_ge(c.sem, const * c.step)
                                    known[c] = const
                        with e.Fori(0, self.trips[k]) as i:
                            self.run(e, steps, waits, i, dict(known))
                {"tensor": block.tensor, "vector": block.vector, "scalar": block.scalar,
                 "gpsimd": block.gpsimd, "sync": block.sync}[engine](body)

    def run(self, e, steps, waits, i, known):
        moving = {}
        for (fn, _, counter), w in zip(steps, waits):
            for c, const, per in w:
                if per:
                    if moving.get(c, -1) < const:
                        e.wait_ge(c.sem, (i * per + const) * c.step)
                        moving[c] = const
                elif known.get(c, 0) < const:
                    e.wait_ge(c.sem, const * c.step)
                    known[c] = const
            last = fn(e, i)
            if counter:
                last.then_inc(counter.sem, counter.step)


class Space:

    def __init__(self, nc, start):
        self.nc, self.at = nc, start

    def __call__(self, name, shape, dt=F32):
        t = self.nc.alloc_sbuf_tensor_at(name, shape, dt, offset=self.at)
        self.at += (4 * int(np.prod(shape[1:])) + 31) // 32 * 32
        assert self.at <= 229300, (name, self.at)
        return t


def decoder(nc, a, const_dram, const_at, out, phases=3):
    ctx = ExitStack()
    with ctx:
        pr = Program(nc, ctx)
        T = lambda fn, after=(), name=None: pr.do("tensor", fn, after, name)
        V = lambda fn, after=(), name=None: pr.do("vector", fn, after, name)
        A = lambda fn, after=(), name=None: pr.do("scalar", fn, after, name)
        G = lambda fn, after=(), name=None: pr.do("gpsimd", fn, after, name)
        ctx.enter_context(nc.allow_non_contiguous_dma(reason="small parameter vectors"))

        bank = [ctx.enter_context(nc.psum_tensor(f"bank{i}", [P, 512], F32)) for i in range(8)]

        keep = Space(nc, 16512)
        x = keep("x", [P, NT * D])
        cst = keep("cst", [P, const_at["_"]])
        C = lambda name: cst[:, const_at[name][0]:const_at[name][1]]
        sel = keep("sel", [16, 4, P], F32R)
        stat = keep("stat", [P, 4, 6])
        mv = keep("mv", [P, 4, 2])
        gate_word = keep("gate_word", [P, 1])
        rstd = keep("rstd", [P, 4])
        small = keep("small", [P, 4])
        top = keep("top", [P, 4])
        hrow = [keep(f"hrow{i}", [P, 4]) for i in range(2)]
        maxT = keep("maxT", [16, P], F32R)
        maxs = keep("maxs", [P, 8])
        mhl = keep("mhl", [P, 16], F32R)
        selp = keep("selp", [16, 4, P], F32R)
        inv = keep("inv", [P, 8])
        ihl = keep("ihl", [P, 16], F32R)
        invT = keep("invT", [16, P], F32R)
        ssb = [keep(f"ssb{i}", [P, 512]) for i in range(2)]
        ex = [keep(f"ex{i}", [P, 512]) for i in range(2)]
        xhat = keep("xhat", [P, 4, D])
        xth = keep("xth", [P, KD, 512], F32R)
        xtl = keep("xtl", [P, KD, 512], F32R)
        ident = C("ident")

        s1 = Space(nc, keep.at)
        yr = [Space(nc, s1.at)("yr0", [P, 2, 512])]
        w1 = s1("w1", [P, KD, 3 * D])
        w1h, w1l = s1("w1h", [P, KD, 3 * D], F32R), s1("w1l", [P, KD, 3 * D], F32R)
        wo1 = s1("wo1", [P, KD, D])
        lncol = s1("lncol", [P, 4, KD])
        hcol = s1("hcol", [P, 2])
        kcol = s1("kcol", [P, 2, 2])
        bwide = s1("bwide", [P, 2, KD, P])
        brow = s1("brow", [P, 4 * D])
        crow = s1("crow", [P, 3 * D])
        cvT = s1("cvT", [P, KD, P])
        borow = s1("borow", [P, D])
        crh, crl = s1("crh", [P, 512], F32R), s1("crl", [P, 512], F32R)
        onesr = s1("onesr", [P, P], F32R)
        qkb = s1("qkb", [P, 2, 512])
        prod = [s1(f"prod{i}", [P, 512]) for i in range(4)]
        yr.append(s1("yr1", [P, 2, 512]))
        sq = s1("sq", [P, 2, 512])
        hsum = s1("hsum", [P, 64])
        hvar = s1("hvar", [P, 64])
        half_v = s1("half_v", [P, 64])
        newton = s1("newton", [P, 64])
        hstd = s1("hstd", [P, 64])
        qT = [s1(f"qT{i}", [P, 2, 256]) for i in range(2)]
        kbd = [s1(f"kbd{i}", [P, 2, 4, P]) for i in range(2)]
        vbd = [s1(f"vbd{i}", [P, 4, NP * VW]) for i in range(2)]
        rden = s1("rden", [P, 2, 16])
        an = s1("an", [P, 2, D])
        aT = s1("aT", [P, KD, 256])
        w2 = Space(nc, keep.at)
        wbh = w2("wbh", [P, KD, 2, XH * HQ], F32R)
        wbl = w2("wbl", [P, KD, 2, XH * HQ], F32R)
        wqk = w2("wqk", [P, 4, 2, 2, 2, P])
        wop = w2("wop", [P, NP, D])
        third = max(s1.at, w2.at)
        s2 = Space(nc, third)
        wq_s = s2("wq_s", [P, XH, D])
        wkc_s = s2("wkc_s", [P, XH, XQ])
        wqr_s = s2("wqr_s", [HQ, XH, 2, XC])
        wkr_s = s2("wkr_s", [XC, XH, XC])
        wkv_s = s2("wkv_s", [P, XH, XC])
        wo_s = s2("wo_s", [P, 2, XH * XK])
        woT = Space(nc, third)("woT", [P, XH, D])
        wqrT = s2("wqrT", [XC, 8, 4 * HQ])
        wkrT = s2("wkrT", [XC, XH, XC])
        a2 = Space(nc, third)
        ctxs = a2("ctxs", [P, 8, XC])
        kvt = a2("kvt", [P, 8, XC])
        kvr = a2("kvr", [P, 8, XC])
        kvbd = a2("kvbd", [P, 8, P])
        kvbdT = a2("kvbdT", [P, 8, P])
        m4 = [[a2(f"m{i}_{n}", [P, 512]) for n in range(4)] for i in range(2)]
        rope = [[a2(f"r{i}_{n}", [P, 512]) for n in range(2)] for i in range(6)]
        qc = a2("qc", [P, NP, 512])
        rd = [a2(f"rd{i}", [P, 512]) for i in range(2)]
        s3 = Space(nc, keep.at)
        wgh, wgl = s3("wgh", [P, E, KD, F], F32R), s3("wgl", [P, E, KD, F], F32R)
        wuh, wul = s3("wuh", [P, E, KD, F], F32R), s3("wul", [P, E, KD, F], F32R)
        wd = s3("wd", [P, E, KF, D])
        wr, wrh, wrl = s3("wr", [P, KD, E]), s3("wrh", [P, KD, E], F32R), s3("wrl", [P, KD, E], F32R)
        raw = [s3(f"raw{i}", [P, 2, KD, F]) for i in range(3)]
        sg = [s3(f"sg{i}", [P, 512]) for i in range(2)]
        hh = [s3(f"hh{i}", [P, KF, 512]) for i in range(2)]
        ew = s3("ew", [P, 4, E])
        emax = s3("emax", [P, 4])
        esum = s3("esum", [P, 4])
        rank = s3("rank", [P, E])
        cmpa, cmpb = s3("cmpa", [P, E, E]), s3("cmpb", [P, E, E])

        def mm(e, o, l, r, start, stop):
            return e.matmul(o, l, r, start=start, stop=stop, skip_group_check=True)

        def mm3(e, o, lh, ll, rh, rl, start, stop):
            mm(e, o, lh, rh, start, False)
            mm(e, o, lh, rl, False, False)
            return mm(e, o, ll, rh, False, stop)

        def tiles(first, n):
            def at(i):
                f = first(i)
                if isinstance(f, int):
                    return x[:, f * D:(f + n) * D]
                return x[:, bass.ds(f * D, n * D)]
            return at

        xv = a["x"].rearrange("b s d -> (b s) d").rearrange("(t p) d -> p t d", p=P)
        x3 = x[:, :].rearrange("p (t d) -> p t d", d=D)
        dx0 = pr.dma("x0", lambda e, i: e.dma_start(x3[:, 0:2, :], xv[:, 0:2, :]))
        dcst = pr.dma("cst", lambda e, i: e.dma_start(cst[:, :], const_dram), engine="scalar")
        dw = [pr.dma("w1q", lambda e, i: e.dma_start(w1[:, :, 0:D], a["L0_attn_Wq"].rearrange("(k p) n -> p k n", p=P))),
              pr.dma("w1kv", lambda e, i: e.dma_start(w1[:, :, D:3 * D], a["L0_attn_Wkv"].rearrange("(k p) n -> p k n", p=P)))]
        dln = [pr.dma("ln", lambda e, i, n=n, s=s: e.dma_start(lncol[:, n, :], a[s].rearrange("(k p) -> p k", p=P)), engine="scalar")
               for n, s in enumerate(["L0_attn_ln_q_g", "L0_attn_ln_q_b", "L0_attn_ln_kv_g", "L0_attn_ln_kv_b"])]
        dbr = [pr.dma("brow", lambda e, i, s=s, lo=lo, hi=hi: e.dma_start(
            brow[:, lo:hi], a[s].rearrange("(o n) -> o n", o=1).broadcast_to([P, hi - lo])), engine="scalar")
            for s, lo, hi in (("L0_attn_bq", 0, D), ("L0_attn_bkv", D, 3 * D), ("L0_attn_bo", 3 * D, 4 * D))]
        dh = [pr.dma("hcol", lambda e, i, n=n, s=s, r=r: e.dma_start(
            hcol[r * HD:(r + 1) * HD, n:n + 1], a[s].rearrange("(d o) -> d o", o=1)), engine="sync")
            for n, s in enumerate(["L0_attn_ln_h_g", "L0_attn_ln_h_b"]) for r in range(8)]
        dwo = pr.dma("wo1", lambda e, i: e.dma_start(wo1[:, :, :], a["L0_attn_Wo"].rearrange("(k p) n -> p k n", p=P)))
        dx1 = [pr.dma("x1", lambda e, i, t=t: e.dma_start(x3[:, t:t + 7, :], xv[:, t:t + 7, :])) for t in (2, 9)]
        stage_loads = [
            (wq_s[:, :, :], a["L0_xattn_Wq"].rearrange("(h k) i -> k h i", k=XK)),
            (wkc_s[:, :, :], a["L0_xattn_w_kc_q"].rearrange("h k q -> k h q")),
            (wqr_s[:, :, 0, :], a["L0_xattn_W_qr"][:, 0:HQ, :].rearrange("h q r -> q h r")),
            (wqr_s[:, :, 1, :], a["L0_xattn_W_qr"][:, HQ:XQ, :].rearrange("h q r -> q h r")),
            (wkr_s[:, :, :], a["L0_xattn_W_kr"].rearrange("h d r -> d h r")),
            (wkv_s[:, :, :], a["L0_xattn_w_kc_kv"].rearrange("h k d -> k h d")),
            (wo_s[:, :, :], a["L0_xattn_Wo"].rearrange("(t o) n -> o t n", o=P)),
        ]
        dst = [pr.dma("stage", lambda e, i, o=o, s=s: e.dma_start(o, s)) for o, s in stage_loads]

        A(lambda e, i: e.activation(sel[:, :, :], C("sel").rearrange("p (x c) -> p x c", x=4)[0:16], ACT.Copy), [dcst], "sel")
        A(lambda e, i: e.activation(selp[:, :, :], C("sel").rearrange("p (x c) -> p x c", x=4)[0:16], ACT.Copy, scale=-1.0), [dcst], "selp")
        zero = [G(lambda e, i, t=t: e.memset(t[:, :, :], 0.0)) for t in (vbd[0], vbd[1])]
        for t in (vbd[0], vbd[1]):
            G(lambda e, i, t=t: e.tensor_copy(
                t[:, :, :].rearrange("p b (n w) -> p (b n) w", w=VW)[:, :, 2 * HD:VW],
                C("half").rearrange("p (o w) -> p o w", o=1).broadcast_to([P, 4 * NP, 2])), [dcst, zero[-1]], "vones")
        for k in range(KD):
            for n, lo, hi in ((0, 0, D), (2, D, 3 * D)):
                V(lambda e, i, k=k, n=n, lo=lo, hi=hi: e.tensor_scalar(
                    w1h[:, k, lo:hi], w1[:, k, lo:hi], lncol[:, n, k:k + 1], None, ALU.mult), [dw[-1], dw[0], dln[-1]], "w1h")
                V(lambda e, i, k=k, n=n, lo=lo, hi=hi: e.scalar_tensor_tensor(
                    w1l[:, k, lo:hi], w1[:, k, lo:hi], lncol[:, n, k:k + 1], w1h[:, k, lo:hi].bitcast(F32),
                    ALU.mult, ALU.subtract), ["w1h"], "w1l")
        for n in range(2):
            for k in range(KD):
                V(lambda e, i, n=n, k=k: e.tensor_scalar(bwide[:, n, k, :], C("ones"), lncol[:, 2 * n + 1, k:k + 1], None, ALU.mult),
                  [dcst], "bwide")
        for n in range(2):
            V(lambda e, i, n=n: e.tensor_scalar(kcol[:, n, :], hcol[:, :], C("parity")[:, n:n + 1], None, ALU.mult), [dh[-1]], "kcol")

        def bias_rows(e, i):
            for k in range(KD):
                mm(e, bank[0][:, 0:D], bwide[:, 0, k, :], w1[:, k, 0:D], k == 0, k == KD - 1)
            for k in range(KD):
                last = mm(e, bank[1][:, :], bwide[:, 1, k, :], w1[:, k, D:3 * D], k == 0, k == KD - 1)
            return last
        t = T(bias_rows, ["bwide", dw[0], dw[-1]])
        V(lambda e, i: e.tensor_tensor(crow[:, 0:D], bank[0][:, 0:D], brow[:, 0:D], ALU.add), [t, dbr[-1]])
        t = V(lambda e, i: e.tensor_tensor(crow[:, D:3 * D], bank[1][:, :], brow[:, D:3 * D], ALU.add), name="crow")
        V(lambda e, i: e.tensor_copy(crh[:, :], crow[:, 0:512]), ["crow"], "crh")
        V(lambda e, i: e.tensor_tensor(crl[:, :], crow[:, 0:512], crh[:, :].bitcast(F32), ALU.subtract), ["crh"])
        V(lambda e, i: e.tensor_copy(onesr[:, :], C("ones")), [dcst], "crow_split")

        def value_bias_T(e, i):
            for k in range(KD):
                last = e.transpose(bank[2][:, k * P:(k + 1) * P], crow[:, 2 * D + k * P:2 * D + (k + 1) * P], ident)
            return last
        t = T(value_bias_T, [t, dcst])
        t = A(lambda e, i: e.activation(cvT[:, :, :], bank[2][:, 0:2 * P].rearrange("p (k c) -> p k c", k=KD), ACT.Copy), [t])

        def out_bias(e, i):
            for k in range(KD):
                last = mm(e, bank[3][:, 0:D], cvT[:, k, :], wo1[:, k, :], k == 0, k == KD - 1)
            return last
        t = T(out_bias, [t, dwo])
        V(lambda e, i: e.tensor_tensor(borow[:, :], bank[3][:, 0:D], brow[:, 3 * D:4 * D], ALU.add), [t], "borow")

        def layer_norm(tag, xs, n, self_attn, after):
            for t in range(n):
                V(lambda e, i, t=t: e.bn_stats(stat[:, t, :], xs(t)(i)), list(after) + ["mv"], "stat")
            V(lambda e, i: e.memset(gate_word[:, :], 0.0), ["stat", "xhat"], "gate_word")
            for t in range(n):
                V(lambda e, i, t=t: e.bn_aggr(mv[:, t, :], stat[:, t, :]), ["stat", "xhat"], "mv")
            var = mv[:, 0:n, 1]
            if self_attn:
                V(lambda e, i: e.tensor_scalar(small[:, 0:2], var, 1.0 + EPS, EPS * EPS, ALU.mult, ALU.add), ["mv", "rstd"])
                u = V(lambda e, i: e.tensor_scalar(small[:, 2:4], var, EPS, None, ALU.add), ["mv"])
                u = V(lambda e, i: e.reciprocal(small[:, 2:4], small[:, 2:4]), [u])
                u = V(lambda e, i: e.scalar_tensor_tensor(top[:, 2:4], var, 4.0, small[:, 2:4], ALU.mult, ALU.mult), [u, "hstd"])
                u = V(lambda e, i: e.tensor_copy(top[:, 0:2], small[:, 0:2]), [u])
                G(lambda e, i: e.tensor_tensor(rstd[:, :], top[:, 0:4], C("power")[:, 0:4], ALU.pow), [u, "xhat", "hstd"], "rstd")
            else:
                u = V(lambda e, i: e.tensor_scalar(small[:, 0:n], var, EPS, None, ALU.add), ["mv", "rstd"])
                G(lambda e, i: e.tensor_tensor(rstd[:, 0:n], small[:, 0:n], C("power")[:, 4:4 + n], ALU.pow), [u, "xhat"], "rstd")

            def scale():
                for t in range(n):
                    V(lambda e, i, t=t: e.tensor_scalar(xhat[:, t, :], xs(t)(i), mv[:, t, 0:1], rstd[:, t:t + 1],
                                                        ALU.subtract, ALU.mult), ["rstd", "xhatT"], "xhat")
            return scale

        def normed(blk, c):
            yield from idle(6)
            scale = layer_norm("self", lambda t: tiles(lambda i: 2 * blk(i) + t, 1), 2, True, [dx0, dx1[-1]] if c or blk(0) else [dx0])
            yield from idle(3)
            scale()

        def normed_T(c):
            at = slice(256 * c, 256 * c + 256)
            yield from idle(1)

            def xhat_T(e, i):
                for k in range(KD):
                    for t in range(2):
                        last = e.transpose(bank[0][:, k * 256 + t * P:k * 256 + (t + 1) * P], xhat[:, t, k * P:(k + 1) * P], ident)
                return last
            T(xhat_T, ["xhat", "bank0", dcst], "xhatT")
            src = bank[0][:, :].rearrange("p (k n) -> p k n", k=KD)
            A(lambda e, i: e.activation(xth[:, :, at], src, ACT.Copy), ["xhatT", f"proj{c}"], "xth")
            V(lambda e, i: e.tensor_tensor(xtl[:, :, at], src, xth[:, :, at].bitcast(F32), ALU.subtract), ["xth", f"proj{c}"], "bank0")
            pr.named(f"xt{c}", pr.last["bank0"])
            V(lambda e, i: e.tensor_copy(hrow[c][:, 0:2], top[:, 2:4]), ["hrow_read"])
            V(lambda e, i: e.tensor_scalar(hrow[c][:, 2:4], rstd[:, 2:4], 4.0, None, ALU.mult), ["rstd", "hrow_read"], f"hrow{c}")
            pr.named("hstd", pr.last[f"hrow{c}"])

        cols = lambda c, t: slice(256 * c + t * P, 256 * c + (t + 1) * P)

        def project_rotate(c):
            yield from idle(5)
            for t in range(2):
                def qk(e, i, t=t):
                    o = bank[1 + t]
                    mm(e, o[:, :], onesr[0:1, :], crh[0:1, :], True, False)
                    mm(e, o[:, :], onesr[0:1, :], crl[0:1, :], False, False)
                    for k in range(KD):
                        last = mm3(e, o[:, :], xth[:, k, cols(c, t)], xtl[:, k, cols(c, t)],
                                   w1h[:, k, 0:512], w1l[:, k, 0:512], False, k == KD - 1)
                    return last
                T(qk, [f"xt{c}", f"bank{1 + t}", "w1l", "crow_split"], "qk")
                A(lambda e, i, t=t: e.activation(qkb[:, t, :], bank[1 + t][:, :], ACT.Copy), ["qk", "rot_g", "rot_v"], f"bank{1 + t}")
                pr.named("qkb", pr.last[f"bank{1 + t}"])
                yield from idle(2 - t)

            pair = qkb[:, :, :].rearrange("p t (h f two) -> p (t h) f two", f=8, two=2)
            ev, od = pair[:, :, :, 0], pair[:, :, :, 1]
            yp = yr[c][:, :, :].rearrange("p t (h f two) -> p (t h) f two", f=8, two=2)
            cc = C("rotc").rearrange("p (o f) -> p o f", o=1).broadcast_to([P, 64, 8])
            ss = C("rots").rearrange("p (o f) -> p o f", o=1).broadcast_to([P, 64, 8])
            pv = [q[:, :].rearrange("p (h f) -> p h f", f=8) for q in prod]
            G(lambda e, i: e.tensor_tensor(pv[2], ev, ss, ALU.mult), ["qkb", "rot_g"], "p2")
            V(lambda e, i: e.tensor_tensor(pv[3], od, cc, ALU.mult), ["qkb", "rot_g"], "p3")
            G(lambda e, i: e.tensor_tensor(yp[:, :, :, 1], pv[2], pv[3], ALU.add), ["p2", "p3", f"ynT{c}"], "rot_g")
            V(lambda e, i: e.tensor_tensor(pv[0], ev, cc, ALU.mult), ["qkb", "rot_v"], "p0")
            yield
            V(lambda e, i: e.tensor_tensor(pv[1], od, ss, ALU.mult), ["qkb", "rot_v"], "p1")
            V(lambda e, i: e.tensor_tensor(yp[:, :, :, 0], pv[0], pv[1], ALU.subtract), ["p0", "p1", f"ynT{c}"], "rot_v")

        def head_norm(c):
            def vv(e, i):
                for t in range(2):
                    for k in range(KD):
                        last = mm3(e, bank[1][:, t * D:(t + 1) * D], xth[:, k, cols(c, t)], xtl[:, k, cols(c, t)],
                                   w1h[:, k, 512:768], w1l[:, k, 512:768], k == 0, k == KD - 1)
                return last
            y3 = yr[c][:, :, :].rearrange("p t (h d) -> p (t h) d", d=HD)
            wide = lambda v: v[:, :].rearrange("p (h o) -> p h o", o=1).broadcast_to([P, 64, HD])
            V(lambda e, i: e.tensor_reduce(hsum[:, :], y3, AX, ALU.add), ["rot_v", "rot_g"], "hsum")
            yield
            V(lambda e, i: e.scalar_tensor_tensor(y3, wide(hsum), -1.0 / HD, y3, ALU.mult, ALU.add), ["hsum"], "centred")
            yield
            A(lambda e, i: e.activation(sq[:, :, :], yr[c][:, :, :], ACT.Square), ["centred", "hss"], "sq")
            T(vv, [f"xt{c}", "bank1"], f"proj{c}")
            yield
            for b in range(4):
                r, t = slice(64 * (b % 2), 64 * (b % 2) + 64), b // 2
                for h2 in range(2):
                    u = A(lambda e, i, b=b, r=r, t=t, h2=h2: e.activation(
                        vbd[c][64 * h2:64 * h2 + 64, b, :].rearrange("p (n w) -> p n w", w=VW)[:, :, HD * h2:HD * h2 + HD],
                        bank[1][r, t * D:(t + 1) * D].rearrange("p (n h d) -> p n h d", n=NP, h=2)[:, :, h2, :], ACT.Copy),
                        [f"proj{c}", f"av{c}", "vones"], "bank1")
            pr.named(f"values{c}", u)
            V(lambda e, i: e.tensor_reduce(hvar[:, :], sq[:, :, :].rearrange("p t (h d) -> p (t h) d", d=HD), AX, ALU.add), ["sq", "yn"], "hss")
            for t in range(2):
                V(lambda e, i, t=t: e.tensor_scalar(hvar[:, 32 * t:32 * t + 32], hvar[:, 32 * t:32 * t + 32], hrow[c][:, t:t + 1], EPS,
                                                    ALU.mult, ALU.add), ["hss", f"hrow{c}"], "hvar")
            yield
            V(lambda e, i: e.tensor_scalar(newton[:, :].bitcast(I32), hvar[:, :].bitcast(I32), 1, None, ALU.logical_shift_right), ["hvar"], "guess")
            V(lambda e, i: e.tensor_scalar(half_v[:, :], hvar[:, :], -0.5, None, ALU.mult), ["hvar"], "half_v")
            V(lambda e, i: e.tensor_scalar(hstd[:, :].bitcast(I32), newton[:, :].bitcast(I32), -1.0, float(0x5f3759df), ALU.mult, ALU.add),
              ["guess"], "root")
            for n in range(3):
                V(lambda e, i: e.tensor_tensor(newton[:, :], hstd[:, :], hstd[:, :], ALU.mult), ["root"], "n1")
                V(lambda e, i: e.tensor_tensor(newton[:, :], newton[:, :], half_v[:, :], ALU.mult), ["n1", "half_v"], "n2")
                V(lambda e, i: e.scalar_tensor_tensor(hstd[:, :], newton[:, :], 1.5, hstd[:, :], ALU.add, ALU.mult), ["n2"], "root")
                if n == 1:
                    yield
            for t in range(2):
                V(lambda e, i, t=t: e.tensor_scalar(hstd[:, 32 * t:32 * t + 32], hstd[:, 32 * t:32 * t + 32], hrow[c][:, 2 + t:3 + t], None,
                                                    ALU.mult), ["root"], "hscale")
            pr.named("hrow_read", pr.last["hscale"])
            V(lambda e, i: e.tensor_tensor(y3, y3, wide(hstd), ALU.mult), ["hscale", "sq"], "yn")
            yield
            for t in range(2):
                def yn_T(e, i, t=t):
                    for n in range(4):
                        last = e.transpose(bank[0][:, n * P:(n + 1) * P], yr[c][:, t, n * P:(n + 1) * P], ident)
                    return last
                T(yn_T, ["yn", "bank0"], f"ynT{c}")
                A(lambda e, i, t=t: e.activation(
                    qT[c][:, :, t * P:(t + 1) * P], bank[0][:, 0:256].rearrange("p (t n) -> p t n", t=2), ACT.Identity,
                    bias=hcol[:, 1:2], scale=hcol[:, 0:1]), [f"ynT{c}", f"scores{c}", dh[-1]])
                for h2 in range(2):
                    u = A(lambda e, i, t=t, h2=h2: e.activation(
                        kbd[c][:, :, 2 * t:2 * t + 2, 64 * h2:64 * h2 + 64],
                        bank[0][:, 256:512].rearrange("p (t b l) -> p t b l", t=2, b=2), ACT.Identity,
                        bias=kcol[:, h2, 1:2], scale=kcol[:, h2, 0:1]), [f"ynT{c}", f"scores{c}", "kcol"], f"keys{c}")
                pr.named("bank0", u)
                yield

        def softmax_steps(j, s, scale, tb, mrow, free=()):
            p2 = j % 2

            def step_copy():
                A(lambda e, i: e.activation(ssb[p2][:, :], bank[s][:, :], ACT.Copy), [f"S{s}", f"ssbT{p2}"], f"ssb{p2}")

            def step_T():
                def go(e, i):
                    for n in range(4):
                        last = e.transpose(bank[tb][:, n * P:(n + 1) * P], ssb[p2][:, n * P:(n + 1) * P], ident)
                    return last
                T(go, [f"ssb{p2}", "maxs"], f"ssbT{p2}")
                V(lambda e, i: e.tensor_reduce(maxs[:, :], bank[tb][:, :].rearrange("p (n l) -> p n l", l=64), AX, ALU.max),
                  [f"ssbT{p2}", "mlow"], "maxs")
                V(lambda e, i: e.tensor_copy(mhl[:, 0:8], maxs[:, :]), ["maxs", "maxTT"], "mhigh")
                V(lambda e, i: e.tensor_tensor(mhl[:, 8:16], maxs[:, :], mhl[:, 0:8].bitcast(F32), ALU.subtract), ["mhigh"], "mlow")

            def step_maxT():
                T(lambda e, i: e.transpose(mrow, mhl[:, :].bitcast(F32), ident), ["mlow", "maxT"] + list(free), "maxTT")
                V(lambda e, i: e.tensor_copy(maxT[:, :], mrow), ["maxTT", "shift"], "maxT")

            def step_shift():
                def go(e, i):
                    for n in range(4):
                        last = mm(e, bank[s][:, n * P:(n + 1) * P], sel[:, n, :], maxT[:, :], False, n == 3)
                    return last
                T(go, ["maxT", f"ssb{p2}", "sel"], "shift")
                A(lambda e, i: e.activation(ex[p2][:, :], bank[s][:, :], ACT.Exp, scale=scale), ["shift", f"pv{p2}"], f"ex{p2}")
            return step_copy, step_T, step_maxT, step_shift

        def weighted_values(j, c):
            def go(e, i):
                for tt in range(2):
                    for b in range(4):
                        n = tt * 4 + j
                        last = mm(e, bank[6 + b // 2][64 * (b % 2):64 * (b % 2) + 64, n * VW:(n + 1) * VW],
                                  ex[j % 2][:, (tt * 4 + b) * 64:(tt * 4 + b + 1) * 64],
                                  vbd[c][:, b, n * VW:(n + 1) * VW], True, True)
                return last
            T(go, [f"ex{j % 2}", f"values{c}", "an"], f"pv{j % 2}")
            pr.named(f"av{c}", pr.last[f"pv{j % 2}"])

        def attention(c):
            def scores(j):
                def go(e, i):
                    for tt in range(2):
                        for b in range(4):
                            r = slice(32 * j, 32 * j + 32)
                            last = mm(e, bank[3 + j % 2][:, (tt * 4 + b) * 64:(tt * 4 + b + 1) * 64],
                                      kbd[c][r, tt, b, :], qT[c][r, tt, b * 64:(b + 1) * 64],
                                      tt == 0 and b == 0, tt == 1 and b == 3)
                    return last
                T(go, [f"keys{c}", f"ex{j % 2}"], f"S{3 + j % 2}")
                pr.named(f"scores{c}", pr.last[f"S{3 + j % 2}"])

            steps = [softmax_steps(j, 3 + j % 2, 0.25, 5, bank[6][0:16, NP * VW:NP * VW + P]) for j in range(4)]
            yield
            scores(0)
            steps[0][0]()
            yield
            for j in range(4):
                steps[j][1]()
                if j:
                    weighted_values(j - 1, c)
                if j < 3:
                    scores(j + 1)
                    steps[j + 1][0]()
                steps[j][2]()
                yield
                steps[j][3]()
                yield

        def attention_out(blk, c):
            yield from idle(1)
            weighted_values(3, c)
            yield
            for t in range(2):
                o4 = bank[6 + t][:, 0:NP * VW].rearrange("p (n w) -> p n w", w=VW)
                V(lambda e, i, t=t, o4=o4: e.reciprocal(rden[:, t, :].rearrange("p (n w) -> p n w", w=2), o4[:, :, 2 * HD:VW]),
                  [f"av{c}", "an"], "rden")
                V(lambda e, i, t=t, o4=o4: e.tensor_tensor(
                    an[:, t, :].rearrange("p (n h d) -> p n h d", n=NP, h=2),
                    o4[:, :, 0:2 * HD].rearrange("p n (h d) -> p n h d", h=2),
                    rden[:, t, :].rearrange("p (n h o) -> p n h o", n=NP, o=1).broadcast_to([P, NP, 2, HD]), ALU.mult),
                  ["rden", "anT"], "an")
            two = tiles(lambda i: 2 * blk(i), 2)
            G(lambda e, i: e.tensor_tensor(two(i).rearrange("p (t d) -> p t d", t=2), two(i).rearrange("p (t d) -> p t d", t=2),
                                           borow[:, :].rearrange("p (o d) -> p o d", o=1).broadcast_to([P, 2, D]), ALU.add),
              ["borow", f"keys{c}"], "xb")
            yield

            def an_T(e, i):
                for k in range(KD):
                    for t in range(2):
                        last = e.transpose(bank[0][:, k * 256 + t * P:k * 256 + (t + 1) * P], an[:, t, k * P:(k + 1) * P], ident)
                return last
            T(an_T, ["an", "bank0"], "anT")
            A(lambda e, i: e.activation(aT[:, :, :], bank[0][:, :].rearrange("p (k n) -> p k n", k=KD), ACT.Copy), ["anT", "attn_out"], "aT")
            pr.named("bank0", pr.last["aT"])
            yield

            def proj_out(e, i):
                for t in range(2):
                    for k in range(KD):
                        last = mm(e, bank[2][:, t * 256:(t + 1) * 256], aT[:, k, t * P:(t + 1) * P], wo1[:, k, :], k == 0, k == KD - 1)
                return last
            T(proj_out, ["aT", "bank2"], "attn_out")
            yield
            V(lambda e, i: e.tensor_tensor(two(i), bank[2][:, :], two(i), ALU.add), ["attn_out", "xb"], "bank2")

        def interleave(*parts):
            parts = list(parts)
            while parts:
                for g in list(parts):
                    try:
                        next(g)
                    except StopIteration:
                        parts.remove(g)

        def idle(n):
            for _ in range(n):
                yield

        def period(b, of=None):
            of = of or (lambda n: lambda i: n)
            has = lambda n: 0 <= n < NT // 2
            parts = [attention(b % 2)] if has(b) else []
            if has(b - 1):
                parts.append(attention_out(of(b - 1), (b - 1) % 2))
            if has(b + 1):
                parts.append(head_norm((b + 1) % 2))
            if has(b + 2):
                parts.append(normed_T((b + 2) % 2))
                parts.append(project_rotate((b + 2) % 2))
            if has(b + 3):
                parts.append(normed(of(b + 3), (b + 3) % 2))
            interleave(*parts)

        for b in range(-3, 1):
            period(b)
        with pr.loop(2):
            for b in (1, 2):
                period(b, lambda n: lambda i: 2 * i + n)
        for b in range(5, 9):
            period(b)
        pr.barrier()

        if phases >= 2:
            bi = [0]

            def fold(mms, evacs):
                n = bi[0] % 8
                bi[0] += 1
                t = T(lambda e, i: mms(e, bank[n]), [f"fb{n}", dst[-1]])
                for eng, f in evacs(bank[n]):
                    t = (A if eng == "A" else V)(f, [t])
                pr.named(f"fb{n}", t)
                return t
            G(lambda e, i: e.memset(wqk[:, :, :, :, :, :], 0.0), name="wqk0")
            for hp in range(NP):
                for k in range(KD):
                    def mms(e, o, hp=hp, k=k):
                        for g in range(2):
                            last = mm(e, o[:, g * XQ:(g + 1) * XQ], wq_s[:, 2 * hp + g, k * P:(k + 1) * P], wkc_s[:, 2 * hp + g, :], True, True)
                        return last

                    def evacs(o, hp=hp, k=k):
                        src = o[:, 0:2 * XQ].rearrange("p (g t q) -> p g t q", g=2, t=2)
                        at = lambda w: w[:, k, :, 2 * hp * HQ:(2 * hp + 2) * HQ].rearrange("p t (g q) -> p g t q", g=2)
                        return [("A", lambda e, i: e.activation(at(wbh), src, ACT.Copy)),
                                ("V", lambda e, i: e.tensor_tensor(at(wbl), src, at(wbh).bitcast(F32), ALU.subtract))]
                    folded = fold(mms, evacs)
            for g8 in range(8):
                def mms(e, o, g8=g8):
                    for h in range(4):
                        last = e.transpose(o[0:XC, h * HQ:(h + 1) * HQ], wqr_s[:, (g8 // 2) * 4 + h, g8 % 2, :], ident[0:HQ, 0:HQ])
                    return last
                fold(mms, lambda o, g8=g8: [("A", lambda e, i: e.activation(wqrT[:, g8, :], o[0:XC, 0:4 * HQ], ACT.Copy))])
            for g in range(2):
                def mms(e, o, g=g):
                    for h in range(8):
                        last = e.transpose(o[0:XC, h * 64:(h + 1) * 64], wkr_s[:, 8 * g + h, :], ident[0:XC, 0:XC])
                    return last
                t = fold(mms, lambda o, g=g: [("A", lambda e, i: e.activation(
                    wkrT[:, 8 * g:8 * g + 8, :], o[0:XC, :].rearrange("p (h d) -> p h d", d=XC), ACT.Copy))])
            rows = {(0, 0): [(0, 96)], (1, 0): [(96, 128)], (1, 1): [(0, 64)], (2, 1): [(64, 128)],
                    (2, 2): [(0, 32)], (3, 2): [(32, 64), (64, 128)]}
            for (h, j), spans in rows.items():
                def mms(e, o, h=h, j=j):
                    for g8 in range(8):
                        last = mm(e, o[:, g8 * 64:(g8 + 1) * 64], wqrT[:, g8, j * P:(j + 1) * P], wkrT[:, (g8 // 2) * 4 + h, :], True, True)
                    return last

                def evacs(o, h=h, j=j, spans=spans):
                    pair, kt = h // 2, j - h // 2
                    res = []
                    for lo, hi in spans:
                        res.append(("A", lambda e, i, lo=lo, hi=hi: e.activation(
                            wqk[lo:hi, :, pair, :, kt, 64 * (h % 2):64 * (h % 2) + 64],
                            o[lo:hi, :].rearrange("p (g t d) -> p g t d", g=4, t=2), ACT.Copy)))
                    return res
                pr.gate.setdefault("tensor", []).append(t)
                pr.gate.setdefault("scalar", []).append(pr.last["wqk0"])
                fold(mms, evacs)
            for g in range(8):
                def mms(e, o, g=g):
                    for h in range(2):
                        for t in range(2):
                            last = e.transpose(o[:, (h * 2 + t) * P:(h * 2 + t + 1) * P], wo_s[:, t, (2 * g + h) * P:(2 * g + h + 1) * P], ident)
                    return last
                pr.gate.setdefault("vector", []).append(folded)
                t = fold(mms, lambda o, g=g: [("V", lambda e, i: e.tensor_copy(
                    woT[:, 2 * g:2 * g + 2, :], o[:, :].rearrange("p (h n) -> p h n", h=2)))])
            for g in range(4):
                def mms(e, o, g=g):
                    for q in range(2):
                        for h2 in range(2):
                            h = 4 * g + 2 * q + h2
                            last = mm(e, o[64 * h2:64 * h2 + 64, q * D:(q + 1) * D], wkv_s[:, h, :], woT[:, h, :], True, True)
                    return last
                pr.gate.setdefault("tensor", []).append(t)
                fold(mms, lambda o, g=g: [("A", lambda e, i: e.activation(
                    wop[:, 2 * g:2 * g + 2, :], o[:, :].rearrange("p (q n) -> p q n", q=2), ACT.Copy))])
            pr.barrier()

            cv = a["ctx_512"].rearrange("b l d -> l b d")

            def context_load(blk):
                for h in range(2):
                    def go(e, i, h=h):
                        f = blk(i)
                        src = cv[:, f * 8:f * 8 + 8, :] if isinstance(f, int) else cv[:, bass.ds(f * 8, 8), :]
                        return e.dma_start(ctxs[64 * h:64 * h + 64, :, :], src)
                    pr.dma("ctx", go, ["kvt"])

            def context(blk):
                bc = lambda n, lo, hi: C(n)[:, lo:hi].rearrange("p (o d) -> p o d", o=1).broadcast_to([P, 8, hi - lo])
                hc = XC // 2
                G(lambda e, i: e.tensor_tensor(kvr[:, :, :], ctxs[:, :, :], bc("kvc", 0, XC), ALU.mult), ["ctx", "kvbd", "kvt"], "kv_c")
                G(lambda e, i: e.tensor_tensor(kvt[:, :, 0:hc], ctxs[:, :, hc:XC], bc("kvs", 0, hc), ALU.mult), ["kvr"])
                G(lambda e, i: e.tensor_tensor(kvt[:, :, hc:XC], ctxs[:, :, 0:hc], bc("kvs", hc, XC), ALU.mult), ["kvr"], "kvt")
                G(lambda e, i: e.tensor_tensor(kvr[:, :, :], kvr[:, :, :], kvt[:, :, :], ALU.add), ["kv_c", "kvt"], "kvr")

            def context_diag():
                for h2 in range(2):
                    G(lambda e, i, h2=h2: e.tensor_tensor(
                        kvbd[:, :, 64 * h2:64 * h2 + 64], kvr[:, :, :],
                        C("half")[:, h2:h2 + 1].rearrange("p (o d) -> p o d", o=1).broadcast_to([P, 8, XC]), ALU.mult),
                        ["kvr", "ctxv", "kvbdT_ps"], "kvbd")

            def context_diag_T():
                def go(e, i):
                    for b in range(8):
                        last = e.transpose(bank[6 + b // 4][:, (b % 4) * P:(b % 4 + 1) * P], kvbd[:, b, :], ident)
                    return last
                T(go, ["kvbd", "xtl", "maxT", "x_cross"], "kvbdT_ps")
                for n in range(2):
                    A(lambda e, i, n=n: e.activation(kvbdT[:, 4 * n:4 * n + 4, :], bank[6 + n][:, :].rearrange("p (b c) -> p b c", c=P), ACT.Copy),
                      ["kvbdT_ps", "S2", "S3"], "kvbdT")

            def norm_vectors(blk, after):
                layer_norm("cross", lambda t: tiles(lambda i: 4 * blk(i) + t, 1), 4, False, after)()

            def norm_T(k, half):
                at, o = slice(256 * half, 256 * half + 256), bank[7][:, 256:512]

                def go(e, i):
                    for t in range(2):
                        last = e.transpose(o[:, t * P:(t + 1) * P], xhat[:, 2 * half + t, k * P:(k + 1) * P], ident)
                    return last
                T(go, ["xhat", "xtl", "x_cross", "kvbdT", "maxT"], "xhatT")
                A(lambda e, i: e.activation(xth[:, k, at], o, ACT.Copy), ["xhatT", "proj"], "xth")
                V(lambda e, i: e.tensor_tensor(xtl[:, k, at], o, xth[:, k, at].bitcast(F32), ALU.subtract), ["xth", "proj"], "xtl")

            def queries(beside):
                def half_products(g, j):
                    n = (3 * g + j) % 2
                    for half in range(2):
                        def go(e, i, half=half):
                            for k in range(KD):
                                lo = (4 * HQ * g) + P * j
                                last = mm3(e, bank[2 * half + n][:, :], wbh[:, k, half, lo:lo + P], wbl[:, k, half, lo:lo + P],
                                           xth[:, k, :], xtl[:, k, :], k == 0, k == KD - 1)
                            return last
                        T(go, ["xth", "xtl", f"rm{n}", f"ex{n}", f"cn{n}"], "proj")
                    bc = lambda q: C("xrope").rearrange("p (j f s) -> p j f s", j=3, f=4)[:, j, q, :].rearrange(
                        "p (o s) -> p o s", o=1).broadcast_to([P, 8, S])
                    for m, (half, q) in enumerate(((0, 0), (1, 1), (1, 2), (0, 3))):
                        V(lambda e, i, m=m, half=half, q=q: e.tensor_tensor(
                            m4[n][m][:, :].rearrange("p (b s) -> p b s", s=S), bank[2 * half + n][:, :].rearrange("p (b s) -> p b s", s=S),
                            bc(q), ALU.mult), ["proj", f"rope{n}"], f"rm{n}")
                    r = (3 * g + j) % 6
                    G(lambda e, i: e.tensor_tensor(rope[r][0][:, :], m4[n][0][:, :], m4[n][1][:, :], ALU.subtract), [f"rm{n}", f"qk{r}"])
                    G(lambda e, i: e.tensor_tensor(rope[r][1][:, :], m4[n][2][:, :], m4[n][3][:, :], ALU.add), [f"rm{n}", f"qk{r}"], f"rope{n}")
                    pr.named(f"rope_{r}", pr.last[f"rope{n}"])

                def latents(g, pair):
                    o = bank[4 + pair]

                    def go(e, i):
                        for kt in range(2):
                            for half in range(2):
                                r = (3 * g + pair + kt) % 6
                                last = mm(e, o[:, :], wqk[:, g, pair, half, kt, :], rope[r][half][:, :], kt == 0 and half == 0, kt == 1 and half == 1)
                        return last
                    T(go, [f"rope_{(3 * g + pair + 1) % 6}", f"rope_{(3 * g + pair) % 6}", f"qb{pair}"] + (["rd0", "rd1"] if pair else ["invT"]), "lat")
                    pr.named(f"qk{(3 * g + pair) % 6}", pr.last["lat"])
                    if pair:
                        pr.named(f"qk{(3 * g + 2) % 6}", pr.last["lat"])
                    A(lambda e, i: e.activation(qc[:, 2 * g + pair, :], o[:, :], ACT.Copy), ["lat", "cross_out"], f"qb{pair}")
                todo = []
                for n in range(12):
                    g, j = divmod(n, 3)
                    half_products(g, j)
                    beside(n)
                    if j:
                        todo.append((n, g, j - 1))
                    while todo and todo[0][0] <= n - 2:
                        latents(*todo.pop(0)[1:])
                for q in todo:
                    latents(*q[1:])

            def cross_attention():
                def scores(b):
                    s = 2 + b % 2
                    T(lambda e, i: mm(e, bank[s][:, :], kvbdT[:, b, :], qc[:, :, b * 64:(b + 1) * 64], True, True),
                      ["qb0", "qb1", "kvbdT", f"ex{b % 2}", "rm0", "rm1"], f"S{s}")

                def sums(b):
                    def go(e, i):
                        for q in range(4):
                            last = mm(e, bank[4][:, 2 * q:2 * q + 2], ex[b % 2][:, q * P:(q + 1) * P], C("half"), True, True)
                        return last
                    T(go, [f"ex{b % 2}", "invT", "qb0"], "sums")
                    V(lambda e, i: e.reciprocal(inv[:, :], bank[4][:, 0:8]), ["sums", "ilow"], "inv")
                    V(lambda e, i: e.tensor_copy(ihl[:, 0:8], inv[:, :]), ["inv", "invTT"], "ihigh")
                    V(lambda e, i: e.tensor_tensor(ihl[:, 8:16], inv[:, :], ihl[:, 0:8].bitcast(F32), ALU.subtract), ["ihigh"], "ilow")

                def contexts(b):
                    n = b % 2
                    T(lambda e, i: mm(e, bank[n][:, :], kvbd[:, b, :], ex[n][:, :], True, True),
                      [f"ex{n}", f"cn{n}", "kvbd", "rm0", "rm1"], f"pv{n}")
                    pr.named("ctxv", pr.last[f"pv{n}"])

                def spread_a(b):
                    T(lambda e, i: e.transpose(bank[4][0:16, 0:P], ihl[:, :].bitcast(F32), ident), ["ilow", "invT"], "invTT")
                    V(lambda e, i: e.tensor_copy(invT[:, :], bank[4][0:16, 0:P]), ["invTT", "spread"], "invT")

                def spread_b(b):
                    n = b % 2

                    def go(e, i):
                        for q in range(4):
                            last = mm(e, bank[5][:, q * P:(q + 1) * P], selp[:, q, :], invT[:, :], True, True)
                        return last
                    T(go, ["invT", "selp", "rd0", "rd1", "qb1"], "spread")
                    A(lambda e, i: e.activation(rd[n][:, :], bank[5][:, :], ACT.Copy), ["spread", f"cn{n}"], f"rd{n}")

                def normalise(b):
                    n = b % 2
                    V(lambda e, i: e.tensor_tensor(
                        qc[:, :, b * 64:(b + 1) * 64], bank[n][:, :].rearrange("p (n s) -> p n s", s=S),
                        rd[n][:, :].rearrange("p (n s) -> p n s", s=S), ALU.mult), [f"pv{n}", f"rd{n}", f"S{2 + n}"], f"cn{n}")

                steps = [softmax_steps(b, 2 + b % 2, 1.0, 6, bank[7][0:16, 0:P], ["xtl", "x_cross"]) for b in range(8)]
                scores(0)
                steps[0][0]()
                for b in range(8):
                    steps[b][1]()
                    if b < 7:
                        scores(b + 1)
                        steps[b + 1][0]()
                    if b:
                        sums(b - 1)
                    steps[b][2]()
                    if b:
                        contexts(b - 1)
                    if b > 1:
                        normalise(b - 2)
                    steps[b][3]()
                    if b:
                        spread_a(b - 1)
                    yield
                    if b:
                        spread_b(b - 1)
                sums(7)
                contexts(7)
                normalise(6)
                spread_a(7)
                yield
                spread_b(7)
                normalise(7)

            def cross_out(blk, t):
                one = tiles(lambda i: 4 * blk(i) + t, 1)
                for part in range(2):
                    mine = range(part * NP // 2, (part + 1) * NP // 2)

                    def go(e, i, mine=mine):
                        for n in mine:
                            last = mm(e, bank[7][:, 256:512], qc[:, n, t * P:(t + 1) * P], wop[:, n, :], n == mine[0], n == mine[-1])
                        return last
                    T(go, [f"cn{(2 * t + 1) % 2}", "x_cross", "xtl", "maxT"], "cross_out")
                    V(lambda e, i: e.tensor_tensor(one(i), bank[7][:, 256:512], one(i), ALU.add), ["cross_out"], "x_cross")
                    if not part:
                        yield

            def beside_attention(blk, nxt):
                for k, half in ((0, 0), (0, 1), (1, 0), (1, 1)):
                    if nxt:
                        norm_T(k, half)
                    yield
                for t in range(3):
                    yield from cross_out(blk, t)
                    yield

            def ahead(blk):
                context_load(blk)
                yield
                context(blk)

            def block2(blk, nxt):
                def beside(n):
                    if n == 2:
                        context_diag()
                    if n == 9:
                        context_diag_T()
                    if n == 5 and nxt:
                        norm_vectors(nxt, [])
                queries(beside)
                interleave(cross_attention(), beside_attention(blk, nxt), *([ahead(nxt)] if nxt else []))
                interleave(cross_out(blk, 3))

            interleave(ahead(lambda i: 0))
            norm_vectors(lambda i: 0, [])
            for k, half in ((0, 0), (0, 1), (1, 0), (1, 1)):
                norm_T(k, half)
            with pr.loop(3):
                block2(lambda i: i, lambda i: i + 1)
            block2(lambda i: 3, None)
            pr.barrier()

        if phases >= 3:
            dwr = pr.dma("wr", lambda e, i: e.dma_start(wr[:, :, :], a["L0_ffn_Wr"].rearrange("(k p) n -> p k n", p=P)))
            V(lambda e, i: e.tensor_copy(wrh[:, :, :], wr[:, :, :]), [dwr], "wrh")
            V(lambda e, i: e.tensor_tensor(wrl[:, :, :], wr[:, :, :], wrh[:, :, :].bitcast(F32), ALU.subtract), ["wrh"], "wrl")

            def expert_weights(n):
                q = n % 3
                d = [pr.dma(f"raw{q}", lambda e, i, s=s, w=w: e.dma_start(raw[q][:, w, :, :], a[s][n].rearrange("(k p) f -> p k f", p=P)), [f"split{q}"])
                     for w, s in enumerate(["L0_ffn_Wg", "L0_ffn_Wu"])][-1]
                pr.dma(f"wd{n}", lambda e, i: e.dma_start(wd[:, n, :, :], a["L0_ffn_Wd"][n].rearrange("(k p) d -> p k d", p=P)))
                u = None
                for w, (hi, lo) in enumerate(((wgh, wgl), (wuh, wul))):
                    A(lambda e, i, w=w, hi=hi: e.activation(hi[:, n, :, :], raw[q][:, w, :, :], ACT.Copy), [d], "whigh")
                    u = G(lambda e, i, w=w, hi=hi, lo=lo: e.tensor_tensor(lo[:, n, :, :], raw[q][:, w, :, :], hi[:, n, :, :].bitcast(F32), ALU.subtract),
                          ["whigh"], f"split{q}")
                pr.named(f"we{n}", u)

            def norm3(blk, after):
                layer_norm("ffn", lambda t: tiles(lambda i: 4 * blk(i) + t, 1), 4, False, after)()

            def norm3_T():
                for k in range(KD):
                    def go(e, i, k=k):
                        for t in range(4):
                            last = e.transpose(bank[6 + k][:, t * P:(t + 1) * P], xhat[:, t, k * P:(k + 1) * P], ident)
                        return last
                    T(go, ["xhat", "xtl", "elog"], "xhatT")
                    A(lambda e, i, k=k: e.activation(xth[:, k, :], bank[6 + k][:, :], ACT.Copy), ["xhatT", "proj"], "xth")
                    V(lambda e, i, k=k: e.tensor_tensor(xtl[:, k, :], bank[6 + k][:, :], xth[:, k, :].bitcast(F32), ALU.subtract), ["xth", "proj"], "xtl")

            def route():
                def logits(e, i):
                    for t in range(4):
                        for k in range(KD):
                            last = mm3(e, bank[6][:, t * E:(t + 1) * E], xth[:, k, t * P:(t + 1) * P], xtl[:, k, t * P:(t + 1) * P],
                                       wrh[:, k, :], wrl[:, k, :], k == 0, k == KD - 1)
                    return last
                T(logits, ["xtl", "wrl"], "logits")
                l3 = bank[6][:, 0:4 * E].rearrange("p (t n) -> p t n", n=E)
                bc = lambda v: v[:, :].rearrange("p (t o) -> p t o", o=1).broadcast_to([P, 4, E])
                V(lambda e, i: e.tensor_reduce(emax[:, :], l3, AX, ALU.max), ["logits", "ffn_acc"], "emax")
                V(lambda e, i: e.tensor_tensor(ew[:, :, :], l3, bc(emax), ALU.subtract), ["emax", "ffn_acc"], "elog")
                A(lambda e, i: e.activation(ew[:, :, :], ew[:, :, :], ACT.Exp), ["elog"], "eexp")
                before = C("before").rearrange("p (i j) -> p i j", j=E)
                for t in range(4):
                    mine = ew[:, t, :].rearrange("p (i o) -> p i o", o=1).broadcast_to([P, E, E])
                    other = ew[:, t, :].rearrange("p (o j) -> p o j", o=1).broadcast_to([P, E, E])
                    V(lambda e, i, mine=mine, other=other: e.tensor_tensor(cmpa[:, :, :], other, mine, ALU.is_gt), ["eexp", "rank"], "cmpa")
                    V(lambda e, i, mine=mine, other=other: e.tensor_tensor(cmpb[:, :, :], other, mine, ALU.is_equal), ["eexp", "rank"], "cmpb")
                    V(lambda e, i: e.tensor_tensor(cmpb[:, :, :], cmpb[:, :, :], before, ALU.mult), ["cmpb"], "cmpb")
                    V(lambda e, i: e.tensor_tensor(cmpa[:, :, :], cmpa[:, :, :], cmpb[:, :, :], ALU.add), ["cmpa", "cmpb"], "cmpa")
                    V(lambda e, i: e.tensor_reduce(rank[:, :], cmpa[:, :, :], AX, ALU.add), ["cmpa"], "rank")
                    V(lambda e, i, t=t: e.scalar_tensor_tensor(ew[:, t, :], rank[:, :], 2.0, ew[:, t, :], ALU.is_lt, ALU.mult), ["rank"], "rank")
                V(lambda e, i: e.tensor_reduce(esum[:, :], ew[:, :, :], AX, ALU.add), ["rank"], "esum")
                V(lambda e, i: e.reciprocal(esum[:, :], esum[:, :]), ["esum"], "esum")
                V(lambda e, i: e.tensor_tensor(ew[:, :, :], ew[:, :, :], bc(esum), ALU.mult), ["esum"], "ew")

            def gate_up(n):
                p2 = n % 2
                for f in range(KF):
                    for w, (hi, lo) in enumerate(((wgh, wgl), (wuh, wul))):
                        def go(e, i, f=f, w=w, hi=hi, lo=lo):
                            for k in range(KD):
                                last = mm3(e, bank[2 * w + f][:, :], hi[:, n, k, f * P:(f + 1) * P], lo[:, n, k, f * P:(f + 1) * P],
                                           xth[:, k, :], xtl[:, k, :], k == 0, k == KD - 1)
                            return last
                        T(go, ["xth", "xtl", f"gu{f}", f"we{n}"], "proj")
                        pr.named(f"gu_ps{w}", pr.last["proj"])
                    A(lambda e, i, f=f: e.activation(sg[f][:, :], bank[f][:, :], ACT.Silu), ["gu_ps0", f"gu{f}"], f"silu{f}")
                    V(lambda e, i, f=f: e.tensor_tensor(hh[p2][:, f, :], bank[2 + f][:, :], sg[f][:, :], ALU.mult),
                      ["gu_ps1", f"silu{f}", f"down{p2}"], f"gu{f}")
                    pr.named(f"hh{p2}", pr.last[f"gu{f}"])

            def down(n, blk):
                p2 = n % 2
                for half in range(2):
                    def go(e, i, half=half):
                        for t in range(2):
                            for k in range(KF):
                                tt = 2 * half + t
                                last = mm(e, bank[4 + half][:, t * D:(t + 1) * D], hh[p2][:, k, tt * P:(tt + 1) * P], wd[:, n, k, :], k == 0, k == KF - 1)
                        return last
                    T(go, [f"hh{p2}", f"acc{half}", f"wd{n}"], f"down{p2}")
                    for t in range(2):
                        tt = 2 * half + t
                        one = tiles(lambda i, tt=tt: 4 * blk(i) + tt, 1)
                        V(lambda e, i, t=t, tt=tt, one=one, half=half: e.scalar_tensor_tensor(
                            one(i), bank[4 + half][:, t * D:(t + 1) * D], ew[:, tt, n:n + 1], one(i), ALU.mult, ALU.add),
                          [f"down{p2}", "ew", f"acc{half}", "xhat"], f"acc{half}")
                        pr.named("ffn_acc", pr.last[f"acc{half}"])

            ov = out.rearrange("b s d -> (b s) d").rearrange("(t p) d -> p t d", p=P)

            def block3(blk, nxt):
                for n in range(E):
                    gate_up(n)
                    if n:
                        down(n - 1, blk)
                    if n == 4 and nxt:
                        norm3(nxt, [])
                if nxt:
                    norm3_T()
                down(E - 1, blk)

                def store(e, i):
                    f = blk(i)
                    d = ov[:, f * 4:f * 4 + 4, :] if isinstance(f, int) else ov[:, bass.ds(f * 4, 4), :]
                    s = x3[:, f * 4:f * 4 + 4, :] if isinstance(f, int) else x3[:, bass.ds(f * 4, 4), :]
                    return e.dma_start(d, s)
                pr.dma("out", store, ["ffn_acc"])
                if nxt:
                    route()

            norm3(lambda i: 0, [])
            for n in range(E):
                expert_weights(n)
                if n == 0:
                    norm3_T()
                    route()
            block3(lambda i: 0, lambda i: 1)
            with pr.loop(2):
                block3(lambda i: i + 1, lambda i: i + 2)
            block3(lambda i: 3, None)
            pr.barrier()
            pr.add("sync", lambda e, i: e.nop(), [], None)
        else:
            ov = out.rearrange("b s d -> (b s) d").rearrange("(t p) d -> p t d", p=P)
            pr.dma("out", lambda e, i: e.dma_start(ov, x3))
            pr.barrier()
            pr.add("sync", lambda e, i: e.nop(), [], None)
        pr.emit()


_INS = ["x", "ctx_512", "L0_attn_ln_q_g", "L0_attn_ln_q_b", "L0_attn_Wq", "L0_attn_bq", "L0_attn_ln_kv_g", "L0_attn_ln_kv_b",
        "L0_attn_Wkv", "L0_attn_bkv", "L0_attn_ln_h_g", "L0_attn_ln_h_b", "L0_attn_Wo", "L0_attn_bo", "L0_xattn_Wq",
        "L0_xattn_w_kc_q", "L0_xattn_w_kc_kv", "L0_xattn_W_qr", "L0_xattn_W_kr", "L0_xattn_Wo", "L0_ffn_Wr", "L0_ffn_Wg",
        "L0_ffn_Wu", "L0_ffn_Wd"]
PHASES = 3


def kernel(**inputs):
    import concourse.bacc as bacc
    from concourse.bass_utils import run_bass_kernel_spmd

    nc = bacc.Bacc("TRN2", target_bir_lowering=False, num_devices=1)
    arrays, aps = {}, {}

    def give(name, array):
        arrays[f"in_{name}"] = array
        return nc.dram_tensor(f"in_{name}", array.shape, mybir.dt.from_np(array.dtype), kind="ExternalInput").ap()

    for name in _INS:
        aps[name] = give(name, np.ascontiguousarray(inputs[name]))
    parts, at, n = [], {}, 0
    for name, c in constants().items():
        at[name] = (n, n + c.shape[1])
        n += c.shape[1]
        parts.append(c)
    at["_"] = n
    const = give("constants", np.ascontiguousarray(np.concatenate(parts, axis=1)))
    out = nc.dram_tensor("out", (B, S, D), F32, kind="ExternalOutput").ap()
    decoder(nc, aps, const, at, out, PHASES)
    return run_bass_kernel_spmd(nc, [arrays], core_ids=[0]).results[0]["out"]
```

```python
from contextlib import ExitStack, contextmanager
from itertools import islice

import numpy as np

import concourse.bass as bass
from concourse import mybir

F32 = mybir.dt.float32
F32R = mybir.dt.float32r
I32 = mybir.dt.int32
ALU = mybir.AluOpType
ACT = mybir.ActivationFunctionType
AX = mybir.AxisListType.X
EPS = 1e-5

B, S, D = 32, 64, 256
P = 128
NT = B * S // P
KD = D // P
H, HD = 16, 16
NP = H // 2
VW = 2 * HD + 2
XH, XK, XC, XQ = 16, 128, 64, 192
HQ = XQ // 2
E, F = 8, 256
KF = F // P


def constants():
    p = np.arange(P)
    c = {}
    c["ident"] = np.eye(P)
    c["ones"] = np.ones((P, P))
    c["half"] = np.stack([p < 64, p >= 64], 1)
    c["parity"] = np.stack([p // HD % 2 == 0, p // HD % 2 == 1], 1)
    f = (np.float32(8000.0 / 200.0) ** np.linspace(0.0, 1.0, HD // 2, dtype=np.float32)) * np.float32(200.0) / np.float32(1000.0)
    f = (np.float32(200.0) * f / np.float32(1000.0)).astype(np.float32)
    ang = ((p % S).astype(np.float32)[:, None] * f[None, :]).astype(np.float32).astype(np.float64)
    c["rotc"], c["rots"] = np.cos(ang), np.sin(ang)

    def angles(pos, dim):
        inv = (np.float32(1.0) / np.float32(10000.0) ** (np.arange(0, dim, 2, dtype=np.float32) / np.float32(dim))).astype(np.float32)
        return (pos.astype(np.float32)[:, None] * inv[None, :]).astype(np.float32).astype(np.float64)
    a = np.repeat(angles(p % S, XC), 2, axis=1)
    c["kvc"] = np.cos(a)
    c["kvs"] = np.sin(a) * np.where(np.arange(XC) < XC // 2, -1.0, 1.0)
    a = np.repeat(angles(np.arange(S), XQ), 2, axis=1)
    t = np.zeros((P, 3, 4, S))
    for j in range(3):
        i = (P * j + p) % HQ
        t[:, j, 0], t[:, j, 1] = np.cos(a[:, i]).T, np.sin(a[:, i]).T
        t[:, j, 2], t[:, j, 3] = np.cos(a[:, HQ + i]).T, np.sin(a[:, HQ + i]).T
    c["xrope"] = t.reshape(P, -1)
    sel = np.zeros((P, 4, P))
    for hl in range(2):
        for x in range(4):
            for h2 in range(2):
                sel[hl * 8 + x * 2 + h2, x, 64 * h2:64 * h2 + 64] = -1.0
    c["sel"] = sel.reshape(P, -1)
    i = np.arange(E)
    c["before"] = np.tile((i[None, :] < i[:, None]).astype(np.float64).reshape(1, -1), (P, 1))
    c["power"] = np.tile(np.array([[-0.5, -0.5, 0.5, 0.5] + [-0.5] * 32]), (P, 1))
    return {k: np.ascontiguousarray(v, dtype=np.float32) for k, v in c.items()}


class Counter:

    def __init__(self, sem, step):
        self.sem, self.step, self.counts = sem, step, [0]

    def count_up(self, k):
        self.counts += [0] * (k + 1 - len(self.counts))
        self.counts[k] += 1
        return Done(self, k, self.counts[k])


class Done:

    def __init__(self, counter, k, n):
        self.counter, self.k, self.n = counter, k, n


class Carried:

    def __init__(self, name, k, first):
        self.name, self.k, self.first = name, k, first


class Program:
    def __init__(self, nc, ctx):
        self.nc, self.ctx = nc, ctx
        self.trips = [1]
        self.queues = {e: [[]] for e in ("tensor", "vector", "scalar", "gpsimd", "sync")}
        self.counters = {e: Counter(self.semaphore("done_" + e), 1) for e in self.queues if e != "sync"}
        self.channels = {}
        self.last = {}
        self.finals = {}
        self.gate = {}

    def semaphore(self, name):
        return self.ctx.enter_context(self.nc.semaphore(name))

    @property
    def k(self):
        return len(self.trips) - 1

    def segment(self, trips):
        self.trips.append(trips)
        for q in self.queues.values():
            q.append([])

    @contextmanager
    def loop(self, trips):
        self.segment(trips)
        self.inside = set()
        yield
        self.finals[self.k] = dict(self.last)
        self.segment(1)

    def ref(self, name):
        if self.trips[-1] > 1 and name not in self.inside:
            return Carried(name, self.k, self.last.get(name))
        return self.last.get(name)

    def do(self, engine, fn, after=(), name=None):
        done = self.counters[engine].count_up(self.k)
        self.add(engine, fn, after, self.counters[engine])
        return self.named(name, done)

    def dma(self, channel, fn, after=(), name=None, engine="sync"):
        if channel not in self.channels:
            self.channels[channel] = Counter(self.semaphore("dma_" + channel), 16)
        done = self.channels[channel].count_up(self.k)
        self.add(engine, fn, after, self.channels[channel])
        return self.named(name or channel, done)

    def named(self, name, done):
        if name:
            self.last[name] = done
            if self.trips[-1] > 1:
                self.inside.add(name)
        return done

    def add(self, engine, fn, after, counter):
        after = [self.ref(a) if isinstance(a, str) else a for a in after] + self.gate.pop(engine, [])
        self.queues[engine][-1].append((fn, [a for a in after if a], counter))

    def barrier(self):
        ends = [Done(c, self.k, 0) for c in list(self.counters.values()) + list(self.channels.values())]
        for d in ends:
            d.n = d.counter.counts[self.k] if self.k < len(d.counter.counts) else 0
        self.gate = {e: list(ends) for e in self.queues}

    def base(self, c, k):
        return sum(n * t for n, t in zip(c.counts[:k], self.trips[:k]))

    def count(self, c, k):
        return c.counts[k] if k < len(c.counts) else 0

    def value(self, d, k):
        if isinstance(d, Carried):
            first = self.value(d.first, k) if d.first else []
            end = self.finals[d.k].get(d.name)
            if end is None or end.k != d.k:
                return first
            c, per = end.counter, self.count(end.counter, k)
            assert self.base(c, k) >= 1, "a wait for a register's value needs to be positive"
            const = max(self.base(c, k) - per + end.n, 1)
            if first and first[0][0] is c:
                const = max(const, first[0][1])
            return first + [(c, const, per)]
        c = d.counter
        if d.k == k and self.trips[k] > 1:
            return [(c, self.base(c, k) + d.n, self.count(c, k))]
        return [(c, self.base(c, d.k) + (self.trips[d.k] - 1) * self.count(c, d.k) + d.n, 0)]

    def emit(self):
        with self.nc.Block() as block:
            for engine, segments in self.queues.items():
                def body(e, segments=segments):
                    known = {}
                    for k, steps in enumerate(segments):
                        if not steps:
                            continue
                        waits = [[v for a in after for v in self.value(a, k)] for _, after, _ in steps]
                        if self.trips[k] == 1:
                            self.run(e, steps, waits, None, known)
                            continue
                        for w in waits:
                            for c, const, per in w:
                                if not per and known.get(c, 0) < const:
                                    e.wait_ge(c.sem, const * c.step)
                                    known[c] = const
                        with e.Fori(0, self.trips[k]) as i:
                            self.run(e, steps, waits, i, dict(known))
                {"tensor": block.tensor, "vector": block.vector, "scalar": block.scalar,
                 "gpsimd": block.gpsimd, "sync": block.sync}[engine](body)

    def run(self, e, steps, waits, i, known):
        moving = {}
        for (fn, _, counter), w in zip(steps, waits):
            for c, const, per in w:
                if per:
                    if moving.get(c, -1) < const:
                        e.wait_ge(c.sem, (i * per + const) * c.step)
                        moving[c] = const
                elif known.get(c, 0) < const:
                    e.wait_ge(c.sem, const * c.step)
                    known[c] = const
            last = fn(e, i)
            if counter:
                last.then_inc(counter.sem, counter.step)


class Space:

    def __init__(self, nc, start):
        self.nc, self.at = nc, start

    def __call__(self, name, shape, dt=F32):
        t = self.nc.alloc_sbuf_tensor_at(name, shape, dt, offset=self.at)
        self.at += (4 * int(np.prod(shape[1:])) + 31) // 32 * 32
        assert self.at <= 229300, (name, self.at)
        return t


def decoder(nc, a, const_dram, const_at, out):
    ctx = ExitStack()
    with ctx:
        pr = Program(nc, ctx)
        T = lambda fn, after=(), name=None: pr.do("tensor", fn, after, name)
        V = lambda fn, after=(), name=None: pr.do("vector", fn, after, name)
        A = lambda fn, after=(), name=None: pr.do("scalar", fn, after, name)
        G = lambda fn, after=(), name=None: pr.do("gpsimd", fn, after, name)
        ctx.enter_context(nc.allow_non_contiguous_dma(reason="small parameter vectors"))

        bank = [ctx.enter_context(nc.psum_tensor(f"bank{i}", [P, 512], F32)) for i in range(8)]

        keep = Space(nc, 16512)
        x = keep("x", [P, NT * D])
        cst = keep("cst", [P, const_at["_"]])
        C = lambda name: cst[:, const_at[name][0]:const_at[name][1]]
        sel = keep("sel", [16, 4, P], F32R)
        stat = keep("stat", [P, 4, 6])
        mv = keep("mv", [P, 4, 2])
        gate_word = keep("gate_word", [P, 1])
        rstd = keep("rstd", [P, 4])
        small = keep("small", [P, 4])
        top = keep("top", [P, 4])
        hrow = [keep(f"hrow{i}", [P, 4]) for i in range(2)]
        maxT = keep("maxT", [16, P], F32R)
        maxs = keep("maxs", [P, 8])
        mhl = keep("mhl", [P, 16], F32R)
        selp = keep("selp", [16, 4, P], F32R)
        inv = keep("inv", [P, 8])
        ihl = keep("ihl", [P, 16], F32R)
        invT = keep("invT", [16, P], F32R)
        ssb = [keep(f"ssb{i}", [P, 512]) for i in range(2)]
        ex = [keep(f"ex{i}", [P, 512]) for i in range(2)]
        xhat = keep("xhat", [P, 4, D])
        xth = keep("xth", [P, KD, 512], F32R)
        xtl = keep("xtl", [P, KD, 512], F32R)
        ident = C("ident")

        s1 = Space(nc, keep.at)
        yr = [Space(nc, s1.at)("yr0", [P, 2, 512])]
        w1 = s1("w1", [P, KD, 3 * D])
        w1h, w1l = s1("w1h", [P, KD, 3 * D], F32R), s1("w1l", [P, KD, 3 * D], F32R)
        lncol = s1("lncol", [P, 4, KD])
        hcol = s1("hcol", [P, 2])
        kcol = s1("kcol", [P, 2, 2])
        bwide = s1("bwide", [P, 2, KD, P])
        brow = s1("brow", [P, 4 * D])
        crow = s1("crow", [P, 3 * D])
        cvT = s1("cvT", [P, KD, P])
        crh, crl = s1("crh", [P, 512], F32R), s1("crl", [P, 512], F32R)
        onesr = s1("onesr", [P, P], F32R)
        qkb = s1("qkb", [P, 2, 512])
        yr.append(s1("yr1", [P, 2, 512]))
        prod = [s1(f"prod{i}", [P, 512]) for i in range(4)]
        sq = s1("sq", [P, 2, 512])
        hsum = s1("hsum", [P, 64])
        hvar = s1("hvar", [P, 64])
        half_v = s1("half_v", [P, 64])
        newton = s1("newton", [P, 64])
        hstd = s1("hstd", [P, 64])
        kept_at = s1.at
        wo1 = s1("wo1", [P, KD, D])
        borow = s1("borow", [P, D])
        qT = [s1(f"qT{i}", [P, 2, 256]) for i in range(2)]
        kbd = [s1(f"kbd{i}", [P, 2, 4, P]) for i in range(2)]
        vbd = [s1(f"vbd{i}", [P, 4, NP * VW]) for i in range(2)]
        rden = s1("rden", [P, 2, 16])
        an = s1("an", [P, 2, D])
        aT = s1("aT", [P, KD, 256])
        w2 = Space(nc, keep.at)
        wbh = w2("wbh", [P, KD, 2, XH * HQ], F32R)
        wbl = w2("wbl", [P, KD, 2, XH * HQ], F32R)
        assert w2.at <= kept_at
        wqk = w2("wqk", [P, 4, 2, 3, P])
        w2.at = max(w2.at, keep.at + 4 * 4 * E * KD * F)
        wop = w2("wop", [P, NP, D])
        third = max(s1.at, w2.at)
        s2 = Space(nc, third)
        wq_s = s2("wq_s", [P, XH, D])
        wkc_s = s2("wkc_s", [P, XH, XQ])
        wqr_s = s2("wqr_s", [HQ, XH, 2, XC])
        wkr_s = s2("wkr_s", [XC, XH, XC])
        wkv_s = s2("wkv_s", [P, XH, XC])
        wo_s = s2("wo_s", [P, 2, XH * XK])
        woT = Space(nc, third)("woT", [P, XH, D])
        wqrT = s2("wqrT", [XC, 8, 4 * HQ])
        wkrT = s2("wkrT", [XC, XH, XC])
        a2 = Space(nc, third)
        ctxs = a2("ctxs", [P, 8, XC])
        kvt = a2("kvt", [P, 8, XC])
        kvr = a2("kvr", [P, 8, XC])
        kvbd = a2("kvbd", [P, 8, P])
        kvbdT = a2("kvbdT", [P, 8, P])
        rotated_at = a2.at
        m4 = [[a2(f"m{i}_{n}", [P, 512]) for n in range(4)] for i in range(2)]
        rope = [[a2(f"r{i}_{n}", [P, 512]) for n in range(2)] for i in range(6)]
        queries_at = a2.at
        qc = a2("qc", [P, NP, 512])
        rd = [a2(f"rd{i}", [P, 512]) for i in range(2)]
        s3 = Space(nc, keep.at)
        wgh, wgl = s3("wgh", [P, E, KD, F], F32R), s3("wgl", [P, E, KD, F], F32R)
        wuh, wul = s3("wuh", [P, E, KD, F], F32R), s3("wul", [P, E, KD, F], F32R)
        assert s3.at <= w2.at - 4 * NP * D
        s4 = Space(nc, w2.at)
        wr, wrh, wrl = s4("wr", [P, KD, E]), s4("wrh", [P, KD, E], F32R), s4("wrl", [P, KD, E], F32R)
        ew = s4("ew", [P, 4, E])
        emax = s4("emax", [P, 4])
        esum = s4("esum", [P, 4])
        rank = s4("rank", [P, 4, E])
        cmpa, cmpb = s4("cmpa", [P, 4, E, E]), s4("cmpb", [P, 4, E, E])
        assert s4.at <= third
        sg = [s4(f"sg{i}", [P, 512]) for i in range(2)]
        gu = [s4(f"gu{i}", [P, 512]) for i in range(2)]
        hhh = [s4(f"hhh{i}", [P, KF, 512], F32R) for i in range(2)]
        hhl = [s4(f"hhl{i}", [P, KF, 512], F32R) for i in range(2)]
        s5 = Space(nc, max(s4.at, rotated_at))
        raw = [s5(f"raw{i}", [P, 3, KD, F]) for i in range(3)]
        assert s5.at <= queries_at
        wdh, wdl = s5("wdh", [P, E, KF, D], F32R), s5("wdl", [P, E, KF, D], F32R)

        def mm(e, o, l, r, start, stop):
            return e.matmul(o, l, r, start=start, stop=stop, skip_group_check=True)

        def mm3(e, o, lh, ll, rh, rl, start, stop):
            mm(e, o, lh, rh, start, False)
            mm(e, o, lh, rl, False, False)
            return mm(e, o, ll, rh, False, stop)

        def tiles(first, n):
            def at(i):
                f = first(i)
                if isinstance(f, int):
                    return x[:, f * D:(f + n) * D]
                return x[:, bass.ds(f * D, n * D)]
            return at

        xv = a["x"].rearrange("b s d -> (b s) d").rearrange("(t p) d -> p t d", p=P)
        x3 = x[:, :].rearrange("p (t d) -> p t d", d=D)
        dx0 = pr.dma("x0", lambda e, i: e.dma_start(x3[:, 0:2, :], xv[:, 0:2, :]))
        dcst = pr.dma("cst", lambda e, i: e.dma_start(cst[:, :], const_dram), engine="scalar")
        dw = [pr.dma("w1q", lambda e, i: e.dma_start(w1[:, :, 0:D], a["L0_attn_Wq"].rearrange("(k p) n -> p k n", p=P))),
              pr.dma("w1kv", lambda e, i: e.dma_start(w1[:, :, D:3 * D], a["L0_attn_Wkv"].rearrange("(k p) n -> p k n", p=P)))]
        dln = [pr.dma("ln", lambda e, i, n=n, s=s: e.dma_start(lncol[:, n, :], a[s].rearrange("(k p) -> p k", p=P)), engine="scalar")
               for n, s in enumerate(["L0_attn_ln_q_g", "L0_attn_ln_q_b", "L0_attn_ln_kv_g", "L0_attn_ln_kv_b"])]
        dbr = [pr.dma("brow", lambda e, i, s=s, lo=lo, hi=hi: e.dma_start(
            brow[:, lo:hi], a[s].rearrange("(o n) -> o n", o=1).broadcast_to([P, hi - lo])), engine="scalar")
            for s, lo, hi in (("L0_attn_bq", 0, D), ("L0_attn_bkv", D, 3 * D), ("L0_attn_bo", 3 * D, 4 * D))]
        dh = [pr.dma("hcol", lambda e, i, n=n, s=s, r=r: e.dma_start(
            hcol[r * HD:(r + 1) * HD, n:n + 1], a[s].rearrange("(d o) -> d o", o=1)), engine="sync")
            for n, s in enumerate(["L0_attn_ln_h_g", "L0_attn_ln_h_b"]) for r in range(8)]
        dwo = pr.dma("wo1", lambda e, i: e.dma_start(wo1[:, :, :], a["L0_attn_Wo"].rearrange("(k p) n -> p k n", p=P)))
        dx1 = [pr.dma("x1", lambda e, i, t=t: e.dma_start(x3[:, t:t + 7, :], xv[:, t:t + 7, :])) for t in (2, 9)]
        stage_loads = [
            (wq_s[:, :, :], a["L0_xattn_Wq"].rearrange("(h k) i -> k h i", k=XK)),
            (wkc_s[:, :, :], a["L0_xattn_w_kc_q"].rearrange("h k q -> k h q")),
            (wqr_s[:, :, 0, :], a["L0_xattn_W_qr"][:, 0:HQ, :].rearrange("h q r -> q h r")),
            (wqr_s[:, :, 1, :], a["L0_xattn_W_qr"][:, HQ:XQ, :].rearrange("h q r -> q h r")),
            (wkr_s[:, :, :], a["L0_xattn_W_kr"].rearrange("h d r -> d h r")),
            (wkv_s[:, :, :], a["L0_xattn_w_kc_kv"].rearrange("h k d -> k h d")),
            (wo_s[:, :, :], a["L0_xattn_Wo"].rearrange("(t o) n -> o t n", o=P)),
        ]
        dst = [pr.dma("stage", lambda e, i, o=o, s=s: e.dma_start(o, s)) for o, s in stage_loads]

        A(lambda e, i: e.activation(sel[:, :, :], C("sel").rearrange("p (x c) -> p x c", x=4)[0:16], ACT.Copy), [dcst], "sel")
        A(lambda e, i: e.activation(selp[:, :, :], C("sel").rearrange("p (x c) -> p x c", x=4)[0:16], ACT.Copy, scale=-1.0), [dcst], "selp")
        zero = [G(lambda e, i, t=t: e.memset(t[:, :, :], 0.0)) for t in (vbd[0], vbd[1])]
        for t in (vbd[0], vbd[1]):
            G(lambda e, i, t=t: e.tensor_copy(
                t[:, :, :].rearrange("p b (n w) -> p (b n) w", w=VW)[:, :, 2 * HD:VW],
                C("half").rearrange("p (o w) -> p o w", o=1).broadcast_to([P, 4 * NP, 2])), [dcst, zero[-1]], "vones")
        def projection_weights():
            for n in range(2):
                for k in range(KD):
                    V(lambda e, i, n=n, k=k: e.tensor_scalar(bwide[:, n, k, :], C("ones"), lncol[:, 2 * n + 1, k:k + 1], None, ALU.mult),
                      [dcst, dln[-1]], "bwide")
            for k in range(KD):
                for n, lo, hi in ((0, 0, D), (2, D, 3 * D)):
                    V(lambda e, i, k=k, n=n, lo=lo, hi=hi: e.tensor_scalar(
                        w1h[:, k, lo:hi], w1[:, k, lo:hi], lncol[:, n, k:k + 1], None, ALU.mult), [dw[-1], dw[0], dln[-1]], "w1h")
                    V(lambda e, i, k=k, n=n, lo=lo, hi=hi: e.scalar_tensor_tensor(
                        w1l[:, k, lo:hi], w1[:, k, lo:hi], lncol[:, n, k:k + 1], w1h[:, k, lo:hi].bitcast(F32),
                        ALU.mult, ALU.subtract), ["w1h"], "w1l")
            for n in range(2):
                V(lambda e, i, n=n: e.tensor_scalar(kcol[:, n, :], hcol[:, :], C("parity")[:, n:n + 1], None, ALU.mult), [dh[-1]], "kcol")

            def bias_rows(e, i):
                for k in range(KD):
                    mm(e, bank[4][:, 0:D], bwide[:, 0, k, :], w1[:, k, 0:D], k == 0, k == KD - 1)
                for k in range(KD):
                    last = mm(e, bank[5][:, :], bwide[:, 1, k, :], w1[:, k, D:3 * D], k == 0, k == KD - 1)
                return last
            t = T(bias_rows, ["bwide", dw[0], dw[-1]])
            V(lambda e, i: e.tensor_tensor(crow[:, 0:D], bank[4][:, 0:D], brow[:, 0:D], ALU.add), [t, dbr[-1]])
            t = V(lambda e, i: e.tensor_tensor(crow[:, D:3 * D], bank[5][:, :], brow[:, D:3 * D], ALU.add), name="crow")
            V(lambda e, i: e.tensor_copy(crh[:, :], crow[:, 0:512]), ["crow"], "crh")
            V(lambda e, i: e.tensor_tensor(crl[:, :], crow[:, 0:512], crh[:, :].bitcast(F32), ALU.subtract), ["crh"])
            V(lambda e, i: e.tensor_copy(onesr[:, :], C("ones")), [dcst], "crow_split")

        def output_bias():
            def value_bias_T(e, i):
                for k in range(KD):
                    last = e.transpose(bank[6][:, k * P:(k + 1) * P], crow[:, 2 * D + k * P:2 * D + (k + 1) * P], ident)
                return last
            t = T(value_bias_T, ["crow", dcst])
            t = A(lambda e, i: e.activation(cvT[:, :, :], bank[6][:, 0:2 * P].rearrange("p (k c) -> p k c", k=KD), ACT.Copy), [t])

            def out_bias(e, i):
                for k in range(KD):
                    last = mm(e, bank[7][:, 0:D], cvT[:, k, :], wo1[:, k, :], k == 0, k == KD - 1)
                return last
            t = T(out_bias, [t, dwo])
            V(lambda e, i: e.tensor_tensor(borow[:, :], bank[7][:, 0:D], brow[:, 3 * D:4 * D], ALU.add), [t], "borow")

        def layer_norm(tag, xs, n, self_attn, after):
            for t in range(n):
                V(lambda e, i, t=t: e.bn_stats(stat[:, t, :], xs(t)(i)), list(after) + ["mv"], "stat")
            V(lambda e, i: e.memset(gate_word[:, :], 0.0), ["stat", "xhat"], "gate_word")
            for t in range(n):
                V(lambda e, i, t=t: e.bn_aggr(mv[:, t, :], stat[:, t, :]), ["stat", "xhat"], "mv")
            var = mv[:, 0:n, 1]
            if self_attn:
                V(lambda e, i: e.tensor_scalar(small[:, 0:2], var, 1.0 + EPS, EPS * EPS, ALU.mult, ALU.add), ["mv", "rstd"])
                u = V(lambda e, i: e.tensor_scalar(small[:, 2:4], var, EPS, None, ALU.add), ["mv"])
                u = V(lambda e, i: e.reciprocal(small[:, 2:4], small[:, 2:4]), [u])
                u = V(lambda e, i: e.scalar_tensor_tensor(top[:, 2:4], var, 4.0, small[:, 2:4], ALU.mult, ALU.mult), [u, "hstd"])
                u = V(lambda e, i: e.tensor_copy(top[:, 0:2], small[:, 0:2]), [u])
                G(lambda e, i: e.tensor_tensor(rstd[:, :], top[:, 0:4], C("power")[:, 0:4], ALU.pow), [u, "xhat", "hstd"], "rstd")
            else:
                u = V(lambda e, i: e.tensor_scalar(small[:, 0:n], var, EPS, None, ALU.add), ["mv", "rstd"])
                G(lambda e, i: e.tensor_tensor(rstd[:, 0:n], small[:, 0:n], C("power")[:, 4:4 + n], ALU.pow), [u, "xhat"], "rstd")

            def scale():
                for t in range(n):
                    V(lambda e, i, t=t: e.tensor_scalar(xhat[:, t, :], xs(t)(i), mv[:, t, 0:1], rstd[:, t:t + 1],
                                                        ALU.subtract, ALU.mult), ["rstd", "xhatT"], "xhat")
            return scale

        def normed(blk, c):
            yield from idle(6)
            scale = layer_norm("self", lambda t: tiles(lambda i: 2 * blk(i) + t, 1), 2, True, [dx0, dx1[-1]] if c or blk(0) else [dx0])
            yield from idle(3)
            scale()

        def normed_T(c):
            at = slice(256 * c, 256 * c + 256)
            yield from idle(1)

            def xhat_T(e, i):
                for k in range(KD):
                    for t in range(2):
                        last = e.transpose(bank[0][:, k * 256 + t * P:k * 256 + (t + 1) * P], xhat[:, t, k * P:(k + 1) * P], ident)
                return last
            T(xhat_T, ["xhat", "bank0", dcst], "xhatT")
            src = bank[0][:, :].rearrange("p (k n) -> p k n", k=KD)
            A(lambda e, i: e.activation(xth[:, :, at], src, ACT.Copy), ["xhatT", f"proj{c}"], "xth")
            V(lambda e, i: e.tensor_tensor(xtl[:, :, at], src, xth[:, :, at].bitcast(F32), ALU.subtract), ["xth", f"proj{c}"], "bank0")
            pr.named(f"xt{c}", pr.last["bank0"])
            V(lambda e, i: e.tensor_copy(hrow[c][:, 0:2], top[:, 2:4]), ["hrow_read"])
            V(lambda e, i: e.tensor_scalar(hrow[c][:, 2:4], rstd[:, 2:4], 4.0, None, ALU.mult), ["rstd", "hrow_read"], f"hrow{c}")
            pr.named("hstd", pr.last[f"hrow{c}"])

        cols = lambda c, t: slice(256 * c + t * P, 256 * c + (t + 1) * P)

        def project_rotate(c):
            yield from idle(5)
            for t in range(2):
                def qk(e, i, t=t):
                    o = bank[1 + t]
                    for k in range(KD):
                        last = mm3(e, o[:, :], xth[:, k, cols(c, t)], xtl[:, k, cols(c, t)],
                                   w1h[:, k, 0:512], w1l[:, k, 0:512], k == 0, False)
                    return last

                def bias(e, i, t=t):
                    mm(e, bank[1 + t][:, :], onesr[0:1, :], crh[0:1, :], False, False)
                    return mm(e, bank[1 + t][:, :], onesr[0:1, :], crl[0:1, :], False, True)
                T(qk, [f"xt{c}", f"bank{1 + t}", "w1l"])
                T(bias, ["crow_split"], "qk")
                A(lambda e, i, t=t: e.activation(qkb[:, t, :], bank[1 + t][:, :], ACT.Copy), ["qk", "rot_g", "rot_v"], f"bank{1 + t}")
                pr.named("qkb", pr.last[f"bank{1 + t}"])
                yield from idle(2 - t)

            pair = qkb[:, :, :].rearrange("p t (h f two) -> p (t h) f two", f=8, two=2)
            ev, od = pair[:, :, :, 0], pair[:, :, :, 1]
            yp = yr[c][:, :, :].rearrange("p t (h f two) -> p (t h) f two", f=8, two=2)
            cc = C("rotc").rearrange("p (o f) -> p o f", o=1).broadcast_to([P, 64, 8])
            ss = C("rots").rearrange("p (o f) -> p o f", o=1).broadcast_to([P, 64, 8])
            pv = [q[:, :].rearrange("p (h f) -> p h f", f=8) for q in prod]
            G(lambda e, i: e.tensor_tensor(pv[2], ev, ss, ALU.mult), ["qkb", "rot_g"], "p2")
            V(lambda e, i: e.tensor_tensor(pv[3], od, cc, ALU.mult), ["qkb", "rot_g"], "p3")
            G(lambda e, i: e.tensor_tensor(yp[:, :, :, 1], pv[2], pv[3], ALU.add), ["p2", "p3", f"ynT{c}"], "rot_g")
            V(lambda e, i: e.tensor_tensor(pv[0], ev, cc, ALU.mult), ["qkb", "rot_v"], "p0")
            yield
            V(lambda e, i: e.tensor_tensor(pv[1], od, ss, ALU.mult), ["qkb", "rot_v"], "p1")
            V(lambda e, i: e.tensor_tensor(yp[:, :, :, 0], pv[0], pv[1], ALU.subtract), ["p0", "p1", f"ynT{c}"], "rot_v")

        def head_norm(c):
            def vv(e, i):
                for t in range(2):
                    for k in range(KD):
                        last = mm3(e, bank[1][:, t * D:(t + 1) * D], xth[:, k, cols(c, t)], xtl[:, k, cols(c, t)],
                                   w1h[:, k, 512:768], w1l[:, k, 512:768], k == 0, k == KD - 1)
                return last
            y3 = yr[c][:, :, :].rearrange("p t (h d) -> p (t h) d", d=HD)
            wide = lambda v: v[:, :].rearrange("p (h o) -> p h o", o=1).broadcast_to([P, 64, HD])
            V(lambda e, i: e.tensor_reduce(hsum[:, :], y3, AX, ALU.add), ["rot_v", "rot_g"], "hsum")
            yield
            V(lambda e, i: e.scalar_tensor_tensor(y3, wide(hsum), -1.0 / HD, y3, ALU.mult, ALU.add), ["hsum"], "centred")
            yield
            A(lambda e, i: e.activation(sq[:, :, :], yr[c][:, :, :], ACT.Square), ["centred", "hss"], "sq")
            T(vv, [f"xt{c}", "bank1"], f"proj{c}")
            yield
            for odd in range(2):
                for h2 in range(2):
                    u = A(lambda e, i, odd=odd, h2=h2: e.activation(
                        vbd[c][64 * h2:64 * h2 + 64, :, :].rearrange("p (t o) (n w) -> p t o n w", o=2, w=VW)[:, :, odd, :, HD * h2:HD * h2 + HD],
                        bank[1][64 * odd:64 * odd + 64, :].rearrange("p (t n h d) -> p t n h d", t=2, n=NP, h=2)[:, :, :, h2, :], ACT.Copy),
                        [f"proj{c}", f"av{c}", "vones"], "bank1")
            pr.named(f"values{c}", u)
            V(lambda e, i: e.tensor_reduce(hvar[:, :], sq[:, :, :].rearrange("p t (h d) -> p (t h) d", d=HD), AX, ALU.add), ["sq", "yn"], "hss")
            for t in range(2):
                V(lambda e, i, t=t: e.tensor_scalar(hvar[:, 32 * t:32 * t + 32], hvar[:, 32 * t:32 * t + 32], hrow[c][:, t:t + 1], EPS,
                                                    ALU.mult, ALU.add), ["hss", f"hrow{c}"], "hvar")
            yield
            V(lambda e, i: e.tensor_scalar(newton[:, :].bitcast(I32), hvar[:, :].bitcast(I32), 1, None, ALU.logical_shift_right), ["hvar"], "guess")
            V(lambda e, i: e.tensor_scalar(half_v[:, :], hvar[:, :], -0.5, None, ALU.mult), ["hvar"], "half_v")
            V(lambda e, i: e.tensor_scalar(hstd[:, :].bitcast(I32), newton[:, :].bitcast(I32), -1.0, float(0x5f3759df), ALU.mult, ALU.add),
              ["guess"], "root")
            for n in range(3):
                V(lambda e, i: e.tensor_tensor(newton[:, :], hstd[:, :], hstd[:, :], ALU.mult), ["root"], "n1")
                V(lambda e, i: e.tensor_tensor(newton[:, :], newton[:, :], half_v[:, :], ALU.mult), ["n1", "half_v"], "n2")
                V(lambda e, i: e.scalar_tensor_tensor(hstd[:, :], newton[:, :], 1.5, hstd[:, :], ALU.add, ALU.mult), ["n2"], "root")
                if n == 1:
                    yield
            for t in range(2):
                V(lambda e, i, t=t: e.tensor_scalar(hstd[:, 32 * t:32 * t + 32], hstd[:, 32 * t:32 * t + 32], hrow[c][:, 2 + t:3 + t], None,
                                                    ALU.mult), ["root"], "hscale")
            pr.named("hrow_read", pr.last["hscale"])
            V(lambda e, i: e.tensor_tensor(y3, y3, wide(hstd), ALU.mult), ["hscale", "sq"], "yn")
            yield
            for t in range(2):
                def yn_T(e, i, t=t):
                    for n in range(4):
                        last = e.transpose(bank[0][:, n * P:(n + 1) * P], yr[c][:, t, n * P:(n + 1) * P], ident)
                    return last
                T(yn_T, ["yn", "bank0"], f"ynT{c}")
                A(lambda e, i, t=t: e.activation(
                    qT[c][:, :, t * P:(t + 1) * P], bank[0][:, 0:256].rearrange("p (t n) -> p t n", t=2), ACT.Identity,
                    bias=hcol[:, 1:2], scale=hcol[:, 0:1]), [f"ynT{c}", f"scores{c}", dh[-1]])
                for h2 in range(2):
                    u = A(lambda e, i, t=t, h2=h2: e.activation(
                        kbd[c][:, :, 2 * t:2 * t + 2, 64 * h2:64 * h2 + 64],
                        bank[0][:, 256:512].rearrange("p (t b l) -> p t b l", t=2, b=2), ACT.Identity,
                        bias=kcol[:, h2, 1:2], scale=kcol[:, h2, 0:1]), [f"ynT{c}", f"scores{c}", "kcol"], f"keys{c}")
                pr.named("bank0", u)
                yield

        def softmax_steps(j, s, scale, tb, mrow, free=()):
            p2 = j % 2

            def step_copy():
                A(lambda e, i: e.activation(ssb[p2][:, :], bank[s][:, :], ACT.Copy), [f"S{s}", f"ssbT{p2}"], f"ssb{p2}")

            def step_T():
                def go(e, i):
                    for n in range(4):
                        last = e.transpose(bank[tb][:, n * P:(n + 1) * P], ssb[p2][:, n * P:(n + 1) * P], ident)
                    return last
                T(go, [f"ssb{p2}", "maxs"], f"ssbT{p2}")
                V(lambda e, i: e.tensor_reduce(maxs[:, :], bank[tb][:, :].rearrange("p (n l) -> p n l", l=64), AX, ALU.max),
                  [f"ssbT{p2}", "mlow"], "maxs")
                V(lambda e, i: e.tensor_copy(mhl[:, 0:8], maxs[:, :]), ["maxs", "maxTT"], "mhigh")
                V(lambda e, i: e.tensor_tensor(mhl[:, 8:16], maxs[:, :], mhl[:, 0:8].bitcast(F32), ALU.subtract), ["mhigh"], "mlow")

            def step_maxT():
                T(lambda e, i: e.transpose(mrow, mhl[:, :].bitcast(F32), ident), ["mlow", "maxT"] + list(free), "maxTT")
                V(lambda e, i: e.tensor_copy(maxT[:, :], mrow), ["maxTT", "shift"], "maxT")

            def step_shift():
                def go(e, i):
                    for n in range(4):
                        last = mm(e, bank[s][:, n * P:(n + 1) * P], sel[:, n, :], maxT[:, :], False, n == 3)
                    return last
                T(go, ["maxT", f"ssb{p2}", "sel"], "shift")
                A(lambda e, i: e.activation(ex[p2][:, :], bank[s][:, :], ACT.Exp, scale=scale), ["shift", f"pv{p2}"], f"ex{p2}")
            return step_copy, step_T, step_maxT, step_shift

        def weighted_values(j, c):
            def go(e, i):
                for tt in range(2):
                    for b in range(4):
                        n = tt * 4 + j
                        last = mm(e, bank[6 + b // 2][64 * (b % 2):64 * (b % 2) + 64, n * VW:(n + 1) * VW],
                                  ex[j % 2][:, (tt * 4 + b) * 64:(tt * 4 + b + 1) * 64],
                                  vbd[c][:, b, n * VW:(n + 1) * VW], True, True)
                return last
            T(go, [f"ex{j % 2}", f"values{c}", "an"], f"pv{j % 2}")
            pr.named(f"av{c}", pr.last[f"pv{j % 2}"])

        def attention(c):
            def scores(j):
                def go(e, i):
                    for tt in range(2):
                        for b in range(4):
                            r = slice(32 * j, 32 * j + 32)
                            last = mm(e, bank[3 + j % 2][:, (tt * 4 + b) * 64:(tt * 4 + b + 1) * 64],
                                      kbd[c][r, tt, b, :], qT[c][r, tt, b * 64:(b + 1) * 64],
                                      tt == 0 and b == 0, tt == 1 and b == 3)
                    return last
                T(go, [f"keys{c}", f"ex{j % 2}"], f"S{3 + j % 2}")
                pr.named(f"scores{c}", pr.last[f"S{3 + j % 2}"])

            steps = [softmax_steps(j, 3 + j % 2, 0.25, 5, bank[6][0:16, NP * VW:NP * VW + P]) for j in range(4)]
            yield
            scores(0)
            steps[0][0]()
            yield
            for j in range(4):
                steps[j][1]()
                if j:
                    weighted_values(j - 1, c)
                if j < 3:
                    scores(j + 1)
                    steps[j + 1][0]()
                steps[j][2]()
                yield
                steps[j][3]()
                yield

        def attention_out(blk, c):
            yield from idle(1)
            weighted_values(3, c)
            yield
            for t in range(2):
                o4 = bank[6 + t][:, 0:NP * VW].rearrange("p (n w) -> p n w", w=VW)
                V(lambda e, i, t=t, o4=o4: e.reciprocal(rden[:, t, :].rearrange("p (n w) -> p n w", w=2), o4[:, :, 2 * HD:VW]),
                  [f"av{c}", "an"], "rden")
                V(lambda e, i, t=t, o4=o4: e.tensor_tensor(
                    an[:, t, :].rearrange("p (n h d) -> p n h d", n=NP, h=2),
                    o4[:, :, 0:2 * HD].rearrange("p n (h d) -> p n h d", h=2),
                    rden[:, t, :].rearrange("p (n h o) -> p n h o", n=NP, o=1).broadcast_to([P, NP, 2, HD]), ALU.mult),
                  ["rden", "anT"], "an")
            two = tiles(lambda i: 2 * blk(i), 2)
            G(lambda e, i: e.tensor_tensor(two(i).rearrange("p (t d) -> p t d", t=2), two(i).rearrange("p (t d) -> p t d", t=2),
                                           borow[:, :].rearrange("p (o d) -> p o d", o=1).broadcast_to([P, 2, D]), ALU.add),
              ["borow", f"keys{c}"], "xb")
            yield

            def an_T(e, i):
                for k in range(KD):
                    for t in range(2):
                        last = e.transpose(bank[0][:, k * 256 + t * P:k * 256 + (t + 1) * P], an[:, t, k * P:(k + 1) * P], ident)
                return last
            T(an_T, ["an", "bank0"], "anT")
            A(lambda e, i: e.activation(aT[:, :, :], bank[0][:, :].rearrange("p (k n) -> p k n", k=KD), ACT.Copy), ["anT", "attn_out"], "aT")
            pr.named("bank0", pr.last["aT"])
            yield

            def proj_out(e, i):
                for t in range(2):
                    for k in range(KD):
                        last = mm(e, bank[2][:, t * 256:(t + 1) * 256], aT[:, k, t * P:(t + 1) * P], wo1[:, k, :], k == 0, k == KD - 1)
                return last
            T(proj_out, ["aT", "bank2"], "attn_out")
            yield
            V(lambda e, i: e.tensor_tensor(two(i), bank[2][:, :], two(i), ALU.add), ["attn_out", "xb"], "bank2")

        def interleave(*parts):
            parts = list(parts)
            while parts:
                for g in list(parts):
                    try:
                        next(g)
                    except StopIteration:
                        parts.remove(g)

        def chain(*parts):
            for g in parts:
                yield from g

        def idle(n):
            for _ in range(n):
                yield

        def period(b, of=None, **beside):
            of = of or (lambda n: lambda i: n)
            has = lambda n: 0 <= n < NT // 2
            parts = [attention(b % 2)] if has(b) else []
            if has(b - 1):
                parts.append(attention_out(of(b - 1), (b - 1) % 2))
            if has(b + 2):
                parts.append(normed_T((b + 2) % 2))
                parts.append(project_rotate((b + 2) % 2))
            if has(b + 1):
                parts.append(head_norm((b + 1) % 2))
            if has(b + 3):
                parts.append(normed(of(b + 3), (b + 3) % 2))
            interleave(*parts, *beside.values())

        def fold_in(n, free, mms, evacs, after=(), over=(), name=None):
            t = T(lambda e, i: mms(e, bank[n]), [free, dst[-1]] + list(after))
            for eng, f in evacs(bank[n]):
                t = (A if eng == "A" else V)(f, [t] + list(over))
            pr.named(free, t)
            return pr.named(name, t)

        def folded_queries():
            for hp in range(NP):
                for k in range(KD):
                    def mms(e, o, hp=hp, k=k):
                        for g in range(2):
                            last = mm(e, o[:, g * XQ:(g + 1) * XQ], wq_s[:, 2 * hp + g, k * P:(k + 1) * P], wkc_s[:, 2 * hp + g, :], True, True)
                        return last

                    def evacs(o, hp=hp, k=k):
                        src = o[:, 0:2 * XQ].rearrange("p (g t q) -> p g t q", g=2, t=2)
                        at = lambda w: w[:, k, :, 2 * hp * HQ:(2 * hp + 2) * HQ].rearrange("p t (g q) -> p g t q", g=2)
                        return [("A", lambda e, i: e.activation(at(wbh), src, ACT.Copy)),
                                ("V", lambda e, i: e.tensor_tensor(at(wbl), src, at(wbh).bitcast(F32), ALU.subtract))]
                    fold_in(1 + k, f"bank{1 + k}", mms, evacs, over=["proj1", "keys1", "rot_g", "rot_v", "xb"], name="folded")
                yield

        def transposed_keys():
            for g8 in range(8):
                def mms(e, o, g8=g8):
                    for h in range(4):
                        last = e.transpose(o[0:XC, h * HQ:(h + 1) * HQ], wqr_s[:, (g8 // 2) * 4 + h, g8 % 2, :], ident[0:HQ, 0:HQ])
                    return last
                fold_in(1, "bank1", mms, lambda o, g8=g8: [("A", lambda e, i: e.activation(wqrT[:, g8, :], o[0:XC, 0:4 * HQ], ACT.Copy))])
                yield
            for g in range(2):
                def mms(e, o, g=g):
                    for h in range(8):
                        last = e.transpose(o[0:XC, h * 64:(h + 1) * 64], wkr_s[:, 8 * g + h, :], ident[0:XC, 0:XC])
                    return last
                fold_in(1, "bank1", mms, lambda o, g=g: [("A", lambda e, i: e.activation(
                    wkrT[:, 8 * g:8 * g + 8, :], o[0:XC, :].rearrange("p (h d) -> p h d", d=XC), ACT.Copy))])
                yield

        def copy_of(to, source, vector):
            if vector:
                return lambda e, i: e.tensor_copy(to, source)
            return lambda e, i: e.activation(to, source, ACT.Copy)

        def transposed_output():
            for g in range(8):
                def mms(e, o, g=g):
                    for h in range(2):
                        for t in range(2):
                            last = e.transpose(o[:, (h * 2 + t) * P:(h * 2 + t + 1) * P], wo_s[:, t, (2 * g + h) * P:(2 * g + h + 1) * P], ident)
                    return last
                n = 1 + 2 * (g % 2)
                fold_in(n, f"bank{n}", mms, lambda o, g=g: [("V" if g % 2 else "A", copy_of(
                    woT[:, 2 * g:2 * g + 2, :], o[:, :].rearrange("p (h n) -> p h n", h=2), g % 2))],
                    after=["ex0", "ex1"], over=["folded"])
                if g % 2:
                    yield

        def first_norm():
            yield from idle(4)
            scale = layer_norm("cross", lambda t: tiles(lambda i: t, 1), 4, False, [])
            yield from idle(2)
            scale()
            yield
            for c in range(2):
                def go(e, i, c=c):
                    for k in range(KD):
                        for t in range(2):
                            last = e.transpose(bank[0][:, k * 256 + t * P:k * 256 + (t + 1) * P], xhat[:, 2 * c + t, k * P:(k + 1) * P], ident)
                    return last
                at = slice(256 * c, 256 * c + 256)
                T(go, ["xhat", "bank0"], "xhatT")
                src = bank[0][:, :].rearrange("p (k n) -> p k n", k=KD)
                A(lambda e, i, at=at, src=src: e.activation(xth[:, :, at], src, ACT.Copy), ["xhatT", "proj0", "proj1"], "xth")
                V(lambda e, i, at=at, src=src: e.tensor_tensor(xtl[:, :, at], src, xth[:, :, at].bitcast(F32), ALU.subtract), ["xth"], "xtl")
                pr.named("bank0", pr.last["xtl"])
                yield

        period(-3)
        projection_weights()
        period(-2)
        output_bias()
        period(-1)
        period(0)
        with pr.loop(2):
            for b in (1, 2):
                period(b, lambda n: lambda i: 2 * i + n)
        keys, queries_in = transposed_keys(), folded_queries()
        period(5, beside=chain(idle(4), islice(keys, 6)))
        period(6, beside=chain(idle(4), keys))
        period(7, beside=chain(idle(1), islice(queries_in, 3), idle(1), queries_in), also=first_norm())
        period(8, beside=transposed_output())
        pr.barrier()

        def expert_load(n, after=()):
            for w, name in enumerate(["L0_ffn_Wg", "L0_ffn_Wu", "L0_ffn_Wd"]):
                pr.dma(f"raw{n % 3}", lambda e, i, w=w, name=name: e.dma_start(
                    raw[n % 3][:, w, :, :], a[name][n].rearrange("(k p) f -> p k f", p=P)), list(after) + [f"split{n % 3}", f"wd{n - 3}"])

        def expert_split(n, w, after=()):
            hi, lo = ((wgh, wgl), (wuh, wul), (wdh, wdl))[w]
            A(lambda e, i: e.activation(hi[:, n, :, :], raw[n % 3][:, w, :, :], ACT.Copy), [f"raw{n % 3}"] + list(after), "whigh")
            done = (G if w < 2 else V)(lambda e, i: e.tensor_tensor(
                lo[:, n, :, :], raw[n % 3][:, w, :, :], hi[:, n, :, :].bitcast(F32), ALU.subtract),
                ["whigh"] + list(after), f"split{n % 3}" if w < 2 else f"wd{n}")
            if w < 2:
                pr.named(f"we{n}", done)

        bi = [0]

        def fold(mms, evacs):
            n = bi[0] % 8
            bi[0] += 1
            return fold_in(n, f"fb{n}", mms, evacs)
        G(lambda e, i: e.memset(wqk[:, :, :, :, :], 0.0), name="wqk0")
        rows = {(0, 0): [(0, 96)], (1, 0): [(96, 128)], (1, 1): [(0, 64)], (2, 1): [(64, 128)],
                (2, 2): [(0, 32)], (3, 2): [(32, 64), (64, 128)]}
        for j in range(3):
            for two in range(2):
                def mms(e, o, j=j, two=two):
                    for n in range(4):
                        g8 = 4 * two + n
                        h = (g8 // 2) * 4 + j
                        last = mm(e, o[:, n * P:(n + 1) * P], wqrT[:, g8, j * P:(j + 1) * P],
                                  wkrT[:, h:h + 2, :].rearrange("p h d -> p (h d)"), True, True)
                    return last

                def evacs(o, j=j, two=two):
                    res = []
                    for h in (j, j + 1):
                        src = o[:, :].rearrange("p (g t x d) -> p g t x d", g=2, t=2, x=2)[:, :, :, h - j, :]
                        at = slice(64 * (h % 2), 64 * (h % 2) + 64)
                        for lo, hi in rows[h, j]:
                            for t in range(2):
                                to, tile = (slice(64 * t, 64 * t + 64), 2) if j == 1 else (slice(lo, hi), t)
                                res.append(("A", lambda e, i, lo=lo, hi=hi, t=t, to=to, tile=tile, src=src, at=at, h=h: e.activation(
                                    wqk[to, 2 * two:2 * two + 2, h // 2, tile, at], src[lo:hi, :, t, :], ACT.Copy)))
                    return res
                pr.gate.setdefault("scalar", []).append(pr.last["wqk0"])
                fold(mms, evacs)
        for g in range(4):
            def mms(e, o, g=g):
                for q in range(2):
                    for h2 in range(2):
                        h = 4 * g + 2 * q + h2
                        last = mm(e, o[64 * h2:64 * h2 + 64, q * D:(q + 1) * D], wkv_s[:, h, :], woT[:, h, :], True, True)
                return last
            fold(mms, lambda o, g=g: [("A", lambda e, i: e.activation(
                wop[:, 2 * g:2 * g + 2, :], o[:, :].rearrange("p (q n) -> p q n", q=2), ACT.Copy))])
        pr.barrier()

        cv = a["ctx_512"].rearrange("b l d -> l b d")

        def context_load(blk):
            for h in range(2):
                def go(e, i, h=h):
                    f = blk(i)
                    src = cv[:, f * 8:f * 8 + 8, :] if isinstance(f, int) else cv[:, bass.ds(f * 8, 8), :]
                    return e.dma_start(ctxs[64 * h:64 * h + 64, :, :], src)
                pr.dma("ctx", go, ["kvt"])

        def context(blk):
            bc = lambda n, lo, hi: C(n)[:, lo:hi].rearrange("p (o d) -> p o d", o=1).broadcast_to([P, 8, hi - lo])
            hc = XC // 2
            G(lambda e, i: e.tensor_tensor(kvr[:, :, :], ctxs[:, :, :], bc("kvc", 0, XC), ALU.mult), ["ctx", "kvbd", "kvt"], "kv_c")
            G(lambda e, i: e.tensor_tensor(kvt[:, :, 0:hc], ctxs[:, :, hc:XC], bc("kvs", 0, hc), ALU.mult), ["kvr"])
            G(lambda e, i: e.tensor_tensor(kvt[:, :, hc:XC], ctxs[:, :, 0:hc], bc("kvs", hc, XC), ALU.mult), ["kvr"], "kvt")
            G(lambda e, i: e.tensor_tensor(kvr[:, :, :], kvr[:, :, :], kvt[:, :, :], ALU.add), ["kv_c", "kvt"], "kvr")

        def context_diag():
            for h2 in range(2):
                G(lambda e, i, h2=h2: e.tensor_tensor(
                    kvbd[:, :, 64 * h2:64 * h2 + 64], kvr[:, :, :],
                    C("half")[:, h2:h2 + 1].rearrange("p (o d) -> p o d", o=1).broadcast_to([P, 8, XC]), ALU.mult),
                    ["kvr", "ctxv", "kvbdT_ps"], "kvbd")

        def context_diag_T():
            def go(e, i):
                for b in range(8):
                    last = e.transpose(bank[6 + b // 4][:, (b % 4) * P:(b % 4 + 1) * P], kvbd[:, b, :], ident)
                return last
            T(go, ["kvbd", "xtl", "maxT", "x_cross"], "kvbdT_ps")
            for n in range(2):
                A(lambda e, i, n=n: e.activation(kvbdT[:, 4 * n:4 * n + 4, :], bank[6 + n][:, :].rearrange("p (b c) -> p b c", c=P), ACT.Copy),
                  ["kvbdT_ps", "S2", "S3"], "kvbdT")

        def norm_vectors(blk, after):
            layer_norm("cross", lambda t: tiles(lambda i: 4 * blk(i) + t, 1), 4, False, after)()

        def norm_T(k, half):
            at, o = slice(256 * half, 256 * half + 256), bank[7][:, 256:512]

            def go(e, i):
                for t in range(2):
                    last = e.transpose(o[:, t * P:(t + 1) * P], xhat[:, 2 * half + t, k * P:(k + 1) * P], ident)
                return last
            T(go, ["xhat", "xtl", "x_cross", "kvbdT", "maxT"], "xhatT")
            A(lambda e, i: e.activation(xth[:, k, at], o, ACT.Copy), ["xhatT", "proj"], "xth")
            V(lambda e, i: e.tensor_tensor(xtl[:, k, at], o, xth[:, k, at].bitcast(F32), ALU.subtract), ["xth", "proj"], "xtl")

        def queries(beside):
            def half_products(g, j):
                n = (3 * g + j) % 2
                for half in range(2):
                    def go(e, i, half=half):
                        for k in range(KD):
                            lo = (4 * HQ * g) + P * j
                            last = mm3(e, bank[2 * half + n][:, :], wbh[:, k, half, lo:lo + P], wbl[:, k, half, lo:lo + P],
                                       xth[:, k, :], xtl[:, k, :], k == 0, k == KD - 1)
                        return last
                    T(go, ["xth", "xtl", f"rm{n}", f"ex{n}", f"cn{n}"], "proj")
                bc = lambda q: C("xrope").rearrange("p (j f s) -> p j f s", j=3, f=4)[:, j, q, :].rearrange(
                    "p (o s) -> p o s", o=1).broadcast_to([P, 8, S])
                for m, (half, q) in enumerate(((0, 0), (1, 1), (1, 2), (0, 3))):
                    V(lambda e, i, m=m, half=half, q=q: e.tensor_tensor(
                        m4[n][m][:, :].rearrange("p (b s) -> p b s", s=S), bank[2 * half + n][:, :].rearrange("p (b s) -> p b s", s=S),
                        bc(q), ALU.mult), ["proj", f"rope{n}"], f"rm{n}")
                r = (3 * g + j) % 6
                add = V if j == 1 or g == 3 and j == 2 else G
                for half, (first, second, op) in enumerate(((0, 1, ALU.subtract), (2, 3, ALU.add))):
                    parts = [(slice(0, P), rope[r][half][:, :])] if j != 1 else [
                        (slice(64 * q, 64 * q + 64), rope[r][q][64 * half:64 * half + 64, :]) for q in range(2)]
                    for rows, to in parts:
                        add(lambda e, i, rows=rows, to=to, first=first, second=second, op=op: e.tensor_tensor(
                            to, m4[n][first][rows, :], m4[n][second][rows, :], op), [f"rm{n}", f"qk{r}"], f"rope{n}")
                pr.named(f"rope_{r}", pr.last[f"rope{n}"])

            def latents(g, pair):
                o = bank[4 + pair]

                def go(e, i):
                    own, shared = rope[(3 * g + 2 * pair) % 6], rope[(3 * g + 1) % 6]
                    for tile, moving in enumerate((own[0], own[1], shared[pair])):
                        last = mm(e, o[:, :], wqk[:, g, pair, tile, :], moving[:, :], tile == 0, tile == 2)
                    return last
                T(go, [f"rope_{(3 * g + pair + 1) % 6}", f"rope_{(3 * g + pair) % 6}", f"qb{pair}"] + (["rd0", "rd1"] if pair else ["invT"]), "lat")
                pr.named(f"qk{(3 * g + pair) % 6}", pr.last["lat"])
                if pair:
                    pr.named(f"qk{(3 * g + 2) % 6}", pr.last["lat"])
                A(lambda e, i: e.activation(qc[:, 2 * g + pair, :], o[:, :], ACT.Copy), ["lat", "cross_out"], f"qb{pair}")
            todo = []
            for n in range(12):
                g, j = divmod(n, 3)
                half_products(g, j)
                beside(n)
                if j:
                    todo.append((n, g, j - 1))
                while todo and todo[0][0] <= n - 2:
                    latents(*todo.pop(0)[1:])
            for q in todo:
                latents(*q[1:])

        def cross_attention():
            def scores(b):
                s = 2 + b % 2
                T(lambda e, i: mm(e, bank[s][:, :], kvbdT[:, b, :], qc[:, :, b * 64:(b + 1) * 64], True, True),
                  ["qb0", "qb1", "kvbdT", f"ex{b % 2}", "rm0", "rm1"], f"S{s}")

            def sums(b):
                def go(e, i):
                    for q in range(4):
                        last = mm(e, bank[4][:, 2 * q:2 * q + 2], ex[b % 2][:, q * P:(q + 1) * P], C("half"), True, True)
                    return last
                T(go, [f"ex{b % 2}", "invT", "qb0"], "sums")
                V(lambda e, i: e.reciprocal(inv[:, :], bank[4][:, 0:8]), ["sums", "ilow"], "inv")

            def split_inverse():
                V(lambda e, i: e.tensor_copy(ihl[:, 0:8], inv[:, :]), ["inv", "invTT"], "ihigh")
                V(lambda e, i: e.tensor_tensor(ihl[:, 8:16], inv[:, :], ihl[:, 0:8].bitcast(F32), ALU.subtract), ["ihigh"], "ilow")

            def contexts(b):
                n = b % 2
                T(lambda e, i: mm(e, bank[n][:, :], kvbd[:, b, :], ex[n][:, :], True, True),
                  [f"ex{n}", f"cn{n}", "kvbd", "rm0", "rm1"], f"pv{n}")
                pr.named("ctxv", pr.last[f"pv{n}"])

            def spread_a(b):
                T(lambda e, i: e.transpose(bank[4][0:16, 0:P], ihl[:, :].bitcast(F32), ident), ["ilow", "invT"], "invTT")
                V(lambda e, i: e.tensor_copy(invT[:, :], bank[4][0:16, 0:P]), ["invTT", "spread"], "invT")

            def spread_b(b):
                n = b % 2

                def go(e, i):
                    for q in range(4):
                        last = mm(e, bank[5][:, q * P:(q + 1) * P], selp[:, q, :], invT[:, :], True, True)
                    return last
                T(go, ["invT", "selp", "rd0", "rd1", "qb1"], "spread")
                A(lambda e, i: e.activation(rd[n][:, :], bank[5][:, :], ACT.Copy), ["spread", f"cn{n}"], f"rd{n}")

            def normalise(b):
                n = b % 2
                V(lambda e, i: e.tensor_tensor(
                    qc[:, :, b * 64:(b + 1) * 64], bank[n][:, :].rearrange("p (n s) -> p n s", s=S),
                    rd[n][:, :].rearrange("p (n s) -> p n s", s=S), ALU.mult), [f"pv{n}", f"rd{n}", f"S{2 + n}"], f"cn{n}")

            steps = [softmax_steps(b, 2 + b % 2, 1.0, 6, bank[7][0:16, 0:P], ["xtl", "x_cross"]) for b in range(8)]
            scores(0)
            steps[0][0]()
            steps[0][1]()
            for b in range(8):
                if b < 7:
                    scores(b + 1)
                    steps[b + 1][0]()
                if b:
                    sums(b - 1)
                steps[b][2]()
                if b:
                    split_inverse()
                    contexts(b - 1)
                if b > 1:
                    normalise(b - 2)
                steps[b][3]()
                if b:
                    spread_a(b - 1)
                yield
                if b < 7:
                    steps[b + 1][1]()
                if b:
                    spread_b(b - 1)
            sums(7)
            split_inverse()
            contexts(7)
            normalise(6)
            spread_a(7)
            yield
            spread_b(7)
            normalise(7)

        def cross_out(blk, t, o, free, whole):
            ready = pr.ref(f"cn{(2 * t + 1) % 2}")
            one = tiles(lambda i: 4 * blk(i) + t, 1)
            for part in range(2):
                mine = range(part * NP // 2, (part + 1) * NP // 2)
                first, last_one = (0, NP - 1) if whole else (mine[0], mine[-1])

                def go(e, i, mine=mine, first=first, last_one=last_one):
                    for n in mine:
                        last = mm(e, o, qc[:, n, t * P:(t + 1) * P], wop[:, n, :], n == first, n == last_one)
                    return last
                T(go, [ready] + free, "cross_out")
                if part or not whole:
                    V(lambda e, i: e.tensor_tensor(one(i), o, one(i), ALU.add), ["cross_out"], "x_cross")
                if not part:
                    yield

        def beside_attention(blk):
            for k, half in ((0, 0), (0, 1), (1, 0), (1, 1)):
                norm_T(k, half)
                yield
            for t in range(3):
                yield from cross_out(blk, t, bank[7][:, 256:512], ["x_cross", "xtl", "maxT"], t == 2)
                yield

        def experts_ahead():
            pr.dma("wr", lambda e, i: e.dma_start(wr[:, :, :], a["L0_ffn_Wr"].rearrange("(k p) n -> p k n", p=P)))
            for n in range(3):
                expert_load(n, ["proj", "lat", "rope0", "rope1"])
            yield from idle(2)
            for n in range(3):
                for w in range(2):
                    expert_split(n, w, ["lat"])
                    yield
            V(lambda e, i: e.tensor_copy(wrh[:, :, :], wr[:, :, :]), ["wr"], "wrh")
            V(lambda e, i: e.tensor_tensor(wrl[:, :, :], wr[:, :, :], wrh[:, :, :].bitcast(F32), ALU.subtract), ["wrh"], "wrl")

        def ahead(blk):
            context_load(blk)
            yield
            context(blk)

        def block2(blk, nxt):
            def beside(n):
                if n == 2:
                    context_diag()
                if n == 9:
                    context_diag_T()
                if n == 5:
                    norm_vectors(nxt or (lambda i: 0), [])
            queries(beside)
            interleave(cross_attention(), beside_attention(blk), ahead(nxt) if nxt else experts_ahead())
            interleave(cross_out(blk, 3, bank[6][:, 0:256], ["maxs"], True))

        interleave(ahead(lambda i: 0))
        with pr.loop(3):
            block2(lambda i: i, lambda i: i + 1)
        block2(lambda i: 3, None)
        pr.barrier()

        def norm3(blk):
            return layer_norm("ffn", lambda t: tiles(lambda i: 4 * blk(i) + t, 1), 4, False, [])

        def norm3_T():
            for k in range(KD):
                def go(e, i, k=k):
                    for t in range(4):
                        last = e.transpose(bank[6 + k][:, t * P:(t + 1) * P], xhat[:, t, k * P:(k + 1) * P], ident)
                    return last
                T(go, ["xhat", "xtl", "elog"], f"xhatT{k}")
            pr.named("xhatT", pr.last["xhatT1"])

        def high3():
            for k in range(KD):
                A(lambda e, i, k=k: e.activation(xth[:, k, :], bank[6 + k][:, :], ACT.Copy), [f"xhatT{k}", "proj"], f"xth{k}")
            pr.named("xth", pr.last["xth1"])

        def low3():
            for k in range(KD):
                V(lambda e, i, k=k: e.tensor_tensor(xtl[:, k, :], bank[6 + k][:, :], xth[:, k, :].bitcast(F32), ALU.subtract), [f"xth{k}", "proj"], "xtl")

        bc = lambda v: v[:, :].rearrange("p (t o) -> p t o", o=1).broadcast_to([P, 4, E])

        def route():
            def logits(e, i):
                for t in range(4):
                    for k in range(KD):
                        last = mm3(e, bank[6][:, t * E:(t + 1) * E], xth[:, k, t * P:(t + 1) * P], xtl[:, k, t * P:(t + 1) * P],
                                   wrh[:, k, :], wrl[:, k, :], k == 0, k == KD - 1)
                return last
            T(logits, ["xtl", "wrl"], "logits")
            l3 = bank[6][:, 0:4 * E].rearrange("p (t n) -> p t n", n=E)
            V(lambda e, i: e.tensor_reduce(emax[:, :], l3, AX, ALU.max), ["logits", "ffn_acc"], "emax")
            V(lambda e, i: e.tensor_tensor(ew[:, :, :], l3, bc(emax), ALU.subtract), ["emax", "ffn_acc"], "elog")
            A(lambda e, i: e.activation(ew[:, :, :], ew[:, :, :], ACT.Exp), ["elog"], "eexp")

        def route_top():
            mine = ew[:, :, :].rearrange("p t (i o) -> p t i o", o=1).broadcast_to([P, 4, E, E])
            other = ew[:, :, :].rearrange("p t (o j) -> p t o j", o=1).broadcast_to([P, 4, E, E])
            before = C("before").rearrange("p (o i j) -> p o i j", o=1, j=E).broadcast_to([P, 4, E, E])
            V(lambda e, i: e.tensor_tensor(cmpa[:, :, :, :], other, mine, ALU.is_gt), ["eexp"], "cmpa")
            V(lambda e, i: e.tensor_tensor(cmpb[:, :, :, :], other, mine, ALU.is_equal), ["eexp"], "cmpb")
            V(lambda e, i: e.tensor_tensor(cmpb[:, :, :, :], cmpb[:, :, :, :], before, ALU.mult), ["cmpb"], "cmpb")
            V(lambda e, i: e.tensor_tensor(cmpa[:, :, :, :], cmpa[:, :, :, :], cmpb[:, :, :, :], ALU.add), ["cmpa", "cmpb"], "cmpa")
            V(lambda e, i: e.tensor_reduce(rank[:, :, :], cmpa[:, :, :, :], AX, ALU.add), ["cmpa"], "rank")
            V(lambda e, i: e.scalar_tensor_tensor(ew[:, :, :], rank[:, :, :], 2.0, ew[:, :, :], ALU.is_lt, ALU.mult), ["rank"], "top_two")
            V(lambda e, i: e.tensor_reduce(esum[:, :], ew[:, :, :], AX, ALU.add), ["top_two"], "esum")
            V(lambda e, i: e.reciprocal(esum[:, :], esum[:, :]), ["esum"], "esum")
            V(lambda e, i: e.tensor_tensor(ew[:, :, :], ew[:, :, :], bc(esum), ALU.mult), ["esum"], "ew")

        def gate_up(n):
            p2 = n % 2
            for f in range(KF):
                for w, (hi, lo) in enumerate(((wgh, wgl), (wuh, wul))):
                    def go(e, i, f=f, w=w, hi=hi, lo=lo):
                        for k in range(KD):
                            last = mm3(e, bank[2 * w + f][:, :], hi[:, n, k, f * P:(f + 1) * P], lo[:, n, k, f * P:(f + 1) * P],
                                       xth[:, k, :], xtl[:, k, :], k == 0, k == KD - 1)
                        return last
                    T(go, ["xth", "xtl", f"gu{f}", f"we{n}"], "proj")
                    pr.named(f"gu_ps{w}", pr.last["proj"])
                A(lambda e, i, f=f: e.activation(sg[f][:, :], bank[f][:, :], ACT.Silu), ["gu_ps0", f"gu{f}"], f"silu{f}")
                V(lambda e, i, f=f: e.tensor_tensor(gu[f][:, :], bank[2 + f][:, :], sg[f][:, :], ALU.mult),
                  ["gu_ps1", f"silu{f}", f"hlow{f}"], f"gu{f}")
                A(lambda e, i, f=f: e.activation(hhh[p2][:, f, :], gu[f][:, :], ACT.Copy), [f"gu{f}", f"down{p2}"], f"hhigh{f}")
                (V if f else G)(lambda e, i, f=f: e.tensor_tensor(hhl[p2][:, f, :], gu[f][:, :], hhh[p2][:, f, :].bitcast(F32), ALU.subtract),
                  [f"hhigh{f}"], f"hlow{f}")
                pr.named(f"hh{p2}_{f}", pr.last[f"hlow{f}"])

        def down(n, blk):
            p2 = n % 2
            for half in range(2):
                def go(e, i, half=half):
                    for t in range(2):
                        for k in range(KF):
                            tt = 2 * half + t
                            at = slice(tt * P, (tt + 1) * P)
                            last = mm3(e, bank[4 + half][:, t * D:(t + 1) * D], hhh[p2][:, k, at], hhl[p2][:, k, at],
                                       wdh[:, n, k, :], wdl[:, n, k, :], k == 0, k == KF - 1)
                    return last
                T(go, [f"hh{p2}_0", f"hh{p2}_1", f"acc{half}", f"wd{n}"], f"down{p2}")
                for t in range(2):
                    tt = 2 * half + t
                    one = tiles(lambda i, tt=tt: 4 * blk(i) + tt, 1)
                    V(lambda e, i, t=t, tt=tt, one=one, half=half: e.scalar_tensor_tensor(
                        one(i), bank[4 + half][:, t * D:(t + 1) * D], ew[:, tt, n:n + 1], one(i), ALU.mult, ALU.add),
                      [f"down{p2}", "ew", f"acc{half}", "xhat"], f"acc{half}")
                    pr.named("ffn_acc", pr.last[f"acc{half}"])

        ov = out.rearrange("b s d -> (b s) d").rearrange("(t p) d -> p t d", p=P)

        def block3(blk, nxt, weights=False):
            for n in range(E):
                gate_up(n)
                if n == 0:
                    route_top()
                if weights and n + 3 < E:
                    expert_load(n + 3)
                    for w in range(3):
                        expert_split(n + 3, w)
                if n == E - 2 and nxt:
                    norm3_T()
                if n == E - 1 and nxt:
                    high3()
                if n:
                    down(n - 1, blk)
                if n == 2 and nxt:
                    scale = norm3(nxt)
                if n == 4 and nxt:
                    scale()
            if nxt:
                low3()
            down(E - 1, blk)

            def store(e, i):
                f = blk(i)
                d = ov[:, f * 4:f * 4 + 4, :] if isinstance(f, int) else ov[:, bass.ds(f * 4, 4), :]
                s = x3[:, f * 4:f * 4 + 4, :] if isinstance(f, int) else x3[:, bass.ds(f * 4, 4), :]
                return e.dma_start(d, s)
            pr.dma("out", store, ["ffn_acc"])
            if nxt:
                route()

        route()
        for n in range(3):
            expert_split(n, 2)
        block3(lambda i: 0, lambda i: 1, True)
        with pr.loop(2):
            block3(lambda i: i + 1, lambda i: i + 2)
        block3(lambda i: 3, None)
        pr.barrier()
        pr.add("sync", lambda e, i: e.nop(), [], None)
        pr.emit()


_INS = ["x", "ctx_512", "L0_attn_ln_q_g", "L0_attn_ln_q_b", "L0_attn_Wq", "L0_attn_bq", "L0_attn_ln_kv_g", "L0_attn_ln_kv_b",
        "L0_attn_Wkv", "L0_attn_bkv", "L0_attn_ln_h_g", "L0_attn_ln_h_b", "L0_attn_Wo", "L0_attn_bo", "L0_xattn_Wq",
        "L0_xattn_w_kc_q", "L0_xattn_w_kc_kv", "L0_xattn_W_qr", "L0_xattn_W_kr", "L0_xattn_Wo", "L0_ffn_Wr", "L0_ffn_Wg",
        "L0_ffn_Wu", "L0_ffn_Wd"]


def kernel(**inputs):
    import concourse.bacc as bacc
    from concourse.bass_utils import run_bass_kernel_spmd

    nc = bacc.Bacc("TRN2", target_bir_lowering=False, num_devices=1)
    arrays, aps = {}, {}

    def give(name, array):
        arrays[f"in_{name}"] = array
        return nc.dram_tensor(f"in_{name}", array.shape, mybir.dt.from_np(array.dtype), kind="ExternalInput").ap()

    for name in _INS:
        aps[name] = give(name, np.ascontiguousarray(inputs[name]))
    parts, at, n = [], {}, 0
    for name, c in constants().items():
        at[name] = (n, n + c.shape[1])
        n += c.shape[1]
        parts.append(c)
    at["_"] = n
    const = give("constants", np.ascontiguousarray(np.concatenate(parts, axis=1)))
    out = nc.dram_tensor("out", (B, S, D), F32, kind="ExternalOutput").ap()
    decoder(nc, aps, const, at, out)
    return run_bass_kernel_spmd(nc, [arrays], core_ids=[0]).results[0]["out"]
```
